# Optimizing a Trainium2 kernel written in Bass

```python
import numpy as np
import jax
import jax.numpy as jnp

def _softmax(x, axis=-1):
    return jax.nn.softmax(x, axis=axis)

def _gelu(x):
    return jax.nn.gelu(x, approximate=True)

def _silu(x):
    return jax.nn.silu(x)

def _sigmoid(x):
    return jax.nn.sigmoid(x)

def _layernorm(x, axis=-1, eps=1e-05):
    m = jnp.mean(x, axis=axis, keepdims=True)
    v = jnp.var(x, axis=axis, keepdims=True)
    return (x - m) / jnp.sqrt(v + eps)

def _scatter_add(tgt, idx, src, axis=0):
    return tgt.at[idx].add(src)

def _segment_sum(src, seg, n):
    return jax.ops.segment_sum(src, seg, n)
kernel_name = 'mk_perceiver_d1_seqx_r4_670a15'

def setup_inputs(seed: int=0):
    np.random.seed(seed)
    _w = jnp.asarray

    def _rec_inputs():
        import jax
        import jax.numpy as jnp
        _rk = jax.random.key(seed)
        x = -0.000125 + 0.9999 * jax.random.normal(jax.random.fold_in(_rk, 1), (4, 256, 256), jnp.float32)
        _lenS = 256 - jax.random.randint(jax.random.fold_in(_rk, 7), (4,), 0, max(1, 256 // 4) + 1, jnp.int32)
        _lenS2 = 4096 - jax.random.randint(jax.random.fold_in(_rk, 8), (4,), 0, max(1, 4096 // 4) + 1, jnp.int32)
        _ctx_1024P = jax.random.normal(jax.random.fold_in(_rk, 11), (4, 16, 256), jnp.float32)
        _ctx_1024c = jax.random.dirichlet(jax.random.fold_in(_rk, 511), 0.3 * jnp.ones((16,), jnp.float32), (4, 4096))
        _ctx_1024t = jnp.einsum('bsk,bkd->bsd', _ctx_1024c, _ctx_1024P)
        _ctx_1024t = _ctx_1024t * jax.lax.rsqrt(jnp.mean(jnp.square(_ctx_1024t)) + 1e-12) * 0.953939
        ctx_1024 = -1.52775e-05 + 0.999936 * (_ctx_1024t + 0.3 * jax.random.normal(jax.random.fold_in(_rk, 611), (4, 4096, 256), jnp.float32))
        return (x, ctx_1024)
    x, ctx_1024 = _rec_inputs()

    def _L0_xattn_setup():
        import jax, jax.numpy as jnp
        import numpy as np
        import math
        B, SQ, SK, DQ, DK = (16, 512, 512, 256, 256)
        key = jax.random.key(seed)
        ks = jax.random.split(key, 6)
        return {'bert_feature': jax.random.normal(ks[0], (B, SQ, DQ), dtype=jnp.float32), 'knowledge_feature': jax.random.normal(ks[1], (B, SK, DK), dtype=jnp.float32), 'w1_w': jax.random.normal(ks[2], (DK, DQ), dtype=jnp.float32) * 0.02, 'w1_b': jax.random.normal(ks[3], (DK,), dtype=jnp.float32) * 0.02, 'w2_w': jax.random.normal(ks[4], (DQ, DQ + DK), dtype=jnp.float32) * 0.02, 'w2_b': jax.random.normal(ks[5], (DQ,), dtype=jnp.float32) * 0.02}
    _L0_xattn_all = _L0_xattn_setup()
    _L0_xattn_in = {k: v for k, v in _L0_xattn_all.items() if k in ('w1_w', 'w1_b', 'w2_w', 'w2_b')}
    del _L0_xattn_all

    def _L0_attn_setup():
        import jax, jax.numpy as jnp
        import numpy as np
        import math
        D_MODEL = 256
        NUM_HEADS = 16
        WINDOW = 64
        key = jax.random.key(seed)
        ks = jax.random.split(key, 9)
        B, N = (1, 1024)
        x = jax.random.normal(ks[0], (B, N, D_MODEL), jnp.float32)

        def w(k):
            return jax.random.normal(k, (D_MODEL, D_MODEL), jnp.float32) * 0.02
        return {'x': x, 'q_w': w(ks[1]), 'q_b': jnp.zeros((D_MODEL,), jnp.float32), 'k_w': w(ks[2]), 'k_b': jnp.zeros((D_MODEL,), jnp.float32), 'v_w': w(ks[3]), 'v_b': jnp.zeros((D_MODEL,), jnp.float32), 'o_w': w(ks[4]), 'o_b': jnp.zeros((D_MODEL,), jnp.float32)}
    _L0_attn_all = _L0_attn_setup()
    _L0_attn_in = {k: v for k, v in _L0_attn_all.items() if k in ('q_w', 'q_b', 'k_w', 'k_b', 'v_w', 'v_b', 'o_w', 'o_b')}
    del _L0_attn_all

    def _L0_ffn_setup():
        import jax, jax.numpy as jnp
        import numpy as np
        B, S, H = (2, 512, 256)
        E, I, K = (8, 1024, 2)

        def _moe_forward(x, gate_w, wg, wu, wd):
            b, s, h = x.shape
            x_flat = x.reshape(-1, h)
            logits = x_flat @ gate_w.T
            top_v, top_i = jax.lax.top_k(logits, K)
            probs = jax.nn.softmax(top_v.astype(jnp.float32), axis=-1).astype(logits.dtype)
            one_hot = jax.nn.one_hot(top_i, E, dtype=probs.dtype)
            combine = jnp.einsum('tk,tke->et', probs, one_hot)

            def body(acc, ws):
                wge, wue, wde, we = ws
                hidden = jax.nn.silu(x_flat @ wge.T) * (x_flat @ wue.T)
                return (acc + we[:, None] * (hidden @ wde.T), None)
            out, _ = jax.lax.scan(body, jnp.zeros_like(x_flat), (wg, wu, wd, combine))
            return out.reshape(b, s, h)
        key = jax.random.key(seed)
        ks = jax.random.split(key, 5)
        scale_h = 1.0 / np.sqrt(H)
        scale_i = 1.0 / np.sqrt(I)
        x = jax.random.normal(ks[0], (B, S, H), dtype=jnp.float32)
        gate_w = jax.random.normal(ks[1], (E, H), dtype=jnp.float32) * scale_h
        wg = jax.random.normal(ks[2], (E, I, H), dtype=jnp.float32) * scale_h
        wu = jax.random.normal(ks[3], (E, I, H), dtype=jnp.float32) * scale_h
        wd = jax.random.normal(ks[4], (E, H, I), dtype=jnp.float32) * scale_i
        return {'x': x, 'gate_w': gate_w, 'wg': wg, 'wu': wu, 'wd': wd}
    _L0_ffn_all = _L0_ffn_setup()
    _L0_ffn_in = {k: v for k, v in _L0_ffn_all.items() if k in ('gate_w', 'wg', 'wu', 'wd')}
    del _L0_ffn_all
    return {'x': x, 'ctx_1024': ctx_1024, 'L0_xattn_w1_w': _L0_xattn_in['w1_w'], 'L0_xattn_w1_b': _L0_xattn_in['w1_b'], 'L0_xattn_w2_w': _L0_xattn_in['w2_w'], 'L0_xattn_w2_b': _L0_xattn_in['w2_b'], 'L0_attn_q_w': _L0_attn_in['q_w'], 'L0_attn_q_b': _L0_attn_in['q_b'], 'L0_attn_k_w': _L0_attn_in['k_w'], 'L0_attn_k_b': _L0_attn_in['k_b'], 'L0_attn_v_w': _L0_attn_in['v_w'], 'L0_attn_v_b': _L0_attn_in['v_b'], 'L0_attn_o_w': _L0_attn_in['o_w'], 'L0_attn_o_b': _L0_attn_in['o_b'], 'L0_ffn_gate_w': _L0_ffn_in['gate_w'], 'L0_ffn_wg': _L0_ffn_in['wg'], 'L0_ffn_wu': _L0_ffn_in['wu'], 'L0_ffn_wd': _L0_ffn_in['wd']}

def reference(x, ctx_1024, L0_xattn_w1_w, L0_xattn_w1_b, L0_xattn_w2_w, L0_xattn_w2_b, L0_attn_q_w, L0_attn_q_b, L0_attn_k_w, L0_attn_k_b, L0_attn_v_w, L0_attn_v_b, L0_attn_o_w, L0_attn_o_b, L0_ffn_gate_w, L0_ffn_wg, L0_ffn_wu, L0_ffn_wd):
    import jax
    import jax.numpy as jnp

    def _L0_xattn_ref(bert_feature, knowledge_feature, w1_w, w1_b, w2_w, w2_b):
        import jax, jax.numpy as jnp
        import numpy as np
        import math
        B, SQ, SK, DQ, DK = (16, 512, 512, 256, 256)
        d_k = knowledge_feature.shape[-1]
        bf = jnp.einsum('bqd,kd->bqk', bert_feature, w1_w) + w1_b
        scores = jnp.einsum('bqd,bkd->bqk', bf, knowledge_feature) / math.sqrt(d_k)
        attn = jax.nn.softmax(scores, axis=-1)
        output = jnp.einsum('bqk,bkd->bqd', attn, knowledge_feature)
        fused = jnp.concatenate([bert_feature, output], axis=-1)
        return jnp.einsum('bqf,of->bqo', fused, w2_w) + w2_b

    def _L0_attn_ref(x, q_w, q_b, k_w, k_b, v_w, v_b, o_w, o_b):
        import jax, jax.numpy as jnp
        import numpy as np
        import math
        D_MODEL = 256
        NUM_HEADS = 16
        WINDOW = 64
        B, N, D = x.shape
        H = NUM_HEADS
        W = WINDOW
        dh = D // H
        nb = N // W
        Q = (x @ q_w.T + q_b).reshape(B, N, H, dh)
        K = (x @ k_w.T + k_b).reshape(B, N, H, dh)
        V = (x @ v_w.T + v_b).reshape(B, N, H, dh)
        Qb = Q.reshape(B, nb, W, H, dh)
        pad = jnp.zeros((B, W, H, dh), x.dtype)
        Kp = jnp.concatenate([pad, K], axis=1).reshape(B, nb + 1, W, H, dh)
        Vp = jnp.concatenate([pad, V], axis=1).reshape(B, nb + 1, W, H, dh)
        Kw = jnp.concatenate([Kp[:, :-1], Kp[:, 1:]], axis=2)
        Vw = jnp.concatenate([Vp[:, :-1], Vp[:, 1:]], axis=2)
        scores = jnp.einsum('bnqhd,bnkhd->bnhqk', Qb, Kw) / math.sqrt(dh)
        q_idx = jnp.arange(W)[:, None]
        k_idx = jnp.arange(2 * W)[None, :]
        rel_ok = (k_idx >= q_idx) & (k_idx <= q_idx + W)
        b_idx = jnp.arange(nb)[:, None, None]
        j_global = b_idx * W + k_idx[None] - W
        mask = rel_ok[None] & (j_global >= 0)
        scores = jnp.where(mask[None, :, None, :, :], scores, -jnp.inf)
        wts = jax.nn.softmax(scores, axis=-1)
        out = jnp.einsum('bnhqk,bnkhd->bnqhd', wts, Vw).reshape(B, N, D)
        return out @ o_w.T + o_b

    def _L0_ffn_ref(x, gate_w, wg, wu, wd):
        import jax, jax.numpy as jnp
        import numpy as np
        B, S, H = (2, 512, 256)
        E, I, K = (8, 1024, 2)

        def _moe_forward(x, gate_w, wg, wu, wd):
            b, s, h = x.shape
            x_flat = x.reshape(-1, h)
            logits = x_flat @ gate_w.T
            top_v, top_i = jax.lax.top_k(logits, K)
            probs = jax.nn.softmax(top_v.astype(jnp.float32), axis=-1).astype(logits.dtype)
            one_hot = jax.nn.one_hot(top_i, E, dtype=probs.dtype)
            combine = jnp.einsum('tk,tke->et', probs, one_hot)

            def body(acc, ws):
                wge, wue, wde, we = ws
                hidden = jax.nn.silu(x_flat @ wge.T) * (x_flat @ wue.T)
                return (acc + we[:, None] * (hidden @ wde.T), None)
            out, _ = jax.lax.scan(body, jnp.zeros_like(x_flat), (wg, wu, wd, combine))
            return out.reshape(b, s, h)
        return _moe_forward(x, gate_w, wg, wu, wd)
    x = x + _L0_xattn_ref(_layernorm(x, axis=-1), ctx_1024, L0_xattn_w1_w, L0_xattn_w1_b, L0_xattn_w2_w, L0_xattn_w2_b)
    x = x + _L0_attn_ref(_layernorm(x, axis=-1), L0_attn_q_w, L0_attn_q_b, L0_attn_k_w, L0_attn_k_b, L0_attn_v_w, L0_attn_v_b, L0_attn_o_w, L0_attn_o_b)
    x = x + _L0_ffn_ref(_layernorm(x, axis=-1), L0_ffn_gate_w, L0_ffn_wg, L0_ffn_wu, L0_ffn_wd)
    return x

_drawn_inputs = setup_inputs


def setup_inputs(seed=0):
    import zlib

    import numpy as np

    out = dict(_drawn_inputs(seed))
    spreads = {'L0_attn_q_b': (0.0, 0.8),
     'L0_attn_k_b': (0.0, 0.8),
     'L0_attn_v_b': (0.0, 0.1),
     'L0_attn_o_b': (0.0, 0.1)}
    factors = {'L0_xattn_w1_b': 8.0, 'L0_attn_q_w': 5.704, 'L0_attn_k_w': 6.781}
    for name, (base, spread) in spreads.items():
        noise = np.random.default_rng([zlib.crc32(name.encode()), seed]).standard_normal(out[name].shape)
        drawn = base * np.exp(spread * noise) if base else spread * noise
        out[name] = jnp.asarray(drawn.astype(out[name].dtype))
    for name, factor in factors.items():
        out[name] = (out[name] * factor).astype(out[name].dtype)
    return out
```

```python
import concourse.bass as bass
from concourse import mybir
from contextlib import ExitStack

F32 = mybir.dt.float32
I32 = mybir.dt.int32
ALU = mybir.AluOpType
ACT = mybir.ActivationFunctionType
X_AXIS = mybir.AxisListType.X

P = 128
BATCH, NTOK, D = 4, 256, 256
KEYS = 4096
TOK = BATCH * NTOK
TILES = TOK // P
TPB = NTOK // P
DC = D // P
KT = KEYS // P
BANK = 512
TPG = BANK // P
CHUNKS = KEYS // BANK
PIECES = 4
HEADS, DH, WIN = 16, 16, 64
SPAN = P + WIN
HC = 4
PADTOK = WIN + NTOK
E, INNER, TOPK = 8, 1024, 2
IC = INNER // P
MAT = D * INNER // P
NMAT = 3
MATGROUPS = MAT // BANK
SLOT_TILES = (TOK * TOPK + E * (P - 1)) // P
SLOTS = SLOT_TILES * P
EPS = 1e-5
LOWEST = -3.0e38
MASKED = -1.0e30
FIRST = 1
EPB = E // BATCH


def perceiver(nc, x, ctx, w1_w, w1_b, w2_w, w2_b, q_w, q_b, k_w, k_b, v_w, v_b, o_w, o_b,
              gate_w, wg, wu, wd, out):
    stack = ExitStack()
    with stack:
        def sb(name, cols, dt=F32):
            return stack.enter_context(nc.sbuf_tensor(name, [P, cols], dt))

        def sem(name):
            return stack.enter_context(nc.semaphore(name))

        wt_dram = nc.dram_tensor("turned_weights", [E, P, NMAT * MAT], F32).ap()
        xg_dram = nc.dram_tensor("rows_by_expert", [SLOTS, D], F32).ap()
        yg_dram = nc.dram_tensor("results_by_expert", [SLOTS, D], F32).ap()

        region_a = sb("region_a", 2 * KT * D)
        region_s = sb("region_s", TPB * KEYS)
        region_w = sb("region_w", 4 * MAT)

        def cut(region, widths):
            at, parts = 0, []
            for w in widths:
                parts.append(region[:, at:at + w])
                at += w
            assert at <= region.shape[1], (at, region.shape)
            return parts

        ctx_sb = [region_a[:, n * KT * D:(n + 1) * KT * D].rearrange("p (t d) -> p t d", t=KT) for n in range(2)]
        scores = [region_s[:, n * KEYS:(n + 1) * KEYS] for n in range(TPB)]
        w_nat0, w_nat1, w_turn0, w_turn1 = cut(region_w, [MAT] * 4)
        w_nat, w_turn = [w_nat0, w_nat1], [w_turn0, w_turn1]
        xn_f, xnT_f, w1_nat, w2_nat, q_nat, k_nat, v_nat, o_nat = cut(
            region_s, [TILES * D, DC * TOK, DC * D, DC * 2 * D, DC * D, DC * D, DC * D, DC * D])
        xn = xn_f.rearrange("p (t d) -> p t d", t=TILES)
        xnT = xnT_f.rearrange("p (c n) -> p c n", c=DC)
        qT_f, kT_f, va_f, vb_f, x2nT_f = cut(
            region_a, [HC * TOK, HC * BATCH * PADTOK, TILES * D, TILES * D, DC * BATCH * PADTOK])
        qT = qT_f.rearrange("p (c n) -> p c n", c=HC)
        kT = kT_f.rearrange("p (c b n) -> p c b n", c=HC, b=BATCH)
        v_first = va_f.rearrange("p (t d) -> p t d", t=TILES)
        v_last = vb_f.rearrange("p (t d) -> p t d", t=TILES)
        x2nT = x2nT_f.rearrange("p (c b n) -> p c b n", c=DC, b=BATCH)
        x2n_f, sl0, sl1, heads_f = cut(region_s, [TILES * D, HEADS // 2 * SPAN, HEADS // 2 * SPAN, TILES * D])
        x2n = x2n_f.rearrange("p (t d) -> p t d", t=TILES)
        local = [s.rearrange("p (j c k) -> p j c k", j=4, c=2) for s in (sl0, sl1)]
        heads = heads_f.rearrange("p (t d) -> p t d", t=TILES)
        headsT_f, q_st0, q_st1, k_st0, k_st1 = cut(region_w, [DC * TOK, HC * P, HC * P, HC * SPAN, HC * SPAN])
        headsT = headsT_f.rearrange("p (c n) -> p c n", c=DC)
        q_st = [s.rearrange("p (c n) -> p c n", c=HC) for s in (q_st0, q_st1)]
        k_st = [s.rearrange("p (c n) -> p c n", c=HC) for s in (k_st0, k_st1)]
        w_up = [region_a[:, n * 2 * MAT:(n + 1) * 2 * MAT] for n in range(2)]
        w_down = [region_a[:, (4 + n) * MAT:(5 + n) * MAT] for n in range(2)]
        x3n_f, x3nT_f, silu0, silu1, hid0, hid1 = cut(region_s, [TILES * D, DC * TOK] + [INNER] * 4)
        x3n = x3n_f.rearrange("p (t d) -> p t d", t=TILES)
        x3nT = x3nT_f.rearrange("p (c n) -> p c n", c=DC)
        silu, hid = [silu0, silu1], [hid0, hid1]
        xg0, xg1, xgT0, xgT1, hidT0, hidT1, yt0, yt1 = cut(
            region_w, [D] * 2 + [DC * P] * 2 + [INNER] * 2 + [D] * 2)
        xg, xgT, hidT, yt = [xg0, xg1], [xgT0, xgT1], [hidT0, hidT1], [yt0, yt1]
        y_f = region_a[:, 0:2 * TILES * D]
        y_of = y_f.rearrange("p (k t d) -> p k t d", k=TOPK, t=TILES)

        xr_t = sb("residual", TILES * D)
        xr = xr_t[:, :].rearrange("p (t d) -> p t d", t=TILES)
        bfT_t = sb("bfT", DC * TOK)
        bfT = bfT_t[:, :].rearrange("p (c n) -> p c n", c=DC)
        bf_st = [sb(f"bf_batch{n}", DC * NTOK)[:, :].rearrange("p (c n) -> p c n", c=DC) for n in range(2)]
        ctxT_t = sb("ctxT", 2 * DC * BANK)
        ctxT = ctxT_t[:, :].rearrange("p (r c n) -> p r c n", r=2, c=DC)
        pT_t = sb("probsT", 4 * BANK)
        pT = pT_t[:, :].rearrange("p (r k n) -> p r k n", r=4, k=TPG)
        w1T = sb("w1T", DC * D)[:, :].rearrange("p (c n) -> p c n", c=DC)
        w2T = sb("w2T", 2 * DC * D)[:, :].rearrange("p (c n) -> p c n", c=2 * DC)
        qwT = sb("qwT", DC * HC * P)[:, :].rearrange("p (c n) -> p c n", c=DC)
        kwT = sb("kwT", DC * HC * P)[:, :].rearrange("p (c n) -> p c n", c=DC)
        vwT = sb("vwT", DC * D)[:, :].rearrange("p (c n) -> p c n", c=DC)
        owT = sb("owT", DC * D)[:, :].rearrange("p (c n) -> p c n", c=DC)
        gwT = sb("gwT", DC * E)[:, :].rearrange("p (c e) -> p c e", c=DC)
        ident = sb("ident", P)
        zeros = sb("zeros", D)
        mask = sb("mask", TPB * SPAN)[:, :].rearrange("p (t k) -> p t k", t=TPB)
        earlier = sb("earlier", P)
        ones = sb("ones", P)
        b1c = sb("b1_cols", DC)
        qbc = sb("qb_cols", HC)
        kbc = sb("kb_cols", HC)
        b2r = sb("b2_rows", D)
        vbr = sb("vb_rows", D)
        obr = sb("ob_rows", D)
        eps_c = sb("eps", 1)
        bn = sb("ln_stats", TILES * 6)[:, :].rearrange("p (t s) -> p t s", t=TILES)
        mv = sb("ln_mean_var", TILES * 2)[:, :].rearrange("p (t s) -> p t s", t=TILES)
        sd = sb("ln_sd", TILES)
        rstd = sb("ln_rstd", TILES)
        cmax = sb("chunk_max", TPB * CHUNKS)[:, :].rearrange("p (t c) -> p t c", t=TPB)
        nmax = sb("neg_max", TPB)
        lpart = sb("piece_sums", TPB * PIECES)[:, :].rearrange("p (t c) -> p t c", t=TPB)
        lsum = sb("sums", TPB)
        linv = sb("inv_sums", TPB)
        o_sb = sb("cross_out", TPB * D)[:, :].rearrange("p (t d) -> p t d", t=TPB)
        oT = sb("cross_outT", TPB * D)[:, :].rearrange("p (t c n) -> p t c n", t=TPB, c=DC)
        hmax = sb("head_max", 2 * 8)[:, :].rearrange("p (s j c) -> p s j c", s=2, j=4)
        hsum = sb("head_sum", 2 * HEADS)[:, :].rearrange("p (t h) -> p t h", t=TPB)
        hinv = sb("head_inv", 2 * HEADS)[:, :].rearrange("p (t h) -> p t h", t=TPB)
        lo = sb("logits", TILES * E)[:, :].rearrange("p (t e) -> p t e", t=TILES)
        above = sb("above", TILES * E * E)[:, :].rearrange("p (t e f) -> p t e f", t=TILES, e=E)
        ties = sb("ties", TILES * E * E)[:, :].rearrange("p (t e f) -> p t e f", t=TILES, e=E)
        lower_i = sb("lower_i", E * E)[:, :].rearrange("p (e f) -> p e f", e=E)
        place = sb("place", TILES * E)[:, :].rearrange("p (t e) -> p t e", t=TILES)
        chosen = sb("chosen", TILES * E)[:, :].rearrange("p (t e) -> p t e", t=TILES)
        nth = [sb(f"choice{n}", TILES * E)[:, :].rearrange("p (t e) -> p t e", t=TILES) for n in range(TOPK)]
        lmax = sb("logit_max", TILES)
        ex = sb("gate_exp", TILES * E)[:, :].rearrange("p (t e) -> p t e", t=TILES)
        gsum = sb("gate_sum", TILES)
        ginv = sb("gate_inv", TILES)
        prob = [sb(f"prob{n}", TILES) for n in range(TOPK)]
        slotf = [sb(f"slotf{n}", TILES) for n in range(TOPK)]
        slot = [sb(f"slot{n}", TILES, I32) for n in range(TOPK)]
        tots = sb("tile_counts", TILES * E)[:, :].rearrange("p (t e) -> p t e", t=TILES)
        before = sb("counts_before", TILES * E)[:, :].rearrange("p (t e) -> p t e", t=TILES)
        pos = sb("positions", TILES * E)[:, :].rearrange("p (t e) -> p t e", t=TILES)
        cnt = sb("counts", E)
        steps = sb("steps", E)
        need = sb("tiles_needed", E)
        first = sb("first_tile", E)
        tileno = sb("tile_numbers", SLOT_TILES)
        owner_f = sb("owner_f", SLOT_TILES)
        owner = sb("owner", SLOT_TILES, I32)
        cmp23 = sb("owner_cmp", SLOT_TILES * (E - 1))[:, :].rearrange("p (j e) -> p j e", j=SLOT_TILES)

        psum = stack.enter_context(nc.psum_tensor("psum", [P, 8 * BANK], F32))
        bank = [psum[:, n * BANK:(n + 1) * BANK] for n in range(8)]

        consts = sem("consts")
        pool_step = sem("pool_step")
        x_loaded, small_loaded = sem("x_loaded"), sem("small_loaded")
        zero_stored = sem("zero_stored")
        ctx_loaded = [[sem(f"ctx_loaded{n}_{q}") for q in range(4)] for n in range(2)]
        w_loaded = [sem(f"w_loaded{n}") for n in range(2)]
        w_stored = [sem(f"w_stored{n}") for n in range(2)]
        dve_step = sem("dve_step")
        var_ready, sd_ready, xn_ready = sem("var_ready"), sem("sd_ready"), sem("xn_ready")
        setup_done, setup_act, setup_dve = sem("setup_done"), sem("setup_act"), sem("setup_dve")
        b1_scaled = sem("b1_scaled")
        bf_ready = sem("bf_ready")
        ctx_turned, ctxT_ready = sem("ctx_turned"), sem("ctxT_ready")
        scores_done, scores_out = sem("scores_done"), sem("scores_out")
        max_ready, exp_done = sem("max_ready"), sem("exp_done")
        probs_turned, probsT_ready, pv_done = sem("probs_turned"), sem("probsT_ready"), sem("pv_done")
        w_turned, w_out = sem("w_turned"), sem("w_out")
        o_ready, o_turned, oT_ready = sem("o_ready"), sem("o_turned"), sem("oT_ready")
        fused_done, x1_ready = sem("fused_done"), sem("x1_ready")
        p2_done, p2_act, p2_dve = sem("p2_done"), sem("p2_act"), sem("p2_dve")
        staged = sem("staged")
        local_done, local_out = sem("local_done"), sem("local_out")
        centred, local_exp = sem("centred"), sem("local_exp")
        first_turned, last_turned = sem("first_turned"), sem("last_turned")
        first_ready, last_ready = sem("first_ready"), sem("last_ready")
        localpv_done, heads_ready = sem("localpv_done"), sem("heads_ready")
        p2c_done, p2c_act, x2_ready = sem("p2c_done"), sem("p2c_act"), sem("x2_ready")
        p3_done, p3_act, logits_out = sem("p3_done"), sem("p3_act"), sem("logits_out")
        lm_ready, gate_exp = sem("lm_ready"), sem("gate_exp_done")
        chosen_ready, ranks_done = sem("chosen_ready"), sem("ranks_done")
        slots_ready = sem("slots_ready")
        scattered = sem("scattered")
        up_loaded = [sem(f"up_loaded{n}") for n in range(2)]
        down_loaded = [sem(f"down_loaded{n}") for n in range(2)]
        xg_loaded = [sem(f"xg_loaded{n}") for n in range(2)]
        xg_turned, xgT_ready = sem("xg_turned"), sem("xgT_ready")
        g_done, u_done = sem("g_done"), sem("u_done")
        silu_ready, hid_ready = sem("silu_ready"), sem("hid_ready")
        hid_turned, hidT_ready = sem("hid_turned"), sem("hidT_ready")
        y_done, y_ready = sem("y_done"), sem("y_ready")
        y_stored = [sem(f"y_stored{n}") for n in range(2)]
        gathered = [sem(f"gathered{n}") for n in range(TILES)]
        out_ready, out_stored = sem("out_ready"), sem("out_stored")

        rooms = [w_turned, pv_done, scores_done, local_done, o_ready, localpv_done, probs_turned, *w_stored, last_turned,
                 probsT_ready, scores_out, w_out, x1_ready, oT_ready, local_out, first_ready, last_ready, heads_ready, *y_stored]

        small = [(w1_nat.rearrange("p (c n) -> p c n", c=DC), w1_w.rearrange("(c p) n -> p c n", p=P)),
                 (w2_nat.rearrange("p (c n) -> p c n", c=DC), w2_w.rearrange("(c p) n -> p c n", p=P)),
                 (q_nat.rearrange("p (c n) -> p c n", c=DC), q_w.rearrange("(c p) n -> p c n", p=P)),
                 (k_nat.rearrange("p (c n) -> p c n", c=DC), k_w.rearrange("(c p) n -> p c n", p=P)),
                 (v_nat.rearrange("p (c n) -> p c n", c=DC), v_w.rearrange("(c p) n -> p c n", p=P)),
                 (o_nat.rearrange("p (c n) -> p c n", c=DC), o_w.rearrange("(c p) n -> p c n", p=P)),
                 (b1c[:, :], w1_b.rearrange("(c p) -> p c", p=P)),
                 (b2r[:, :], w2_b.rearrange("(a n) -> a n", a=1).broadcast_to([P, D])),
                 (vbr[:, :], v_b.rearrange("(a n) -> a n", a=1).broadcast_to([P, D])),
                 (obr[:, :], o_b.rearrange("(a n) -> a n", a=1).broadcast_to([P, D])),
                 ]
        for c in range(DC):
            small.append((gwT[:, c, :], gate_w[:, c * P:(c + 1) * P].rearrange("e p -> p e")))
        for j in range(4):
            small += [(cols[32 * j:32 * j + DH, :], b.rearrange("(c j i) -> j i c", j=4, i=DH)[j])
                      for cols, b in ((qbc, q_b), (kbc, k_b))]
        N_SMALL = len(small)
        N_CONST = 14

        block = stack.enter_context(nc.Block())

        @block.sync
        def _(sp):
            sp.dma_start(xr, x.rearrange("b (t p) d -> p (b t) d", p=P)).then_inc(x_loaded, 16)
            sp.wait_ge(consts, N_CONST)
            for dst, src in small:
                with nc.allow_non_contiguous_dma(reason="a few small columns, once"):
                    sp.dma_start(dst, src).then_inc(small_loaded, 16)

            def load_ctx(b, i, n):
                src = ctx[bass.ds(b, 1)].rearrange("a (p t) d -> p (a t) d", p=P)
                for q in range(4):
                    t = slice(q * KT // 4, (q + 1) * KT // 4)
                    sp.dma_start(ctx_sb[n][:, t, :], src[:, t, :]).then_inc(ctx_loaded[n][q], 16)

            def load_piece(b, k):
                e = b * EPB + k // NMAT
                m = k % NMAT
                if k >= 2:
                    sp.wait_ge(w_turned, b * (EPB * NMAT * MATGROUPS) + (k - 1) * MATGROUPS + FIRST)
                else:
                    sp.wait_ge(w_turned, b * (EPB * NMAT * MATGROUPS) + FIRST)
                if m < 2:
                    src = (wg, wu)[m][bass.ds(e, 1)].rearrange("a (c p) n -> p (a c) n", p=P)
                    dst = w_nat[k % 2].rearrange("p (c n) -> p c n", c=IC)
                else:
                    src = wd[bass.ds(e, 1)].rearrange("a (c p) n -> p (a c) n", p=P)
                    dst = w_nat[k % 2].rearrange("p (c n) -> p c n", c=DC)
                sp.dma_start(dst, src).then_inc(w_loaded[k % 2], 16)

            def store_piece(b, k):
                e = b * EPB + k // NMAT
                m = k % NMAT
                sp.wait_ge(w_out, b * (EPB * NMAT * MATGROUPS) + (k + 1) * MATGROUPS + FIRST)
                sp.dma_start(wt_dram[bass.ds(e, 1), :, m * MAT:(m + 1) * MAT].rearrange("a p n -> p (a n)"),
                             w_turn[k % 2]).then_inc(w_stored[k % 2], 16)

            load_ctx(0, 0, 0)

            def two_batches(i, more):
                for n in range(2):
                    b = i * 2 + n
                    load_piece(b, 0)
                    load_piece(b, 1)
                    if n == 0:
                        sp.wait_ge(pv_done, b * (TPB * CHUNKS) + FIRST)
                        load_ctx(b + 1, i, 1)
                    for k in range(EPB * NMAT):
                        store_piece(b, k)
                        if k + 2 < EPB * NMAT:
                            load_piece(b, k + 2)
                    if n == 1 and more:
                        sp.wait_ge(pv_done, b * (TPB * CHUNKS) + FIRST)
                        load_ctx(b + 1, i, 0)

            with sp.Fori(0, BATCH // 2 - 1) as i:
                two_batches(i, True)
            two_batches(BATCH // 2 - 1, False)

            sp.wait_ge(slots_ready, 1)
            for n in range(2):
                sp.wait_ge(w_stored[n], 16 * E * NMAT // 2 + FIRST)
            sp.wait_ge(scattered, 16 * TOPK * TILES)

            def load_tile(j, n, waits):
                if waits:
                    sp.wait_ge(xg_turned, j - 1)
                e = sp.value_load(owner[0:1, bass.ds(j, 1)], min_val=0, max_val=E - 1)
                sp.dma_start(xg[n], xg_dram[bass.ds(j * P, P), :]).then_inc(xg_loaded[n], 16)
                rows = wt_dram[bass.ds(e, 1), :, :].rearrange("a p n -> p (a n)")
                if waits:
                    sp.wait_ge(u_done, (j - 1) * 2)
                sp.dma_start(w_up[n], rows[:, 0:2 * MAT]).then_inc(up_loaded[n], 16)
                if waits:
                    sp.wait_ge(y_done, j - 1)
                sp.dma_start(w_down[n], rows[:, 2 * MAT:3 * MAT]).then_inc(down_loaded[n], 16)

            for n in range(2):
                load_tile(n, n, False)
            with sp.Fori(2, SLOT_TILES - 1, 2) as j2:
                for n in range(2):
                    load_tile(j2 + n, n, True)
            load_tile(SLOT_TILES - 1, 0, True)

            for t in range(TILES):
                sp.wait_ge(out_ready, t + 1)
                sp.dma_start(out.rearrange("b (t p) d -> p (b t) d", p=P)[:, t, :], x3n[:, t, :]).then_inc(out_stored, 16)
            sp.wait_ge(out_stored, 16 * TILES)

        @block.gpsimd
        def _(pool):
            for room in rooms:
                pool.sem_inc(room, FIRST)
            nc.gpsimd.memset(zeros[:, :], 0.0).then_inc(consts, 1)
            nc.gpsimd.memset(qbc[:, :], 0.0).then_inc(consts, 1)
            nc.gpsimd.memset(kbc[:, :], 0.0).then_inc(consts, 1)
            nc.gpsimd.memset(qwT, 0.0).then_inc(consts, 1)
            nc.gpsimd.memset(kwT, 0.0).then_inc(consts, 1)
            nc.gpsimd.memset(eps_c[:, :], EPS).then_inc(consts, 1)
            nc.gpsimd.memset(ones[:, :], 1.0).then_inc(consts, 1)
            nc.gpsimd.memset(ident[:, :], 0.0).then_inc(pool_step, 1)
            nc.gpsimd.memset(mask, 0.0).then_inc(pool_step, 1)
            nc.gpsimd.memset(lower_i, 1.0).then_inc(pool_step, 1)
            pool.wait_ge(pool_step, 3)
            nc.gpsimd.affine_select(out=ident[:, :], in_=ident[:, :], compare_op=ALU.not_equal, fill=1.0, base=0,
                                    pattern=[[-1, P]], channel_multiplier=1).then_inc(consts, 1)
            nc.gpsimd.affine_select(out=earlier[:, :], in_=ones[:, :], compare_op=ALU.is_gt, fill=0.0, base=0,
                                    pattern=[[1, P]], channel_multiplier=-1).then_inc(consts, 1)
            nc.gpsimd.affine_select(out=lower_i, in_=lower_i, compare_op=ALU.is_gt, fill=0.0, base=0,
                                    pattern=[[1, E], [-1, E]], channel_multiplier=0).then_inc(consts, 1)
            nc.gpsimd.iota(steps[:, :], pattern=[[P, E]], base=0, channel_multiplier=0,
                           allow_small_or_imprecise_dtypes=True).then_inc(consts, 1)
            nc.gpsimd.iota(tileno[:, :], pattern=[[1, SLOT_TILES]], base=0, channel_multiplier=0,
                           allow_small_or_imprecise_dtypes=True).then_inc(consts, 1)
            nc.gpsimd.affine_select(out=mask, in_=mask, compare_op=ALU.is_ge, fill=MASKED, base=0,
                                    pattern=[[0, TPB], [1, SPAN]], channel_multiplier=-1).then_inc(pool_step, 1)
            pool.wait_ge(pool_step, 4)
            nc.gpsimd.affine_select(out=mask, in_=mask, compare_op=ALU.is_ge, fill=MASKED, base=WIN,
                                    pattern=[[0, TPB], [-1, SPAN]], channel_multiplier=1).then_inc(pool_step, 1)
            pool.wait_ge(pool_step, 5)
            nc.gpsimd.affine_select(out=mask[:, 0, :], in_=mask[:, 0, :], compare_op=ALU.is_ge, fill=MASKED, base=-WIN,
                                    pattern=[[1, SPAN]], channel_multiplier=0).then_inc(consts, 2)
            pool.wait_ge(consts, N_CONST)
            pool.dma_start(xg_dram.rearrange("(t p) d -> p t d", p=P),
                           zeros[:, :].rearrange("p (a d) -> p a d", a=1).broadcast_to([P, SLOT_TILES, D])).then_inc(zero_stored, 16)

            pool.wait_ge(setup_act, 11)
            with pool.Fori(0, BATCH // 2) as i:
                pool.wait_ge(scores_done, i * (2 * TPB * CHUNKS) + FIRST)
                for n in range(2):
                    nc.gpsimd.tensor_copy(bf_st[n], bfT[:, :, bass.ds(i * (2 * NTOK) + n * NTOK, NTOK)]).then_inc(bf_ready, 1)

            pool.wait_ge(pv_done, BATCH * TPB * CHUNKS + FIRST)
            nc.gpsimd.memset(x2nT[:, :, :, 0:WIN], 0.0).then_inc(staged, 1)
            nc.gpsimd.memset(kT[:, :, :, 0:WIN], 0.0).then_inc(staged, 1)
            pool.wait_ge(p2_act, 4 + 4 * HC)
            pool.wait_ge(w_stored[0], 16 * E * NMAT // 2 + FIRST)
            pool.wait_ge(w_stored[1], 16 * E * NMAT // 2 + FIRST)
            pool.wait_ge(staged, 2)
            with pool.Fori(0, BATCH) as b:
                pool.wait_ge(local_done, b * (2 * TPB) + FIRST)
                for t in range(TPB):
                    nc.gpsimd.tensor_copy(q_st[t], qT[:, :, bass.ds(b * NTOK + t * P, P)]).then_inc(staged, 1)
                    nc.gpsimd.tensor_copy(k_st[t], kT[:, :, bass.ds(b, 1), t * P:t * P + SPAN].rearrange("p c a n -> p c (a n)")).then_inc(staged, 1)

            pool.wait_ge(slots_ready, 1)
            pool.wait_ge(zero_stored, 16)
            for t in range(TILES):
                for n in range(TOPK):
                    pool.indirect_dma_start(
                        out=xg_dram, out_offset=bass.IndirectOffsetOnAxis(ap=slot[n][:, t:t + 1], axis=0),
                        in_=x3n[:, t, :], in_offset=None).then_inc(scattered, 16)
            pool.wait_ge(y_stored[0], 16 * ((SLOT_TILES + 1) // 2) + FIRST)
            pool.wait_ge(y_stored[1], 16 * (SLOT_TILES // 2) + FIRST)
            for t in range(TILES):
                for n in range(TOPK):
                    pool.indirect_dma_start(
                        out=y_of[:, n, t, :], out_offset=None,
                        in_=yg_dram, in_offset=bass.IndirectOffsetOnAxis(ap=slot[n][:, t:t + 1], axis=0)).then_inc(gathered[t], 16)

        @block.scalar
        def _(act):
            def sqrt_of_var(k):
                act.wait_ge(var_ready, k)
                nc.scalar.activation(sd[:, :], mv[:, :, 1], ACT.Sqrt, bias=eps_c[:, :]).then_inc(sd_ready, 1)

            def copy(dst, src):
                return nc.scalar.activation(dst, src, ACT.Copy)

            act.wait_ge(consts, N_CONST)
            act.wait_ge(small_loaded, 16 * N_SMALL)
            nc.scalar.activation(b1c[:, :], b1c[:, :], ACT.Copy, scale=float(D) ** -0.5).then_inc(b1_scaled, 1)
            sqrt_of_var(1)
            for s in range(4):
                act.wait_ge(setup_done, s + 1)
                copy(xnT[:, s // 2, (s % 2) * BANK:(s % 2 + 1) * BANK], bank[s]).then_inc(setup_act, 1)
            act.wait_ge(setup_done, 5)
            copy(w1T, bank[4].rearrange("p (c n) -> p c n", c=DC)).then_inc(setup_act, 1)
            for s in range(2):
                act.wait_ge(setup_done, 6 + s)
                copy(w2T[:, 2 * s:2 * s + 2, :], bank[5 + s].rearrange("p (c n) -> p c n", c=2)).then_inc(setup_act, 1)
            act.wait_ge(b1_scaled, 1)
            for s in range(4):
                act.wait_ge(setup_done, 8 + s)
                kc, half = s // 2, s % 2
                nc.scalar.activation(bfT[:, kc, half * BANK:(half + 1) * BANK], bank[(7 + s) % 8], ACT.Identity,
                                     bias=b1c[:, kc:kc + 1], scale=float(D) ** -0.5).then_inc(setup_act, 1)
            for s, (dst, padded) in enumerate(((qwT, True), (kwT, True), (vwT, False), (owT, False))):
                act.wait_ge(setup_done, 16 + s)
                src = bank[(15 + s) % 8]
                if padded:
                    for c in range(DC):
                        last = copy(dst[:, c, :].rearrange("p (h s) -> p h s", s=32)[:, :, 0:DH],
                                    src[:, c * D:(c + 1) * D].rearrange("p (h i) -> p h i", i=DH))
                else:
                    last = copy(dst, src.rearrange("p (c n) -> p c n", c=DC))
                last.then_inc(setup_act, 1)

            with act.Fori(0, BATCH) as b:
                for ch in range(CHUNKS):
                    for c in range(DC):
                        act.wait_ge(ctx_turned, b * (CHUNKS * DC) + (ch * DC + c + 1))
                        if c == 0:
                            act.wait_ge(scores_done, b * (CHUNKS * TPB) + max(ch - 1, 0) * TPB + FIRST)
                        copy(ctxT[:, ch % 2, c, :], bank[c]).then_inc(ctxT_ready, 1)
                for t in range(TPB):
                    act.wait_ge(max_ready, b * TPB + t + 1)
                    if t == 0:
                        act.wait_ge(o_ready, b * TPB + FIRST)
                    for k in range(PIECES):
                        part = scores[t][:, k * (KEYS // PIECES):(k + 1) * (KEYS // PIECES)]
                        nc.scalar.activation(part, part, ACT.Exp, bias=nmax[:, t:t + 1],
                                             accum_out=lpart[:, t, k:k + 1]).then_inc(exp_done, 1)

            sqrt_of_var(2)
            act.wait_ge(staged, 2)
            for s in range(4):
                act.wait_ge(p2_done, s + 1)
                c, half = s // 2, s % 2
                copy(x2nT[:, c, 2 * half:2 * half + 2, WIN:PADTOK],
                     bank[s].rearrange("p (b n) -> p b n", b=2)).then_inc(p2_act, 1)
            for s in range(4, 4 + 2 * HC):
                act.wait_ge(p2_done, s + 1)
                c, half = (s - 4) // 2, s % 2
                nc.scalar.activation(qT[:, c, half * BANK:(half + 1) * BANK], bank[s % 8], ACT.Identity,
                                     bias=qbc[:, c:c + 1]).then_inc(p2_act, 1)
            for s in range(4 + 2 * HC, 4 + 4 * HC):
                act.wait_ge(p2_done, s + 1)
                c, half = (s - 4 - 2 * HC) // 2, s % 2
                nc.scalar.activation(kT[:, c, 2 * half:2 * half + 2, WIN:PADTOK],
                                     bank[s % 8].rearrange("p (b n) -> p b n", b=2), ACT.Identity,
                                     bias=kbc[:, c:c + 1]).then_inc(p2_act, 1)

            with act.Fori(0, BATCH) as b:
                def local_softmax(n):
                    act.wait_ge(centred, b * 4 + n + 1)
                    flat = (sl0, sl1)[n % 2]
                    nc.scalar.activation(flat, flat, ACT.Exp, scale=float(DH) ** -0.5).then_inc(local_exp, 1)

                def local_turn(n):
                    for g in range(2):
                        act.wait_ge(first_turned, b * 8 + n * 2 + g + 1)
                        if g == 0:
                            act.wait_ge(localpv_done, b * 4 + n + FIRST)
                        copy(pT[:, g], bank[4 + g].rearrange("p (k n) -> p k n", k=4)).then_inc(first_ready, 1)
                        act.wait_ge(last_turned, b * 8 + n * 2 + g + 1 + FIRST)
                        copy(pT[0:WIN, 2 + g], bank[6][0:WIN].rearrange("p (k n) -> p k n", k=4)).then_inc(last_ready, 1)

                local_softmax(0)
                local_softmax(1)
                local_turn(0)
                local_softmax(2)
                local_turn(1)
                local_softmax(3)
                local_turn(2)
                local_turn(3)

            for s in range(4):
                act.wait_ge(p2c_done, s + 1)
                copy(headsT[:, s // 2, (s % 2) * BANK:(s % 2 + 1) * BANK], bank[s]).then_inc(p2c_act, 1)

            sqrt_of_var(3)
            for s in range(4):
                act.wait_ge(p3_done, s + 1)
                copy(x3nT[:, s // 2, (s % 2) * BANK:(s % 2 + 1) * BANK], bank[s]).then_inc(p3_act, 1)
            act.wait_ge(lm_ready, 1)
            nc.scalar.activation(ex, ex, ACT.Exp).then_inc(gate_exp, 1)

            def tile_silu(j, n):
                for half in range(2):
                    act.wait_ge(g_done, j * 2 + half + 1)
                    if half == 0 and j is not 0:
                        act.wait_ge(hid_ready, j)
                    nc.scalar.activation(silu[n][:, half * BANK:(half + 1) * BANK], bank[half], ACT.Silu).then_inc(silu_ready, 1)

            def tile_hidT(j, n):
                for half in range(2):
                    act.wait_ge(hid_turned, j * 2 + half + 1)
                    copy(hidT[n][:, half * BANK:(half + 1) * BANK], bank[4 + half]).then_inc(hidT_ready, 1)

            def tile_store(j, n):
                act.wait_ge(y_ready, j + 1)
                act.dma_start(yg_dram[bass.ds(j * P, P), :], yt[n]).then_inc(y_stored[n], 16)

            tile_silu(0, 0)
            with act.Fori(1, SLOT_TILES, 2) as j2:
                for n in range(2):
                    tile_silu(j2 + n, 1 - n)
                    tile_hidT(j2 + (n - 1), n)
                    tile_store(j2 + (n - 1), n)
            tile_hidT(SLOT_TILES - 1, 0)
            tile_store(SLOT_TILES - 1, 0)

        @block.vector
        def _(dve):
            step = [0]

            def then(ins):
                step[0] += 1
                ins.then_inc(dve_step, 1)
                dve.wait_ge(dve_step, step[0])

            def layer_norm(dst, k):
                for t in range(TILES):
                    last = nc.vector.bn_stats(bn[:, t, :], xr[:, t, :])
                then(last)
                for t in range(TILES):
                    last = nc.vector.bn_aggr(mv[:, t, :], bn[:, t, :])
                last.then_inc(var_ready, 1)
                dve.wait_ge(sd_ready, k)
                then(nc.vector.reciprocal(rstd[:, :], sd[:, :]))
                for t in range(TILES):
                    nc.vector.tensor_scalar(dst[:, t, :], xr[:, t, :], mv[:, t, 0:1], rstd[:, t:t + 1],
                                            ALU.subtract, ALU.mult).then_inc(xn_ready, 1)

            dve.wait_ge(x_loaded, 16)
            layer_norm(xn, 1)
            for s in range(4):
                dve.wait_ge(setup_done, 12 + s)
                part = xr[:, 2 * s:2 * s + 2, :]
                then(nc.vector.tensor_tensor(part, part, bank[(11 + s) % 8].rearrange("p (t d) -> p t d", t=2), ALU.add))
                if s == 0:
                    dve.wait_ge(small_loaded, 16 * N_SMALL)
                nc.vector.tensor_tensor(part, part, b2r[:, :].rearrange("p (a d) -> p a d", a=1).broadcast_to([P, 2, D]),
                                        ALU.add).then_inc(setup_dve, 1)

            step_at = step[0]
            PER = 4
            with dve.Fori(0, BATCH) as b:
                mine = [0]

                def then_b(ins):
                    mine[0] += 1
                    ins.then_inc(dve_step, 1)
                    dve.wait_ge(dve_step, b * PER + (step_at + mine[0]))

                dve.wait_ge(probs_turned, b * (TPB * CHUNKS) + FIRST)
                for ch in range(CHUNKS):
                    for t in range(TPB):
                        dve.wait_ge(scores_done, b * (CHUNKS * TPB) + (ch * TPB + t + 1) + FIRST)
                        nc.vector.tensor_scalar(scores[t][:, ch * BANK:(ch + 1) * BANK], bank[2 + t], 1.0, LOWEST, ALU.mult, ALU.max,
                                                accum_out=cmax[:, t, ch:ch + 1]).then_inc(scores_out, 1)
                    for g in range(3 * ch, 3 * ch + 3):
                        k = g // MATGROUPS
                        if g % MATGROUPS == 0:
                            dve.wait_ge(w_stored[k % 2], b * (16 * EPB * NMAT // 2) + 16 * (k // 2) + FIRST)
                        dve.wait_ge(w_turned, b * (EPB * NMAT * MATGROUPS) + g + 1 + FIRST)
                        nc.vector.tensor_copy(w_turn[k % 2][:, (g % MATGROUPS) * BANK:(g % MATGROUPS + 1) * BANK],
                                              bank[4 + g % 2]).then_inc(w_out, 1)
                dve.wait_ge(scores_out, b * (CHUNKS * TPB) + CHUNKS * TPB + FIRST)
                for t in range(TPB):
                    nc.vector.tensor_reduce(nmax[:, t:t + 1], cmax[:, t, :], axis=X_AXIS, op=ALU.max, negate=True).then_inc(max_ready, 1)

                def probs_out(g):
                    dve.wait_ge(probs_turned, b * (TPB * CHUNKS) + g + 1 + FIRST)
                    dve.wait_ge(pv_done, b * (TPB * CHUNKS) + max(g - 3, 0) + FIRST)
                    nc.vector.tensor_copy(pT[:, g % 4], bank[g % 2].rearrange("p (k n) -> p k n", k=TPG)).then_inc(probsT_ready, 1)

                def normalise(t):
                    dve.wait_ge(exp_done, b * (TPB * PIECES) + (t + 1) * PIECES)
                    then_b(nc.vector.tensor_reduce(lsum[:, t:t + 1], lpart[:, t, :], axis=X_AXIS, op=ALU.add))
                    then_b(nc.vector.reciprocal(linv[:, t:t + 1], lsum[:, t:t + 1]))
                    dve.wait_ge(pv_done, b * (TPB * CHUNKS) + (t + 1) * CHUNKS + FIRST)
                    nc.vector.tensor_scalar(o_sb[:, t, :], bank[6][:, 0:D], linv[:, t:t + 1], None, ALU.mult).then_inc(o_ready, 1)

                for g in range(CHUNKS + 1):
                    probs_out(g)
                normalise(0)
                for g in range(CHUNKS + 1, TPB * CHUNKS):
                    probs_out(g)
                normalise(1)
                for t in range(TPB):
                    dve.wait_ge(o_turned, b * TPB + t + 1)
                    nc.vector.tensor_copy(oT[:, t], bank[7][:, t * D:(t + 1) * D].rearrange("p (c n) -> p c n", c=DC)).then_inc(oT_ready, 1)
                dve.wait_ge(fused_done, b + 1)
                part = xr[:, bass.ds(b * TPB, TPB), :]
                nc.vector.tensor_tensor(part, part, bank[6].rearrange("p (t d) -> p t d", t=TPB), ALU.add).then_inc(x1_ready, 1)
                assert mine[0] == PER
            step[0] += BATCH * PER

            dve.wait_ge(x1_ready, BATCH + FIRST)
            dve.wait_ge(probs_turned, BATCH * TPB * CHUNKS + FIRST)
            layer_norm(x2n, 2)
            for b in range(BATCH):
                for part, rows in enumerate((P, WIN)):
                    s = 4 + 4 * HC + 2 * b + part
                    dve.wait_ge(p2_done, s + 1)
                    nc.vector.tensor_tensor((v_first, v_last)[part][0:rows, 2 * b:2 * b + 2, :],
                                            bank[s % 8][0:rows].rearrange("p (t d) -> p t d", t=2),
                                            vbr[0:rows, :].rearrange("p (a d) -> p a d", a=1).broadcast_to([rows, 2, D]),
                                            ALU.add).then_inc(p2_dve, 1)
            step_at2 = step[0]
            PER2 = 2 * 4 + 4
            with dve.Fori(0, BATCH) as b:
                mine2 = [0]

                def then_l(ins):
                    mine2[0] += 1
                    ins.then_inc(dve_step, 1)
                    dve.wait_ge(dve_step, b * PER2 + (step_at2 + mine2[0]))

                def centre(n):
                    t = n // 2
                    dve.wait_ge(local_done, b * 4 + n + 1 + FIRST)
                    dve.wait_ge(last_turned, b * 8 + max(n - 1, 0) * 2 + FIRST)
                    s = local[n % 2]
                    psl = psum[:, 0:4 * BANK].rearrange("p (j c k) -> p j c k", j=4, c=2)[:, :, :, 0:SPAN]
                    for c in range(2):
                        last = nc.vector.tensor_tensor(s[:, :, c, :], psl[:, :, c, :],
                                                       mask[:, t:t + 1, :].broadcast_to([P, 4, SPAN]), ALU.add)
                    last.then_inc(local_out, 1)
                    dve.wait_ge(local_out, b * 4 + n + 1 + FIRST)
                    m = hmax[:, n % 2]
                    then_l(nc.vector.tensor_reduce(m, s, axis=X_AXIS, op=ALU.max))
                    f = (sl0, sl1)[n % 2].rearrange("p (h k) -> p h k", k=SPAN)
                    mf = m.rearrange("p j c -> p (j c)").rearrange("p (h a) -> p h a", a=1)
                    nc.vector.tensor_tensor(f, f, mf.broadcast_to([P, 8, SPAN]), ALU.subtract).then_inc(centred, 1)

                def sums(n):
                    t, h = n // 2, n % 2
                    dve.wait_ge(local_exp, b * 4 + n + 1)
                    dst = hsum[:, t, 8 * h:8 * h + 8].rearrange("p (c j) -> p j c", c=2)
                    then_l(nc.vector.tensor_reduce(dst, local[n % 2], axis=X_AXIS, op=ALU.add))

                def out_heads(t):
                    then_l(nc.vector.reciprocal(hinv[:, t, :], hsum[:, t, :]))
                    dve.wait_ge(localpv_done, b * 4 + 2 * t + 2 + FIRST)
                    inv = hinv[:, t, :].rearrange("p (h a) -> p h a", a=1).broadcast_to([P, HEADS, DH])
                    nc.vector.tensor_tensor(heads[:, bass.ds(b * TPB + t, 1), :].rearrange("p a (h i) -> p (a h) i", h=HEADS),
                                            bank[7][:, 0:D].rearrange("p (h i) -> p h i", h=HEADS), inv, ALU.mult).then_inc(heads_ready, 1)

                centre(0)
                centre(1)
                sums(0)
                centre(2)
                sums(1)
                out_heads(0)
                centre(3)
                sums(2)
                sums(3)
                then_l(nc.vector.memset(hmax[:, 0], 0.0))
                then_l(nc.vector.memset(hmax[:, 1], 0.0))
                out_heads(1)
                assert mine2[0] == PER2, mine2
            step[0] += BATCH * PER2
            for s in range(4):
                dve.wait_ge(p2c_done, 4 + s + 1)
                part = xr[:, 2 * s:2 * s + 2, :]
                then(nc.vector.tensor_tensor(part, part, bank[4 + s].rearrange("p (t d) -> p t d", t=2), ALU.add))
                then(nc.vector.tensor_tensor(part, part, obr[:, :].rearrange("p (a d) -> p a d", a=1).broadcast_to([P, 2, D]), ALU.add))

            layer_norm(x3n, 3)
            dve.wait_ge(p3_done, 5)
            then(nc.vector.tensor_copy(lo, bank[4][:, 0:TILES * E].rearrange("p (t e) -> p t e", t=TILES)))
            for t in range(TILES):
                other = lo[:, t, :].rearrange("p (a f) -> p a f", a=1).broadcast_to([P, E, E])
                own = lo[:, t, :].rearrange("p (e a) -> p e a", a=1).broadcast_to([P, E, E])
                nc.vector.tensor_tensor(above[:, t], other, own, ALU.is_gt)
                last = nc.vector.tensor_tensor(ties[:, t], other, own, ALU.is_equal)
            then(last)
            flat = "p t e f -> p t (e f)"
            low = lower_i.rearrange("p e f -> p (e f)").rearrange("p (a n) -> p a n", a=1).broadcast_to([P, TILES, E * E])
            then(nc.vector.tensor_tensor(ties.rearrange(flat), ties.rearrange(flat), low, ALU.mult))
            then(nc.vector.tensor_tensor(above.rearrange(flat), above.rearrange(flat), ties.rearrange(flat), ALU.add))
            then(nc.vector.tensor_reduce(place, above, axis=X_AXIS, op=ALU.add))
            nc.vector.tensor_scalar(chosen, place, float(TOPK) - 0.5, None, ALU.is_lt).then_inc(chosen_ready, 1)
            for n in range(TOPK):
                nc.vector.tensor_scalar(nth[n], place, float(n), None, ALU.is_equal)
            then(nc.vector.tensor_reduce(lmax[:, :], lo, axis=X_AXIS, op=ALU.max))

            def over_e(col):
                return col.rearrange("p (t a) -> p t a", a=1).broadcast_to([P, TILES, E])

            nc.vector.tensor_tensor(ex, lo, over_e(lmax[:, :]), ALU.subtract).then_inc(lm_ready, 1)
            dve.wait_ge(ranks_done, 1)
            nc.vector.tensor_copy(pos, bank[5][:, 0:TILES * E].rearrange("p (t e) -> p t e", t=TILES))
            then(nc.vector.tensor_copy(tots, bank[5][:, TILES * E:2 * TILES * E].rearrange("p (t e) -> p t e", t=TILES)))
            by_t = above
            for e in range(E):
                last = nc.vector.tensor_tensor(by_t[:, e], tots[:, :, e].rearrange("p (a t) -> p a t", a=1).broadcast_to([P, TILES, TILES]),
                                               lower_i, ALU.mult)
            nc.vector.tensor_reduce(cnt[:, :], tots.rearrange("p t e -> p e t"), axis=X_AXIS, op=ALU.add)
            then(nc.vector.tensor_scalar(ginv[:, :], ginv0 := lmax[:, :], 0.0, None, ALU.mult))
            nc.vector.tensor_reduce(before.rearrange("p t e -> p e t"), by_t, axis=X_AXIS, op=ALU.add)
            cmp = ties[:, 0]
            then(nc.vector.tensor_tensor(cmp, cnt[:, :].rearrange("p (e a) -> p e a", a=1).broadcast_to([P, E, E]),
                                         steps[:, :].rearrange("p (a k) -> p a k", a=1).broadcast_to([P, E, E]), ALU.is_gt))
            then(nc.vector.tensor_reduce(need[:, :], cmp, axis=X_AXIS, op=ALU.add))
            then(nc.vector.tensor_tensor(ties[:, 1], need[:, :].rearrange("p (a f) -> p a f", a=1).broadcast_to([P, E, E]), lower_i, ALU.mult))
            then(nc.vector.tensor_reduce(first[:, :], ties[:, 1], axis=X_AXIS, op=ALU.add))
            nc.vector.tensor_tensor(pos, pos, before, ALU.add)
            then(nc.vector.tensor_tensor(cmp23, tileno[:, :].rearrange("p (j a) -> p j a", a=1).broadcast_to([P, SLOT_TILES, E - 1]),
                                         first[:, 1:E].rearrange("p (a e) -> p a e", a=1).broadcast_to([P, SLOT_TILES, E - 1]), ALU.is_ge))
            then(nc.vector.tensor_reduce(owner_f[:, :], cmp23, axis=X_AXIS, op=ALU.add))
            nc.vector.tensor_copy(owner[:, :], owner_f[:, :])
            then(nc.vector.tensor_scalar(need[:, :], first[:, :], float(P), None, ALU.mult))
            then(nc.vector.tensor_tensor(pos, pos, need[:, :].rearrange("p (a e) -> p a e", a=1).broadcast_to([P, TILES, E]), ALU.add))
            for n in range(TOPK):
                then(nc.vector.tensor_tensor(before, pos, nth[n], ALU.mult))
                then(nc.vector.tensor_reduce(slotf[n][:, :], before, axis=X_AXIS, op=ALU.add))
                last = nc.vector.tensor_copy(slot[n][:, :], slotf[n][:, :])
            last.then_inc(slots_ready, 1)
            dve.wait_ge(gate_exp, 1)
            then(nc.vector.tensor_tensor(ex, ex, chosen, ALU.mult))
            then(nc.vector.tensor_reduce(gsum[:, :], ex, axis=X_AXIS, op=ALU.add))
            then(nc.vector.reciprocal(ginv[:, :], gsum[:, :]))
            then(nc.vector.tensor_tensor(ex, ex, over_e(ginv[:, :]), ALU.mult))
            for n in range(TOPK):
                then(nc.vector.tensor_tensor(pos, ex, nth[n], ALU.mult))
                then(nc.vector.tensor_reduce(prob[n][:, :], pos, axis=X_AXIS, op=ALU.add))

            def tile_xgT(j, n):
                dve.wait_ge(xg_turned, j + 1)
                nc.vector.tensor_copy(xgT[n], bank[7][:, 0:DC * P]).then_inc(xgT_ready, 1)

            def tile_hid(j, n):
                for half in range(2):
                    dve.wait_ge(silu_ready, j * 2 + half + 1)
                    dve.wait_ge(u_done, j * 2 + half + 1)
                    cols = slice(half * BANK, (half + 1) * BANK)
                    last = nc.vector.tensor_tensor(hid[n][:, cols], silu[n][:, cols], bank[2 + half], ALU.mult)
                last.then_inc(hid_ready, 1)

            def tile_y(j, n, again):
                dve.wait_ge(y_done, j + 1)
                if again is not None:
                    dve.wait_ge(y_stored[n], again + FIRST)
                nc.vector.tensor_copy(yt[n], bank[6][:, 0:D]).then_inc(y_ready, 1)

            tile_xgT(0, 0)
            tile_hid(0, 0)
            tile_xgT(1, 1)

            def two_tiles(j2, more):
                tile_hid(j2, 1)
                tile_xgT(j2 + 1, 0)
                tile_y(j2 - 1, 0, (j2 - 1) * 8)
                tile_hid(j2 + 1, 0)
                if more:
                    tile_xgT(j2 + 2, 1)
                tile_y(j2, 1, (j2 - 1) * 8)

            with dve.Fori(1, SLOT_TILES - 2, 2) as j2:
                two_tiles(j2, True)
            two_tiles(SLOT_TILES - 2, False)
            tile_y(SLOT_TILES - 1, 0, 16 * (SLOT_TILES // 2))

            for t in range(TILES):
                dve.wait_ge(gathered[t], 16 * TOPK)
                then(nc.vector.scalar_tensor_tensor(out=x3n[:, t, :], in0=y_of[:, 0, t, :], scalar=prob[0][:, t:t + 1],
                                                    in1=xr[:, t, :], op0=ALU.mult, op1=ALU.add))
                nc.vector.scalar_tensor_tensor(out=x3n[:, t, :], in0=y_of[:, 1, t, :], scalar=prob[1][:, t:t + 1],
                                               in1=x3n[:, t, :], op0=ALU.mult, op1=ALU.add).then_inc(out_ready, 1)

        @block.tensor
        def _(pe):
            def turn(dst, src):
                return nc.tensor.transpose(dst, src, ident[0:src.shape[0], 0:src.shape[0]])

            def turn_tiles(src, s):
                c, half = s // 2, s % 2
                for k in range(TPG):
                    last = turn(bank[s][:, k * P:(k + 1) * P], src[:, half * TPG + k, c * P:(c + 1) * P])
                return last

            pe.wait_ge(consts, N_CONST)
            for s in range(4):
                if s < 2:
                    pe.wait_ge(xn_ready, TPG * (s + 1))
                turn_tiles(xn, s).then_inc(setup_done, 1)
            pe.wait_ge(small_loaded, 16 * N_SMALL)

            def turn_weight(nat, width, f0, s):
                w = nat.rearrange("p (c n) -> p c n", c=DC)
                for f in range(2):
                    for o in range(DC):
                        last = turn(bank[s % 8][:, (f * DC + o) * P:(f * DC + o + 1) * P], w[:, o, (f0 + f) * P:(f0 + f + 1) * P])
                return last

            turn_weight(w1_nat, D, 0, 4).then_inc(setup_done, 1)
            for s in range(2):
                turn_weight(w2_nat, 2 * D, 2 * s, 5 + s).then_inc(setup_done, 1)
            pe.wait_ge(setup_act, 5)
            for s in range(4):
                kc, half = s // 2, s % 2
                for c in range(DC):
                    last = nc.tensor.matmul(bank[(7 + s) % 8], w1T[:, c, kc * P:(kc + 1) * P], xnT[:, c, half * BANK:(half + 1) * BANK],
                                            start=c == 0, stop=c == DC - 1)
                last.then_inc(setup_done, 1)
            pe.wait_ge(setup_act, 7)
            for s in range(4):
                for t in range(2):
                    for c in range(DC):
                        last = nc.tensor.matmul(bank[(11 + s) % 8][:, t * D:(t + 1) * D], xnT[:, c, (2 * s + t) * P:(2 * s + t + 1) * P],
                                                w2T[:, c, :], start=c == 0, stop=c == DC - 1)
                last.then_inc(setup_done, 1)
            for s, nat in enumerate((q_nat, k_nat, v_nat, o_nat)):
                pe.wait_ge(setup_act, 8 + s)
                turn_weight(nat, D, 0, 15 + s).then_inc(setup_done, 1)
            pe.wait_ge(setup_act, 15)
            pe.wait_ge(setup_dve, 4)

            GR = TPB * CHUNKS
            WGR = EPB * NMAT * MATGROUPS
            with pe.Fori(0, BATCH // 2) as i:
                for n in range(2):
                    b = i * 2 + n

                    def turn_ctx(ch):
                        if ch % 2 == 0:
                            pe.wait_ge(ctx_loaded[n][ch // 2], i * 16 + 16)
                        for c in range(DC):
                            if ch == 0:
                                pe.wait_ge(probsT_ready, b * GR + FIRST)
                            else:
                                pe.wait_ge(ctxT_ready, b * (CHUNKS * DC) + (ch - 1) * DC + c + 1)
                            for k in range(TPG):
                                last = turn(bank[c][:, k * P:(k + 1) * P], ctx_sb[n][:, ch * TPG + k, c * P:(c + 1) * P])
                            last.then_inc(ctx_turned, 1)

                    def score(ch):
                        pe.wait_ge(ctxT_ready, b * (CHUNKS * DC) + (ch + 1) * DC)
                        for t in range(TPB):
                            pe.wait_ge(scores_out, b * GR + max(ch - 1, 0) * TPB + (t + 1 if ch else 0) + FIRST)
                            for c in range(DC):
                                last = nc.tensor.matmul(bank[2 + t], bf_st[n][:, c, t * P:(t + 1) * P], ctxT[:, ch % 2, c, :],
                                                        start=c == 0, stop=c == DC - 1)
                            last.then_inc(scores_done, 1)

                    def turn_expert(g):
                        k, gq = g // MATGROUPS, g % MATGROUPS
                        if gq == 0:
                            pe.wait_ge(w_loaded[k % 2], b * (16 * EPB * NMAT // 2) + 16 * (k // 2 + 1))
                        pe.wait_ge(w_out, b * WGR + max(g - 1, 0) + FIRST)
                        for q in range(TPG):
                            if k % NMAT < 2:
                                src = w_nat[k % 2].rearrange("p (c n) -> p c n", c=IC)[:, TPG * (gq % 2) + q, (gq // 2) * P:(gq // 2 + 1) * P]
                            else:
                                ic = 2 * gq + q // 2
                                src = w_nat[k % 2].rearrange("p (c n) -> p c n", c=DC)[:, q % 2, ic * P:(ic + 1) * P]
                            last = turn(bank[4 + g % 2][:, q * P:(q + 1) * P], src)
                        last.then_inc(w_turned, 1)

                    pe.wait_ge(bf_ready, b + 1)
                    turn_ctx(0)
                    for ch in range(CHUNKS):
                        if ch + 1 < CHUNKS:
                            turn_ctx(ch + 1)
                        score(ch)
                        for g in range(3 * ch, 3 * ch + 3):
                            turn_expert(g)

                    def turn_probs(g):
                        t, k0 = g // CHUNKS, g % CHUNKS * TPG
                        if k0 % (KT // PIECES) == 0:
                            pe.wait_ge(exp_done, b * (TPB * PIECES) + t * PIECES + k0 // (KT // PIECES) + 1)
                        if g < 2:
                            pe.wait_ge(ctxT_ready, b * (CHUNKS * DC) + CHUNKS * DC)
                        else:
                            pe.wait_ge(probsT_ready, b * GR + g - 1 + FIRST)
                        for k in range(TPG):
                            last = turn(bank[g % 2][:, k * P:(k + 1) * P], scores[t][:, (k0 + k) * P:(k0 + k + 1) * P])
                        last.then_inc(probs_turned, 1)

                    def weigh(g):
                        t, k0 = g // CHUNKS, g % CHUNKS * TPG
                        pe.wait_ge(probsT_ready, b * GR + g + 1 + FIRST)
                        if g == 0:
                            pe.wait_ge(x1_ready, b + FIRST)
                        elif k0 == 0:
                            pe.wait_ge(o_ready, b * TPB + t + FIRST)
                        for k in range(TPG):
                            last = nc.tensor.matmul(bank[6][:, 0:D], pT[:, g % 4, k, :], ctx_sb[n][:, k0 + k, :],
                                                    start=k0 + k == 0, stop=k0 + k == KT - 1)
                        last.then_inc(pv_done, 1)

                    turn_probs(0)
                    for g in range(TPB * CHUNKS):
                        if g + 1 < TPB * CHUNKS:
                            turn_probs(g + 1)
                        weigh(g)
                    for t in range(TPB):
                        pe.wait_ge(o_ready, b * TPB + t + 1 + FIRST)
                        pe.wait_ge(oT_ready, b * TPB + t + FIRST)
                        for c in range(DC):
                            last = turn(bank[7][:, t * D + c * P:t * D + (c + 1) * P], o_sb[:, t, c * P:(c + 1) * P])
                        last.then_inc(o_turned, 1)
                    for t in range(TPB):
                        pe.wait_ge(oT_ready, b * TPB + t + 1 + FIRST)
                        for c in range(DC):
                            last = nc.tensor.matmul(bank[6][:, t * D:(t + 1) * D], oT[:, t, c, :], w2T[:, DC + c, :],
                                                    start=c == 0, stop=c == DC - 1)
                    last.then_inc(fused_done, 1)

            pe.wait_ge(x1_ready, BATCH + FIRST)
            pe.wait_ge(w_out, BATCH * WGR + FIRST)
            for s in range(4):
                if s < 2:
                    pe.wait_ge(xn_ready, TILES + TPG * (s + 1))
                turn_tiles(x2n, s).then_inc(p2_done, 1)
            pe.wait_ge(p2_act, 4)
            pe.wait_ge(staged, 2)
            for s in range(4, 4 + 4 * HC):
                w = qwT if s < 4 + 2 * HC else kwT
                c4, half = (s - 4) // 2 % HC, s % 2
                if s >= 8:
                    pe.wait_ge(p2_act, s - 7)
                for c in range(DC):
                    last = nc.tensor.matmul(bank[s % 8].rearrange("p (b n) -> p b n", b=2), w[:, c, c4 * P:(c4 + 1) * P],
                                            x2nT[:, c, 2 * half:2 * half + 2, WIN:PADTOK], start=c == 0, stop=c == DC - 1)
                last.then_inc(p2_done, 1)
            for b in range(BATCH):
                for part, rows in enumerate((P, WIN)):
                    s = 4 + 4 * HC + 2 * b + part
                    if s < 8 + 4 + 4 * HC:
                        pe.wait_ge(p2_act, s - 7)
                    else:
                        pe.wait_ge(p2_dve, s - 7 - 4 - 4 * HC)
                    for t in range(TPB):
                        at = t * P + part * P
                        for c in range(DC):
                            last = nc.tensor.matmul(bank[s % 8][0:rows, t * D:(t + 1) * D], x2nT[:, c, b, at:at + rows], vwT[:, c, :],
                                                    start=c == 0, stop=c == DC - 1)
                    last.then_inc(p2_done, 1)
            pe.wait_ge(p2_act, 4 + 4 * HC)
            pe.wait_ge(p2_dve, 2 * BATCH)

            with pe.Fori(0, BATCH) as b:
                def local_score(n):
                    t, h = n // 2, n % 2
                    pe.wait_ge(staged, b * (2 * TPB) + 2 + 2 * (t + 1))
                    pe.wait_ge(local_out, b * 4 + n + FIRST)
                    for c in range(2):
                        for j in range(4):
                            rows = slice(32 * j, 32 * j + DH)
                            last = nc.tensor.matmul(bank[j][:, c * D:c * D + SPAN], q_st[t][rows, 2 * h + c, :], k_st[t][rows, 2 * h + c, :],
                                                    start=True, stop=True)
                    last.then_inc(local_done, 1)

                def local_weigh(n):
                    t, h = n // 2, n % 2
                    pe.wait_ge(local_exp, b * 4 + n + 1)
                    for g in range(2):
                        pe.wait_ge(first_ready, b * 8 + n * 2 + FIRST)
                        pe.wait_ge(last_ready, b * 8 + n * 2 + g + FIRST)
                        for j in range(4):
                            last = turn(bank[4 + g][:, j * P:(j + 1) * P], local[n % 2][:, j, g, 0:P])
                        last.then_inc(first_turned, 1)
                        for j in range(4):
                            last = turn(bank[6][0:WIN, j * P:(j + 1) * P], local[n % 2][:, j, g, P:SPAN])
                        last.then_inc(last_turned, 1)
                    if h == 0:
                        pe.wait_ge(heads_ready, b * TPB + t + FIRST)
                    for g in range(2):
                        pe.wait_ge(first_ready, b * 8 + n * 2 + g + 1 + FIRST)
                        pe.wait_ge(last_ready, b * 8 + n * 2 + g + 1 + FIRST)
                        for j in range(4):
                            cols = slice(((2 * h + g) * 4 + j) * DH, ((2 * h + g) * 4 + j + 1) * DH)
                            tile = bass.ds(b * TPB + t, 1)
                            nc.tensor.matmul(bank[7][:, cols], pT[:, g, j, :], v_first[:, tile, cols].rearrange("p a n -> p (a n)"),
                                             start=True, stop=False)
                            last = nc.tensor.matmul(bank[7][:, cols], pT[0:WIN, 2 + g, j, :], v_last[0:WIN, tile, cols].rearrange("p a n -> p (a n)"),
                                                    start=False, stop=True)
                    last.then_inc(localpv_done, 1)

                local_score(0)
                local_score(1)
                local_weigh(0)
                local_score(2)
                local_weigh(1)
                local_score(3)
                local_weigh(2)
                local_weigh(3)

            pe.wait_ge(heads_ready, TILES + FIRST)
            for s in range(4):
                turn_tiles(heads, s).then_inc(p2c_done, 1)
            pe.wait_ge(p2c_act, 4)
            for s in range(4):
                for t in range(2):
                    for c in range(DC):
                        last = nc.tensor.matmul(bank[4 + s][:, t * D:(t + 1) * D], headsT[:, c, (2 * s + t) * P:(2 * s + t + 1) * P],
                                                owT[:, c, :], start=c == 0, stop=c == DC - 1)
                last.then_inc(p2c_done, 1)

            for s in range(4):
                if s < 2:
                    pe.wait_ge(xn_ready, 2 * TILES + TPG * (s + 1))
                turn_tiles(x3n, s).then_inc(p3_done, 1)
            pe.wait_ge(p3_act, 4)
            for t in range(TILES):
                for c in range(DC):
                    last = nc.tensor.matmul(bank[4][:, t * E:(t + 1) * E], x3nT[:, c, t * P:(t + 1) * P], gwT[:, c, :],
                                            start=c == 0, stop=c == DC - 1)
            last.then_inc(p3_done, 1)
            pe.wait_ge(chosen_ready, 1)
            rows = chosen.rearrange("p t e -> p (t e)")
            nc.tensor.matmul(bank[5][:, 0:TILES * E], earlier[:, :], rows, start=True, stop=True)
            nc.tensor.matmul(bank[5][:, TILES * E:2 * TILES * E], ones[:, :], rows, start=True, stop=True).then_inc(ranks_done, 1)

            pe.wait_ge(slots_ready, 1)

            def tile_turn(j, n, arrived):
                pe.wait_ge(xg_loaded[n], arrived)
                if j is not 0:
                    pe.wait_ge(xgT_ready, j)
                for c in range(DC):
                    last = turn(bank[7][:, c * P:(c + 1) * P], xg[n][:, c * P:(c + 1) * P])
                last.then_inc(xg_turned, 1)

            def tile_up(j, n, arrived):
                pe.wait_ge(up_loaded[n], arrived)
                pe.wait_ge(xgT_ready, j + 1)
                for m, done in enumerate((g_done, u_done)):
                    for half in range(2):
                        if j is not 0:
                            if m == 0:
                                pe.wait_ge(silu_ready, j * 2)
                            else:
                                pe.wait_ge(hid_ready, j)
                        for c in range(DC):
                            at = m * MAT + c * INNER + half * BANK
                            last = nc.tensor.matmul(bank[2 * m + half], xgT[n][:, c * P:(c + 1) * P], w_up[n][:, at:at + BANK],
                                                    start=c == 0, stop=c == DC - 1)
                        last.then_inc(done, 1)

            def tile_down(j, n, arrived):
                pe.wait_ge(down_loaded[n], arrived)
                pe.wait_ge(hid_ready, j + 1)
                if j is not 0:
                    pe.wait_ge(hidT_ready, j * 2)
                for half in range(2):
                    for k in range(TPG):
                        at = (half * TPG + k) * P
                        last = turn(bank[4 + half][:, k * P:(k + 1) * P], hid[n][:, at:at + P])
                    last.then_inc(hid_turned, 1)
                if j is not 0:
                    pe.wait_ge(y_ready, j)
                for ic in range(IC):
                    if ic % TPG == 0:
                        pe.wait_ge(hidT_ready, j * 2 + ic // TPG + 1)
                    at = ic * D
                    last = nc.tensor.matmul(bank[6][:, 0:D], hidT[n][:, ic * P:(ic + 1) * P], w_down[n][:, at:at + D],
                                            start=ic == 0, stop=ic == IC - 1)
                last.then_inc(y_done, 1)

            tile_turn(0, 0, 16)
            tile_up(0, 0, 16)
            tile_turn(1, 1, 16)

            def two_tiles(j2, more):
                tile_up(j2, 1, (j2 + 1) * 8)
                tile_turn(j2 + 1, 0, (j2 + 3) * 8)
                tile_down(j2 - 1, 0, (j2 + 1) * 8)
                tile_up(j2 + 1, 0, (j2 + 3) * 8)
                if more:
                    tile_turn(j2 + 2, 1, (j2 + 3) * 8)
                tile_down(j2, 1, (j2 + 1) * 8)

            with pe.Fori(1, SLOT_TILES - 2, 2) as j2:
                two_tiles(j2, True)
            two_tiles(SLOT_TILES - 2, False)
            tile_down(SLOT_TILES - 1, 0, (SLOT_TILES + 1) * 8)


_INS = ["x", "ctx_1024", "L0_xattn_w1_w", "L0_xattn_w1_b", "L0_xattn_w2_w", "L0_xattn_w2_b", "L0_attn_q_w", "L0_attn_q_b",
        "L0_attn_k_w", "L0_attn_k_b", "L0_attn_v_w", "L0_attn_v_b", "L0_attn_o_w", "L0_attn_o_b", "L0_ffn_gate_w",
        "L0_ffn_wg", "L0_ffn_wu", "L0_ffn_wd"]


def kernel(**inputs):
    import numpy as np
    import concourse.bacc as bacc
    from concourse.bass_utils import run_bass_kernel_spmd

    nc = bacc.Bacc("TRN2", target_bir_lowering=False, num_devices=1)
    arrays, args = {}, []
    for name in _INS:
        a = np.ascontiguousarray(inputs[name])
        arrays[name + "_dram"] = a
        args.append(nc.dram_tensor(name + "_dram", a.shape, mybir.dt.from_np(a.dtype), kind="ExternalInput").ap())
    out = nc.dram_tensor("out_dram", (BATCH, NTOK, D), F32, kind="ExternalOutput").ap()
    perceiver(nc, *args, out)
    r = run_bass_kernel_spmd(nc, [arrays], core_ids=[0])
    return r.results[0]["out_dram"]
```

```python
import concourse.bass as bass
from concourse import mybir
from contextlib import ExitStack

F32 = mybir.dt.float32
I32 = mybir.dt.int32
ALU = mybir.AluOpType
ACT = mybir.ActivationFunctionType
X_AXIS = mybir.AxisListType.X

P = 128
BATCH, NTOK, D = 4, 256, 256
KEYS = 4096
TOK = BATCH * NTOK
TILES = TOK // P
TPB = NTOK // P
DC = D // P
KT = KEYS // P
BANK = 512
TPG = BANK // P
CHUNKS = KEYS // BANK
PIECES = 4
HEADS, DH, WIN = 16, 16, 64
HPC = P // DH
SEEN = [P, P + WIN]
KEY0 = [0, P - WIN]
UNITS = [(t, hc) for t in range(2) for hc in range(DC)]
GROUPS = [HPC * (t + 1) // 4 for t, _ in UNITS]
GROUP0 = [sum(GROUPS[:u]) for u in range(len(UNITS))]
E, INNER, TOPK = 8, 1024, 2
IC = INNER // P
MAT = D * INNER // P
NMAT = 3
MATGROUPS = MAT // BANK
SLOT_TILES = (TOK * TOPK + E * (P - 1)) // P
SLOTS = SLOT_TILES * P
EPS = 1e-5
LOWEST = -3.0e38
MASKED = -1.0e30
FIRST = 1
BESIDE = 2
EPB = E // BATCH


def perceiver(nc, x, ctx, w1_w, w1_b, w2_w, w2_b, q_w, q_b, k_w, k_b, v_w, v_b, o_w, o_b,
              gate_w, wg, wu, wd, out):
    stack = ExitStack()
    with stack:
        def sb(name, cols, dt=F32):
            return stack.enter_context(nc.sbuf_tensor(name, [P, cols], dt))

        def sem(name):
            return stack.enter_context(nc.semaphore(name))

        wt_dram = nc.dram_tensor("turned_weights", [E, P, NMAT * MAT], F32).ap()
        xg_dram = nc.dram_tensor("rows_by_expert", [SLOTS, D], F32).ap()
        yg_dram = nc.dram_tensor("results_by_expert", [SLOTS, D], F32).ap()

        region_a = sb("region_a", 2 * KT * D)
        region_s = sb("region_s", TPB * KEYS)
        region_w = sb("region_w", 4 * MAT)

        def cut(region, widths):
            at, parts = 0, []
            for w in widths:
                parts.append(region[:, at:at + w])
                at += w
            assert at <= region.shape[1], (at, region.shape)
            return parts

        ctx_sb = [region_a[:, n * KT * D:(n + 1) * KT * D].rearrange("p (t d) -> p t d", t=KT) for n in range(2)]
        scores = [region_s[:, n * KEYS:(n + 1) * KEYS] for n in range(TPB)]
        w_nat0, w_nat1, w_turn0, w_turn1 = cut(region_w, [MAT] * 4)
        w_nat, w_turn = [w_nat0, w_nat1], [w_turn0, w_turn1]
        xn_f, xnT_f, w1_nat, w2_nat, q_nat, k_nat, v_nat, o_nat = cut(
            region_s, [TILES * D, DC * TOK, DC * D, DC * 2 * D, DC * D, DC * D, DC * D, DC * D])
        xn = xn_f.rearrange("p (t d) -> p t d", t=TILES)
        xnT = xnT_f.rearrange("p (c n) -> p c n", c=DC)
        qT_f, kT_f, v_f, x2nT_f, sl0, sl1, sl2, sl3 = cut(region_a, [DC * TOK] * 4 + [HPC * P] * 2 + [HPC * NTOK] * 2)
        qT, kT, x2nT = [r.rearrange("p (c n) -> p c n", c=DC) for r in (qT_f, kT_f, x2nT_f)]
        v_tok = v_f.rearrange("p (t d) -> p t d", t=TILES)
        local = [s.rearrange("p (h k) -> p h k", h=HPC) for s in (sl0, sl1, sl2, sl3)]
        x2n_f, headsT_f = cut(region_s, [TILES * D, DC * TOK])
        x2n = x2n_f.rearrange("p (t d) -> p t d", t=TILES)
        q_own0, q_own1, v_own_f = cut(region_w, [HPC * P, HPC * P, TPB * DC * HPC * (P + DH)])
        headsT = headsT_f.rearrange("p (c n) -> p c n", c=DC)
        q_own = [s.rearrange("p (h n) -> p h n", h=HPC) for s in (q_own0, q_own1)]
        v_own = v_own_f.rearrange("p (t c n) -> p t c n", t=TPB, c=DC)
        w_up = [region_a[:, n * 2 * MAT:(n + 1) * 2 * MAT] for n in range(2)]
        w_down = [region_a[:, (4 + n) * MAT:(5 + n) * MAT] for n in range(2)]
        x3n_f, x3nT_f, silu0, silu1, hid0, hid1 = cut(region_s, [TILES * D, DC * TOK] + [INNER] * 4)
        x3n = x3n_f.rearrange("p (t d) -> p t d", t=TILES)
        x3nT = x3nT_f.rearrange("p (c n) -> p c n", c=DC)
        silu, hid = [silu0, silu1], [hid0, hid1]
        xg0, xg1, xgT0, xgT1, hidT0, hidT1, yt0, yt1 = cut(
            region_w, [D] * 2 + [DC * P] * 2 + [INNER] * 2 + [D] * 2)
        xg, xgT, hidT, yt = [xg0, xg1], [xgT0, xgT1], [hidT0, hidT1], [yt0, yt1]
        y_f = region_a[:, 0:2 * TILES * D]
        y_of = y_f.rearrange("p (k t d) -> p k t d", k=TOPK, t=TILES)

        xr_t = sb("residual", TILES * D)
        xr = xr_t[:, :].rearrange("p (t d) -> p t d", t=TILES)
        bfT_t = sb("bfT", DC * TOK)
        bfT = bfT_t[:, :].rearrange("p (c n) -> p c n", c=DC)
        bf_st = [sb(f"bf_batch{n}", DC * NTOK)[:, :].rearrange("p (c n) -> p c n", c=DC) for n in range(2)]
        ctxT_t = sb("ctxT", 2 * DC * BANK)
        ctxT = ctxT_t[:, :].rearrange("p (r c n) -> p r c n", r=2, c=DC)
        pT_t = sb("probsT", 4 * BANK)
        pT = pT_t[:, :].rearrange("p (r k n) -> p r k n", r=4, k=TPG)
        w1T = sb("w1T", DC * D)[:, :].rearrange("p (c n) -> p c n", c=DC)
        w2T = sb("w2T", 2 * DC * D)[:, :].rearrange("p (c n) -> p c n", c=2 * DC)
        qwT = sb("qwT", DC * D)[:, :].rearrange("p (c n) -> p c n", c=DC)
        kwT = sb("kwT", DC * D)[:, :].rearrange("p (c n) -> p c n", c=DC)
        vwT = sb("vwT", DC * D)[:, :].rearrange("p (c n) -> p c n", c=DC)
        owT = sb("owT", DC * D)[:, :].rearrange("p (c n) -> p c n", c=DC)
        gwT = sb("gwT", DC * E)[:, :].rearrange("p (c e) -> p c e", c=DC)
        ident = sb("ident", P)
        zeros = sb("zeros", D)
        mask = [sb(f"mask{t}", SEEN[t]) for t in range(TPB)]
        head_rows = sb("head_rows", HPC)
        earlier = sb("earlier", P)
        ones = sb("ones", P)
        b1c = sb("b1_cols", DC)
        qbc = sb("qb_cols", DC)
        kbc = sb("kb_cols", DC)
        b2r = sb("b2_rows", D)
        vbr = sb("vb_rows", D)
        obr = sb("ob_rows", D)
        eps_c = sb("eps", 1)
        bn = sb("ln_stats", TILES * 6)[:, :].rearrange("p (t s) -> p t s", t=TILES)
        mv = sb("ln_mean_var", TILES * 2)[:, :].rearrange("p (t s) -> p t s", t=TILES)
        sd = sb("ln_sd", TILES)
        rstd = sb("ln_rstd", TILES)
        cmax = sb("chunk_max", TPB * CHUNKS)[:, :].rearrange("p (t c) -> p t c", t=TPB)
        nmax = sb("neg_max", TPB)
        lpart = sb("piece_sums", TPB * PIECES)[:, :].rearrange("p (t c) -> p t c", t=TPB)
        lsum = sb("sums", TPB)
        linv = sb("inv_sums", TPB)
        o_sb = sb("cross_out", TPB * D)[:, :].rearrange("p (t d) -> p t d", t=TPB)
        oT = sb("cross_outT", TPB * D)[:, :].rearrange("p (t c n) -> p t c n", t=TPB, c=DC)
        hmax, hbias, hsum, hinv = [sb(name, len(UNITS) * HPC)[:, :].rearrange("p (u h) -> p u h", u=len(UNITS))
                                   for name in ("head_max", "head_bias", "head_sum", "head_inv")]
        pause = sb("pause", 1)
        lo = sb("logits", TILES * E)[:, :].rearrange("p (t e) -> p t e", t=TILES)
        above = sb("above", TILES * E * E)[:, :].rearrange("p (t e f) -> p t e f", t=TILES, e=E)
        ties = sb("ties", TILES * E * E)[:, :].rearrange("p (t e f) -> p t e f", t=TILES, e=E)
        lower_i = sb("lower_i", E * E)[:, :].rearrange("p (e f) -> p e f", e=E)
        place = sb("place", TILES * E)[:, :].rearrange("p (t e) -> p t e", t=TILES)
        chosen = sb("chosen", TILES * E)[:, :].rearrange("p (t e) -> p t e", t=TILES)
        nth = [sb(f"choice{n}", TILES * E)[:, :].rearrange("p (t e) -> p t e", t=TILES) for n in range(TOPK)]
        lmax = sb("logit_max", TILES)
        ex = sb("gate_exp", TILES * E)[:, :].rearrange("p (t e) -> p t e", t=TILES)
        gsum = sb("gate_sum", TILES)
        ginv = sb("gate_inv", TILES)
        prob = [sb(f"prob{n}", TILES) for n in range(TOPK)]
        slotf = [sb(f"slotf{n}", TILES) for n in range(TOPK)]
        slot = [sb(f"slot{n}", TILES, I32) for n in range(TOPK)]
        tots = sb("tile_counts", TILES * E)[:, :].rearrange("p (t e) -> p t e", t=TILES)
        before = sb("counts_before", TILES * E)[:, :].rearrange("p (t e) -> p t e", t=TILES)
        pos = sb("positions", TILES * E)[:, :].rearrange("p (t e) -> p t e", t=TILES)
        cnt = sb("counts", E)
        steps = sb("steps", E)
        need = sb("tiles_needed", E)
        first = sb("first_tile", E)
        tileno = sb("tile_numbers", SLOT_TILES)
        owner_f = sb("owner_f", SLOT_TILES)
        owner = sb("owner", SLOT_TILES, I32)
        cmp23 = sb("owner_cmp", SLOT_TILES * (E - 1))[:, :].rearrange("p (j e) -> p j e", j=SLOT_TILES)

        psum = stack.enter_context(nc.psum_tensor("psum", [P, 8 * BANK], F32))
        bank = [psum[:, n * BANK:(n + 1) * BANK] for n in range(8)]

        consts = sem("consts")
        pool_step = sem("pool_step")
        x_loaded, small_loaded, biases_loaded = sem("x_loaded"), sem("small_loaded"), sem("biases_loaded")
        zero_stored = sem("zero_stored")
        ctx_loaded = [[sem(f"ctx_loaded{n}_{q}") for q in range(4)] for n in range(2)]
        w_loaded = [sem(f"w_loaded{n}") for n in range(2)]
        w_stored = [sem(f"w_stored{n}") for n in range(2)]
        dve_step = sem("dve_step")
        var_ready, sd_ready, xn_ready = sem("var_ready"), sem("sd_ready"), sem("xn_ready")
        setup_done, setup_act, setup_dve = sem("setup_done"), sem("setup_act"), sem("setup_dve")
        b1_scaled = sem("b1_scaled")
        bf_ready = sem("bf_ready")
        ctx_turned, ctxT_ready = sem("ctx_turned"), sem("ctxT_ready")
        scores_done, scores_out = sem("scores_done"), sem("scores_out")
        max_ready, exp_done = sem("max_ready"), sem("exp_done")
        probs_turned, probsT_ready, pv_done = sem("probs_turned"), sem("probsT_ready"), sem("pv_done")
        w_turned, w_out = sem("w_turned"), sem("w_out")
        o_ready, o_turned, oT_ready = sem("o_ready"), sem("o_turned"), sem("oT_ready")
        fused_done, x1_ready = sem("fused_done"), sem("x1_ready")
        p2_done, p2_act, p2_dve = sem("p2_done"), sem("p2_act"), sem("p2_dve")
        zeroed = sem("zeroed")
        q_ready, v_ready = sem("q_ready"), sem("v_ready")
        local_done, row_max, bias_ready, local_exp = sem("local_done"), sem("row_max"), sem("bias_ready"), sem("local_exp")
        inv_ready, normed = sem("inv_ready"), sem("normed")
        local_turned, localT_ready, localpv_done = sem("local_turned"), sem("localT_ready"), sem("localpv_done")
        heads_ready = sem("heads_ready")
        p2c_done = sem("p2c_done")
        p3_done, p3_act, logits_out = sem("p3_done"), sem("p3_act"), sem("logits_out")
        lm_ready, gate_exp = sem("lm_ready"), sem("gate_exp_done")
        chosen_ready, ranks_done = sem("chosen_ready"), sem("ranks_done")
        slots_ready = sem("slots_ready")
        scattered = sem("scattered")
        up_loaded = [sem(f"up_loaded{n}") for n in range(2)]
        down_loaded = [sem(f"down_loaded{n}") for n in range(2)]
        xg_loaded = [sem(f"xg_loaded{n}") for n in range(2)]
        xg_turned, xgT_ready = sem("xg_turned"), sem("xgT_ready")
        g_done, u_done = sem("g_done"), sem("u_done")
        silu_ready, hid_ready = sem("silu_ready"), sem("hid_ready")
        hid_turned, hidT_ready = sem("hid_turned"), sem("hidT_ready")
        y_done, y_ready = sem("y_done"), sem("y_ready")
        y_stored = [sem(f"y_stored{n}") for n in range(2)]
        gathered = [sem(f"gathered{n}") for n in range(TILES)]
        out_ready, out_stored = sem("out_ready"), sem("out_stored")

        rooms = [w_turned, pv_done, scores_done, local_done, o_ready, localpv_done, probs_turned, *w_stored, local_turned,
                 probsT_ready, scores_out, w_out, x1_ready, oT_ready, row_max, localT_ready, heads_ready, *y_stored]

        small = [(w1_nat.rearrange("p (c n) -> p c n", c=DC), w1_w.rearrange("(c p) n -> p c n", p=P)),
                 (w2_nat.rearrange("p (c n) -> p c n", c=DC), w2_w.rearrange("(c p) n -> p c n", p=P)),
                 (q_nat.rearrange("p (c n) -> p c n", c=DC), q_w.rearrange("(c p) n -> p c n", p=P)),
                 (k_nat.rearrange("p (c n) -> p c n", c=DC), k_w.rearrange("(c p) n -> p c n", p=P)),
                 (v_nat.rearrange("p (c n) -> p c n", c=DC), v_w.rearrange("(c p) n -> p c n", p=P)),
                 (o_nat.rearrange("p (c n) -> p c n", c=DC), o_w.rearrange("(c p) n -> p c n", p=P))]
        biases = [(b1c[:, :], w1_b.rearrange("(c p) -> p c", p=P)),
                 (b2r[:, :], w2_b.rearrange("(a n) -> a n", a=1).broadcast_to([P, D])),
                 (vbr[:, :], v_b.rearrange("(a n) -> a n", a=1).broadcast_to([P, D])),
                 (obr[:, :], o_b.rearrange("(a n) -> a n", a=1).broadcast_to([P, D])),
                 ]
        for c in range(DC):
            biases.append((gwT[:, c, :], gate_w[:, c * P:(c + 1) * P].rearrange("e p -> p e")))
        biases += [(cols[:, :], b.rearrange("(c p) -> p c", p=P)) for cols, b in ((qbc, q_b), (kbc, k_b))]
        N_CONST = 11

        block = stack.enter_context(nc.Block())

        @block.sync
        def _(sp):
            sp.dma_start(xr, x.rearrange("b (t p) d -> p (b t) d", p=P)).then_inc(x_loaded, 16)
            for dst, src in small:
                sp.dma_start(dst, src).then_inc(small_loaded, 16)

            def load_ctx(b, i, n):
                src = ctx[bass.ds(b, 1)].rearrange("a (p t) d -> p (a t) d", p=P)
                for q in range(4):
                    t = slice(q * KT // 4, (q + 1) * KT // 4)
                    sp.dma_start(ctx_sb[n][:, t, :], src[:, t, :]).then_inc(ctx_loaded[n][q], 16)

            def load_piece(b, k):
                e = b * EPB + k // NMAT
                m = k % NMAT
                if k >= 2:
                    sp.wait_ge(w_turned, b * (EPB * NMAT * MATGROUPS) + (k - 1) * MATGROUPS + FIRST)
                else:
                    sp.wait_ge(w_turned, b * (EPB * NMAT * MATGROUPS) + FIRST)
                if m < 2:
                    src = (wg, wu)[m][bass.ds(e, 1)].rearrange("a (c p) n -> p (a c) n", p=P)
                    dst = w_nat[k % 2].rearrange("p (c n) -> p c n", c=IC)
                else:
                    src = wd[bass.ds(e, 1)].rearrange("a (c p) n -> p (a c) n", p=P)
                    dst = w_nat[k % 2].rearrange("p (c n) -> p c n", c=DC)
                sp.dma_start(dst, src).then_inc(w_loaded[k % 2], 16)

            def store_piece(b, k):
                e = b * EPB + k // NMAT
                m = k % NMAT
                sp.wait_ge(w_out, b * (EPB * NMAT * MATGROUPS) + (k + 1) * MATGROUPS + FIRST)
                sp.dma_start(wt_dram[bass.ds(e, 1), :, m * MAT:(m + 1) * MAT].rearrange("a p n -> p (a n)"),
                             w_turn[k % 2]).then_inc(w_stored[k % 2], 16)

            load_ctx(0, 0, 0)

            def two_batches(i, more):
                for n in range(2):
                    b = i * 2 + n
                    load_piece(b, 0)
                    load_piece(b, 1)
                    if n == 0 or more:
                        sp.wait_ge(pv_done, b * (TPB * CHUNKS) + FIRST)
                        load_ctx(b + 1, i, 1 - n)
                    for k in range(EPB * NMAT):
                        store_piece(b, k)
                        if k + 2 < EPB * NMAT:
                            load_piece(b, k + 2)

            with sp.Fori(0, BATCH // 2 - 1) as i:
                two_batches(i, True)
            two_batches(BATCH // 2 - 1, False)

            sp.wait_ge(slots_ready, 1)
            for n in range(2):
                sp.wait_ge(w_stored[n], 16 * E * NMAT // 2 + FIRST)
            sp.wait_ge(scattered, 16 * TOPK * TILES)

            def load_tile(j, n, waits):
                if waits:
                    sp.wait_ge(xg_turned, j - 1)
                e = sp.value_load(owner[0:1, bass.ds(j, 1)], min_val=0, max_val=E - 1)
                sp.dma_start(xg[n], xg_dram[bass.ds(j * P, P), :]).then_inc(xg_loaded[n], 16)
                rows = wt_dram[bass.ds(e, 1), :, :].rearrange("a p n -> p (a n)")
                if waits:
                    sp.wait_ge(u_done, (j - 1) * 2)
                sp.dma_start(w_up[n], rows[:, 0:2 * MAT]).then_inc(up_loaded[n], 16)
                if waits:
                    sp.wait_ge(y_done, j - 1)
                sp.dma_start(w_down[n], rows[:, 2 * MAT:3 * MAT]).then_inc(down_loaded[n], 16)

            for n in range(2):
                load_tile(n, n, False)
            with sp.Fori(2, SLOT_TILES - 1, 2) as j2:
                for n in range(2):
                    load_tile(j2 + n, n, True)
            load_tile(SLOT_TILES - 1, 0, True)

            for t in range(TILES):
                sp.wait_ge(out_ready, t + 1)
                sp.dma_start(out.rearrange("b (t p) d -> p (b t) d", p=P)[:, t, :], x3n[:, t, :]).then_inc(out_stored, 16)
            sp.wait_ge(out_stored, 16 * TILES)

        @block.gpsimd
        def _(pool):
            for room in rooms:
                pool.sem_inc(room, FIRST)
            nc.gpsimd.memset(zeros[:, :], 0.0).then_inc(consts, 1)
            nc.gpsimd.memset(eps_c[:, :], EPS).then_inc(consts, 1)
            nc.gpsimd.memset(ones[:, :], 1.0).then_inc(consts, 1)
            nc.gpsimd.memset(ident[:, :], 0.0).then_inc(pool_step, 1)
            nc.gpsimd.memset(mask[0][:, :], 0.0).then_inc(pool_step, 1)
            nc.gpsimd.memset(mask[1][:, :], 0.0).then_inc(pool_step, 1)
            nc.gpsimd.memset(head_rows[:, :], 1.0).then_inc(pool_step, 1)
            nc.gpsimd.memset(lower_i, 1.0).then_inc(pool_step, 1)
            pool.wait_ge(pool_step, 5)
            nc.gpsimd.affine_select(out=ident[:, :], in_=ident[:, :], compare_op=ALU.not_equal, fill=1.0, base=0,
                                    pattern=[[-1, P]], channel_multiplier=1).then_inc(consts, 1)
            nc.gpsimd.affine_select(out=earlier[:, :], in_=ones[:, :], compare_op=ALU.is_gt, fill=0.0, base=0,
                                    pattern=[[1, P]], channel_multiplier=-1).then_inc(consts, 1)
            nc.gpsimd.affine_select(out=lower_i, in_=lower_i, compare_op=ALU.is_gt, fill=0.0, base=0,
                                    pattern=[[1, E], [-1, E]], channel_multiplier=0).then_inc(consts, 1)
            nc.gpsimd.iota(steps[:, :], pattern=[[P, E]], base=0, channel_multiplier=0,
                           allow_small_or_imprecise_dtypes=True).then_inc(consts, 1)
            nc.gpsimd.iota(tileno[:, :], pattern=[[1, SLOT_TILES]], base=0, channel_multiplier=0,
                           allow_small_or_imprecise_dtypes=True).then_inc(consts, 1)
            for t in range(TPB):
                nc.gpsimd.affine_select(out=mask[t][:, :], in_=mask[t][:, :], compare_op=ALU.is_ge, fill=MASKED, base=t * P - KEY0[t],
                                        pattern=[[-1, SEEN[t]]], channel_multiplier=1).then_inc(pool_step, 1)
            nc.gpsimd.affine_select(out=head_rows[:, :], in_=head_rows[:, :], compare_op=ALU.is_ge, fill=0.0, base=0,
                                    pattern=[[-DH, HPC]], channel_multiplier=1).then_inc(pool_step, 1)
            pool.wait_ge(pool_step, 8)
            for t in range(TPB):
                nc.gpsimd.affine_select(out=mask[t][:, :], in_=mask[t][:, :], compare_op=ALU.is_ge, fill=MASKED, base=WIN - t * P + KEY0[t],
                                        pattern=[[1, SEEN[t]]], channel_multiplier=-1).then_inc(consts, 1)
            nc.gpsimd.affine_select(out=head_rows[:, :], in_=head_rows[:, :], compare_op=ALU.is_ge, fill=0.0, base=DH - 1,
                                    pattern=[[DH, HPC]], channel_multiplier=-1).then_inc(consts, 1)
            pool.wait_ge(consts, N_CONST)
            pool.dma_start(xg_dram.rearrange("(t p) d -> p t d", p=P),
                           zeros[:, :].rearrange("p (a d) -> p a d", a=1).broadcast_to([P, SLOT_TILES, D])).then_inc(zero_stored, 16)

            pool.wait_ge(setup_act, 15)
            with pool.Fori(0, BATCH // 2) as i:
                pool.wait_ge(scores_done, i * (2 * TPB * CHUNKS) + FIRST)
                for n in range(2):
                    nc.gpsimd.tensor_copy(bf_st[n], bfT[:, :, bass.ds(i * (2 * NTOK) + n * NTOK, NTOK)]).then_inc(bf_ready, 1)

            pool.wait_ge(pv_done, BATCH * TPB * CHUNKS + FIRST)
            pool.wait_ge(w_turned, BATCH * EPB * NMAT * MATGROUPS + FIRST)
            for n in range(2):
                pool.wait_ge(w_stored[n], 16 * E * NMAT // 2 + FIRST)
            nc.gpsimd.memset(v_own_f, 0.0).then_inc(zeroed, 1)
            for hc in range(DC):
                nc.gpsimd.memset(local[DC + hc][:, :, 0:KEY0[1]], 0.0).then_inc(zeroed, 1)
            pool.wait_ge(p2_act, 4 + 2 * DC)

            def local_queries(b, u):
                t, hc = UNITS[u]
                src = qT[:, hc, bass.ds(b * NTOK + t * P, P)].rearrange("p (a n) -> p a n", a=1).broadcast_to([P, HPC, P])
                own = head_rows[:, :].rearrange("p (h a) -> p h a", a=1).broadcast_to([P, HPC, P])
                nc.gpsimd.tensor_tensor(q_own[u % 2], src, own, ALU.mult).then_inc(q_ready, 1)

            def local_norm(b, u):
                t = UNITS[u][0]
                pool.wait_ge(inv_ready, b * len(UNITS) + u + 1)
                part = local[u][:, :, KEY0[t]:KEY0[t] + SEEN[t]]
                nc.gpsimd.tensor_tensor(part, part, hinv[:, u, :].rearrange("p (h a) -> p h a", a=1).broadcast_to([P, HPC, SEEN[t]]),
                                        ALU.mult).then_inc(normed, 1)

            def local_batch(b, more):
                for u in range(len(UNITS)):
                    if u < 3 or more:
                        local_norm(b if u < 3 else b + 1, (u + 1) % 4)
                    if u < 1 or more:
                        pool.wait_ge(local_done, b * len(UNITS) + u + 2 + FIRST)
                        local_queries(b if u < 1 else b + 1, (u + 3) % 4)

            local_queries(0, 0)
            local_queries(0, 1)
            local_norm(0, 0)
            pool.wait_ge(local_done, 1 + FIRST)
            local_queries(0, 2)
            with pool.Fori(0, BATCH - 1) as b:
                local_batch(b, True)
            local_batch(BATCH - 1, False)

            pool.wait_ge(slots_ready, 1)
            pool.wait_ge(zero_stored, 16)
            for t in range(TILES):
                for n in range(TOPK):
                    pool.indirect_dma_start(
                        out=xg_dram, out_offset=bass.IndirectOffsetOnAxis(ap=slot[n][:, t:t + 1], axis=0),
                        in_=x3n[:, t, :], in_offset=None).then_inc(scattered, 16)
            pool.wait_ge(y_stored[0], 16 * ((SLOT_TILES + 1) // 2) + FIRST)
            pool.wait_ge(y_stored[1], 16 * (SLOT_TILES // 2) + FIRST)
            for t in range(TILES):
                for n in range(TOPK):
                    pool.indirect_dma_start(
                        out=y_of[:, n, t, :], out_offset=None,
                        in_=yg_dram, in_offset=bass.IndirectOffsetOnAxis(ap=slot[n][:, t:t + 1], axis=0)).then_inc(gathered[t], 16)

        @block.scalar
        def _(act):
            def sqrt_of_var(k):
                act.wait_ge(var_ready, k)
                nc.scalar.activation(sd[:, :], mv[:, :, 1], ACT.Sqrt, bias=eps_c[:, :]).then_inc(sd_ready, 1)

            def copy(dst, src):
                return nc.scalar.activation(dst, src, ACT.Copy)

            with nc.allow_non_contiguous_dma(reason="a few small columns, once"):
                for dst, src in biases:
                    act.dma_start(dst, src).then_inc(biases_loaded, 16)
            act.wait_ge(consts, N_CONST)
            sqrt_of_var(1)
            for s, dst in enumerate((w1T, w2T[:, 0:DC, :], w2T[:, DC:2 * DC, :], qwT, kwT, vwT, owT)):
                act.wait_ge(setup_done, s + 1)
                copy(dst, bank[s].rearrange("p (c n) -> p c n", c=DC)).then_inc(setup_act, 1)
            for s in range(4):
                act.wait_ge(setup_done, 8 + s)
                copy(xnT[:, s // 2, (s % 2) * BANK:(s % 2 + 1) * BANK], bank[(7 + s) % 8]).then_inc(setup_act, 1)
            act.wait_ge(biases_loaded, 16 * len(biases))
            nc.scalar.activation(b1c[:, :], b1c[:, :], ACT.Copy, scale=float(D) ** -0.5).then_inc(b1_scaled, 1)
            act.wait_ge(b1_scaled, 1)
            for s in range(4):
                act.wait_ge(setup_done, 12 + s)
                kc, half = s // 2, s % 2
                nc.scalar.activation(bfT[:, kc, half * BANK:(half + 1) * BANK], bank[(11 + s) % 8], ACT.Identity,
                                     bias=b1c[:, kc:kc + 1], scale=float(D) ** -0.5).then_inc(setup_act, 1)

            with act.Fori(0, BATCH) as b:
                def expert_out(g):
                    k = g // MATGROUPS
                    if g % MATGROUPS == 0:
                        act.wait_ge(w_stored[k % 2], b * (16 * EPB * NMAT // 2) + 16 * (k // 2) + FIRST)
                    act.wait_ge(w_turned, b * (EPB * NMAT * MATGROUPS) + g + 1 + FIRST)
                    copy(w_turn[k % 2][:, (g % MATGROUPS) * BANK:(g % MATGROUPS + 1) * BANK], bank[4 + g % 2]).then_inc(w_out, 1)

                def ctx_out(ch):
                    for c in range(DC):
                        act.wait_ge(ctx_turned, b * (CHUNKS * DC) + (ch * DC + c + 1))
                        if c == 0:
                            act.wait_ge(scores_done, b * (CHUNKS * TPB) + max(ch - 1, 0) * TPB + FIRST)
                        copy(ctxT[:, ch % 2, c, :], bank[c]).then_inc(ctxT_ready, 1)

                ctx_out(0)
                for ch in range(CHUNKS):
                    if ch + 1 < CHUNKS:
                        ctx_out(ch + 1)
                    for g in range(BESIDE * ch, BESIDE * (ch + 1)):
                        expert_out(g)
                for g in range(BESIDE * CHUNKS, BESIDE * CHUNKS + 2):
                    expert_out(g)
                for t in range(TPB):
                    act.wait_ge(max_ready, b * TPB + t + 1)
                    if t == 0:
                        act.wait_ge(o_ready, b * TPB + FIRST)
                    for k in range(PIECES):
                        part = scores[t][:, k * (KEYS // PIECES):(k + 1) * (KEYS // PIECES)]
                        nc.scalar.activation(part, part, ACT.Exp, bias=nmax[:, t:t + 1],
                                             accum_out=lpart[:, t, k:k + 1]).then_inc(exp_done, 1)
                for g in range(BESIDE * CHUNKS + 2, EPB * NMAT * MATGROUPS):
                    expert_out(g)

            sqrt_of_var(2)
            for s in range(4):
                act.wait_ge(p2_done, s + 1)
                copy(x2nT[:, s // 2, (s % 2) * BANK:(s % 2 + 1) * BANK], bank[s]).then_inc(p2_act, 1)
            for s in range(4, 4 + 4 * DC):
                act.wait_ge(p2_done, s + 1)
                dst, bias = ((qT, qbc), (kT, kbc))[(s - 4) // (2 * DC)]
                c, half = (s - 4) // 2 % DC, s % 2
                nc.scalar.activation(dst[:, c, half * BANK:(half + 1) * BANK], bank[s % 8], ACT.Identity,
                                     bias=bias[:, c:c + 1]).then_inc(p2_act, 1)

            def local_softmax(b, u):
                t = UNITS[u][0]
                act.wait_ge(bias_ready, b * len(UNITS) + u + 1)
                for h in range(HPC):
                    part = local[u][:, h, KEY0[t]:KEY0[t] + SEEN[t]]
                    last = nc.scalar.activation(part, part, ACT.Exp, bias=hbias[:, u, h:h + 1], scale=float(DH) ** -0.5,
                                                accum_out=hsum[:, u, h:h + 1])
                last.then_inc(local_exp, 1)

            def local_batch(b, more):
                for u in range(len(UNITS)):
                    if u < 2 or more:
                        local_softmax(b if u < 2 else b + 1, (u + 2) % 4)

            local_softmax(0, 0)
            local_softmax(0, 1)
            with act.Fori(0, BATCH - 1) as b:
                local_batch(b, True)
            local_batch(BATCH - 1, False)

            sqrt_of_var(3)
            for s in range(4):
                act.wait_ge(p3_done, s + 1)
                copy(x3nT[:, s // 2, (s % 2) * BANK:(s % 2 + 1) * BANK], bank[s]).then_inc(p3_act, 1)
            act.wait_ge(lm_ready, 1)
            nc.scalar.activation(ex, ex, ACT.Exp).then_inc(gate_exp, 1)

            def tile_silu(j, n):
                for half in range(2):
                    act.wait_ge(g_done, j * 2 + half + 1)
                    if half == 0 and j is not 0:
                        act.wait_ge(hid_ready, j)
                    nc.scalar.activation(silu[n][:, half * BANK:(half + 1) * BANK], bank[half], ACT.Silu).then_inc(silu_ready, 1)

            def tile_hidT(j, n):
                for half in range(2):
                    act.wait_ge(hid_turned, j * 2 + half + 1)
                    copy(hidT[n][:, half * BANK:(half + 1) * BANK], bank[4 + half]).then_inc(hidT_ready, 1)

            def tile_store(j, n):
                act.wait_ge(y_ready, j + 1)
                act.dma_start(yg_dram[bass.ds(j * P, P), :], yt[n]).then_inc(y_stored[n], 16)

            tile_silu(0, 0)
            with act.Fori(1, SLOT_TILES, 2) as j2:
                for n in range(2):
                    tile_silu(j2 + n, 1 - n)
                    tile_hidT(j2 + (n - 1), n)
                    tile_store(j2 + (n - 1), n)
            tile_hidT(SLOT_TILES - 1, 0)
            tile_store(SLOT_TILES - 1, 0)

        @block.vector
        def _(dve):
            step = [0]

            def then(ins):
                step[0] += 1
                ins.then_inc(dve_step, 1)
                dve.wait_ge(dve_step, step[0])

            def layer_norm(dst, k):
                for t in range(TILES):
                    last = nc.vector.bn_stats(bn[:, t, :], xr[:, t, :])
                then(last)
                for t in range(TILES):
                    last = nc.vector.bn_aggr(mv[:, t, :], bn[:, t, :])
                last.then_inc(var_ready, 1)
                dve.wait_ge(sd_ready, k)
                then(nc.vector.reciprocal(rstd[:, :], sd[:, :]))
                for t in range(TILES):
                    nc.vector.tensor_scalar(dst[:, t, :], xr[:, t, :], mv[:, t, 0:1], rstd[:, t:t + 1],
                                            ALU.subtract, ALU.mult).then_inc(xn_ready, 1)

            dve.wait_ge(x_loaded, 16)
            layer_norm(xn, 1)
            for s in range(4):
                dve.wait_ge(setup_done, 16 + s)
                part = xr[:, 2 * s:2 * s + 2, :]
                then(nc.vector.tensor_tensor(part, part, bank[(15 + s) % 8].rearrange("p (t d) -> p t d", t=2), ALU.add))
                if s == 0:
                    dve.wait_ge(biases_loaded, 16 * len(biases))
                nc.vector.tensor_tensor(part, part, b2r[:, :].rearrange("p (a d) -> p a d", a=1).broadcast_to([P, 2, D]),
                                        ALU.add).then_inc(setup_dve, 1)

            step_at = step[0]
            PER = 4
            with dve.Fori(0, BATCH) as b:
                mine = [0]

                def then_b(ins):
                    mine[0] += 1
                    ins.then_inc(dve_step, 1)
                    dve.wait_ge(dve_step, b * PER + (step_at + mine[0]))

                dve.wait_ge(probs_turned, b * (TPB * CHUNKS) + FIRST)
                for ch in range(CHUNKS):
                    for t in range(TPB):
                        dve.wait_ge(scores_done, b * (CHUNKS * TPB) + (ch * TPB + t + 1) + FIRST)
                        nc.vector.tensor_scalar(scores[t][:, ch * BANK:(ch + 1) * BANK], bank[2 + t], 1.0, LOWEST, ALU.mult, ALU.max,
                                                accum_out=cmax[:, t, ch:ch + 1]).then_inc(scores_out, 1)
                dve.wait_ge(scores_out, b * (CHUNKS * TPB) + CHUNKS * TPB + FIRST)
                for t in range(TPB):
                    nc.vector.tensor_reduce(nmax[:, t:t + 1], cmax[:, t, :], axis=X_AXIS, op=ALU.max, negate=True).then_inc(max_ready, 1)

                def probs_out(g):
                    dve.wait_ge(probs_turned, b * (TPB * CHUNKS) + g + 1 + FIRST)
                    dve.wait_ge(pv_done, b * (TPB * CHUNKS) + max(g - 3, 0) + FIRST)
                    nc.vector.tensor_copy(pT[:, g % 4], bank[g % 2].rearrange("p (k n) -> p k n", k=TPG)).then_inc(probsT_ready, 1)

                def normalise(t):
                    dve.wait_ge(exp_done, b * (TPB * PIECES) + (t + 1) * PIECES)
                    then_b(nc.vector.tensor_reduce(lsum[:, t:t + 1], lpart[:, t, :], axis=X_AXIS, op=ALU.add))
                    then_b(nc.vector.reciprocal(linv[:, t:t + 1], lsum[:, t:t + 1]))
                    dve.wait_ge(pv_done, b * (TPB * CHUNKS) + (t + 1) * CHUNKS + FIRST)
                    nc.vector.tensor_scalar(o_sb[:, t, :], bank[6][:, 0:D], linv[:, t:t + 1], None, ALU.mult).then_inc(o_ready, 1)

                for g in range(CHUNKS + 1):
                    probs_out(g)
                normalise(0)
                for g in range(CHUNKS + 1, TPB * CHUNKS):
                    probs_out(g)
                normalise(1)
                for t in range(TPB):
                    dve.wait_ge(o_turned, b * TPB + t + 1)
                    nc.vector.tensor_copy(oT[:, t], bank[7][:, t * D:(t + 1) * D].rearrange("p (c n) -> p c n", c=DC)).then_inc(oT_ready, 1)
                dve.wait_ge(fused_done, b + 1)
                part = xr[:, bass.ds(b * TPB, TPB), :]
                nc.vector.tensor_tensor(part, part, bank[6].rearrange("p (t d) -> p t d", t=TPB), ALU.add).then_inc(x1_ready, 1)
                assert mine[0] == PER
            step[0] += BATCH * PER

            dve.wait_ge(x1_ready, BATCH + FIRST)
            dve.wait_ge(probs_turned, BATCH * TPB * CHUNKS + FIRST)
            layer_norm(x2n, 2)
            for s in range(4):
                dve.wait_ge(p2_done, 4 + 4 * DC + s + 1)
                nc.vector.tensor_tensor(v_tok[:, 2 * s:2 * s + 2, :], bank[(4 + 4 * DC + s) % 8].rearrange("p (t d) -> p t d", t=2),
                                        vbr[:, :].rearrange("p (a d) -> p a d", a=1).broadcast_to([P, 2, D]),
                                        ALU.add).then_inc(p2_dve, 1)
            dve.wait_ge(p2_dve, 4)
            dve.wait_ge(zeroed, 1 + DC)

            def local_values(b):
                dve.wait_ge(localpv_done, b * len(UNITS) + FIRST)
                for t in range(TPB):
                    dst = v_own[:, t].rearrange("p c (h n) -> p (c h) n", h=HPC)[:, :, 0:DH]
                    last = nc.vector.tensor_copy(dst, v_tok[:, bass.ds(b * TPB + t, 1), :].rearrange("p a (h n) -> p (a h) n", n=DH))
                last.then_inc(v_ready, 1)

            def local_max(b, u):
                t = UNITS[u][0]
                dve.wait_ge(local_done, b * len(UNITS) + u + 1 + FIRST)
                wide = P if t == 0 else NTOK
                nc.vector.memset(pause[:, 0:1], 0.0)
                for h in range(HPC):
                    at = (u * HPC * P if t == 0 else 0) + h * wide
                    last = nc.vector.tensor_tensor_reduce(
                        out=local[u][:, h, KEY0[t]:KEY0[t] + SEEN[t]], in0=psum[:, at:at + SEEN[t]], in1=mask[t][:, :],
                        scale=1.0, scalar=LOWEST, op0=ALU.add, op1=ALU.max, accum_out=hmax[:, u, h:h + 1])
                last.then_inc(row_max, 1)
                dve.wait_ge(row_max, b * len(UNITS) + u + 1 + FIRST)
                nc.vector.tensor_scalar(hbias[:, u, :], hmax[:, u, :], -float(DH) ** -0.5, None, ALU.mult).then_inc(bias_ready, 1)

            def local_inv(b, u):
                dve.wait_ge(local_exp, b * len(UNITS) + u + 1)
                nc.vector.reciprocal(hinv[:, u, :], hsum[:, u, :]).then_inc(inv_ready, 1)

            def local_evict(b, u, groups):
                for g in groups:
                    at = GROUP0[u] + g
                    dve.wait_ge(local_turned, b * sum(GROUPS) + at + 1 + FIRST)
                    nc.vector.tensor_copy(pT[:, at % 4], bank[4 + at % 2].rearrange("p (k n) -> p k n", k=TPG)).then_inc(localT_ready, 1)

            def local_out(b, u):
                t, hc = UNITS[u]
                dve.wait_ge(localpv_done, b * len(UNITS) + u + 1 + FIRST)
                nc.vector.tensor_copy(headsT[:, hc, bass.ds(b * NTOK + t * P, P)], bank[6 + u % 2][:, 0:P]).then_inc(heads_ready, 1)

            def local_batch(b, more):
                for u in range(len(UNITS)):
                    local_evict(b, u, range(2))
                    if u < 3 or more:
                        local_inv(b if u < 3 else b + 1, (u + 1) % 4)
                    if u < 2 or more:
                        local_max(b if u < 2 else b + 1, (u + 2) % 4)
                    local_evict(b, u, range(2, GROUPS[u]))
                    local_out(b, u)
                if more:
                    local_values(b + 1)

            local_values(0)
            local_max(0, 0)
            local_max(0, 1)
            local_inv(0, 0)
            with dve.Fori(0, BATCH - 1) as b:
                local_batch(b, True)
            local_batch(BATCH - 1, False)
            for s in range(4):
                dve.wait_ge(p2c_done, s + 1)
                part = xr[:, 2 * s:2 * s + 2, :]
                then(nc.vector.tensor_tensor(part, part, bank[s].rearrange("p (t d) -> p t d", t=2), ALU.add))
                then(nc.vector.tensor_tensor(part, part, obr[:, :].rearrange("p (a d) -> p a d", a=1).broadcast_to([P, 2, D]), ALU.add))

            layer_norm(x3n, 3)
            dve.wait_ge(p3_done, 5)
            then(nc.vector.tensor_copy(lo, bank[4][:, 0:TILES * E].rearrange("p (t e) -> p t e", t=TILES)))
            for t in range(TILES):
                other = lo[:, t, :].rearrange("p (a f) -> p a f", a=1).broadcast_to([P, E, E])
                own = lo[:, t, :].rearrange("p (e a) -> p e a", a=1).broadcast_to([P, E, E])
                nc.vector.tensor_tensor(above[:, t], other, own, ALU.is_gt)
                last = nc.vector.tensor_tensor(ties[:, t], other, own, ALU.is_equal)
            then(last)
            flat = "p t e f -> p t (e f)"
            low = lower_i.rearrange("p e f -> p (e f)").rearrange("p (a n) -> p a n", a=1).broadcast_to([P, TILES, E * E])
            then(nc.vector.tensor_tensor(ties.rearrange(flat), ties.rearrange(flat), low, ALU.mult))
            then(nc.vector.tensor_tensor(above.rearrange(flat), above.rearrange(flat), ties.rearrange(flat), ALU.add))
            then(nc.vector.tensor_reduce(place, above, axis=X_AXIS, op=ALU.add))
            nc.vector.tensor_scalar(chosen, place, float(TOPK) - 0.5, None, ALU.is_lt).then_inc(chosen_ready, 1)
            for n in range(TOPK):
                nc.vector.tensor_scalar(nth[n], place, float(n), None, ALU.is_equal)
            then(nc.vector.tensor_reduce(lmax[:, :], lo, axis=X_AXIS, op=ALU.max))

            def over_e(col):
                return col.rearrange("p (t a) -> p t a", a=1).broadcast_to([P, TILES, E])

            nc.vector.tensor_tensor(ex, lo, over_e(lmax[:, :]), ALU.subtract).then_inc(lm_ready, 1)
            dve.wait_ge(ranks_done, 1)
            nc.vector.tensor_copy(pos, bank[5][:, 0:TILES * E].rearrange("p (t e) -> p t e", t=TILES))
            then(nc.vector.tensor_copy(tots, bank[5][:, TILES * E:2 * TILES * E].rearrange("p (t e) -> p t e", t=TILES)))
            by_t = above
            for e in range(E):
                last = nc.vector.tensor_tensor(by_t[:, e], tots[:, :, e].rearrange("p (a t) -> p a t", a=1).broadcast_to([P, TILES, TILES]),
                                               lower_i, ALU.mult)
            nc.vector.tensor_reduce(cnt[:, :], tots.rearrange("p t e -> p e t"), axis=X_AXIS, op=ALU.add)
            then(nc.vector.tensor_scalar(ginv[:, :], ginv0 := lmax[:, :], 0.0, None, ALU.mult))
            nc.vector.tensor_reduce(before.rearrange("p t e -> p e t"), by_t, axis=X_AXIS, op=ALU.add)
            cmp = ties[:, 0]
            then(nc.vector.tensor_tensor(cmp, cnt[:, :].rearrange("p (e a) -> p e a", a=1).broadcast_to([P, E, E]),
                                         steps[:, :].rearrange("p (a k) -> p a k", a=1).broadcast_to([P, E, E]), ALU.is_gt))
            then(nc.vector.tensor_reduce(need[:, :], cmp, axis=X_AXIS, op=ALU.add))
            then(nc.vector.tensor_tensor(ties[:, 1], need[:, :].rearrange("p (a f) -> p a f", a=1).broadcast_to([P, E, E]), lower_i, ALU.mult))
            then(nc.vector.tensor_reduce(first[:, :], ties[:, 1], axis=X_AXIS, op=ALU.add))
            nc.vector.tensor_tensor(pos, pos, before, ALU.add)
            then(nc.vector.tensor_tensor(cmp23, tileno[:, :].rearrange("p (j a) -> p j a", a=1).broadcast_to([P, SLOT_TILES, E - 1]),
                                         first[:, 1:E].rearrange("p (a e) -> p a e", a=1).broadcast_to([P, SLOT_TILES, E - 1]), ALU.is_ge))
            then(nc.vector.tensor_reduce(owner_f[:, :], cmp23, axis=X_AXIS, op=ALU.add))
            nc.vector.tensor_copy(owner[:, :], owner_f[:, :])
            then(nc.vector.tensor_scalar(need[:, :], first[:, :], float(P), None, ALU.mult))
            then(nc.vector.tensor_tensor(pos, pos, need[:, :].rearrange("p (a e) -> p a e", a=1).broadcast_to([P, TILES, E]), ALU.add))
            for n in range(TOPK):
                then(nc.vector.tensor_tensor(before, pos, nth[n], ALU.mult))
                then(nc.vector.tensor_reduce(slotf[n][:, :], before, axis=X_AXIS, op=ALU.add))
                last = nc.vector.tensor_copy(slot[n][:, :], slotf[n][:, :])
            last.then_inc(slots_ready, 1)
            dve.wait_ge(gate_exp, 1)
            then(nc.vector.tensor_tensor(ex, ex, chosen, ALU.mult))
            then(nc.vector.tensor_reduce(gsum[:, :], ex, axis=X_AXIS, op=ALU.add))
            then(nc.vector.reciprocal(ginv[:, :], gsum[:, :]))
            then(nc.vector.tensor_tensor(ex, ex, over_e(ginv[:, :]), ALU.mult))
            for n in range(TOPK):
                then(nc.vector.tensor_tensor(pos, ex, nth[n], ALU.mult))
                then(nc.vector.tensor_reduce(prob[n][:, :], pos, axis=X_AXIS, op=ALU.add))

            def tile_xgT(j, n):
                dve.wait_ge(xg_turned, j + 1)
                nc.vector.tensor_copy(xgT[n], bank[7][:, 0:DC * P]).then_inc(xgT_ready, 1)

            def tile_hid(j, n):
                for half in range(2):
                    dve.wait_ge(silu_ready, j * 2 + half + 1)
                    dve.wait_ge(u_done, j * 2 + half + 1)
                    cols = slice(half * BANK, (half + 1) * BANK)
                    last = nc.vector.tensor_tensor(hid[n][:, cols], silu[n][:, cols], bank[2 + half], ALU.mult)
                last.then_inc(hid_ready, 1)

            def tile_y(j, n, again):
                dve.wait_ge(y_done, j + 1)
                if again is not None:
                    dve.wait_ge(y_stored[n], again + FIRST)
                nc.vector.tensor_copy(yt[n], bank[6][:, 0:D]).then_inc(y_ready, 1)

            tile_xgT(0, 0)
            tile_hid(0, 0)
            tile_xgT(1, 1)

            def two_tiles(j2, more):
                tile_hid(j2, 1)
                tile_xgT(j2 + 1, 0)
                tile_y(j2 - 1, 0, (j2 - 1) * 8)
                tile_hid(j2 + 1, 0)
                if more:
                    tile_xgT(j2 + 2, 1)
                tile_y(j2, 1, (j2 - 1) * 8)

            with dve.Fori(1, SLOT_TILES - 2, 2) as j2:
                two_tiles(j2, True)
            two_tiles(SLOT_TILES - 2, False)
            tile_y(SLOT_TILES - 1, 0, 16 * (SLOT_TILES // 2))

            for t in range(TILES):
                dve.wait_ge(gathered[t], 16 * TOPK)
                then(nc.vector.scalar_tensor_tensor(out=x3n[:, t, :], in0=y_of[:, 0, t, :], scalar=prob[0][:, t:t + 1],
                                                    in1=xr[:, t, :], op0=ALU.mult, op1=ALU.add))
                nc.vector.scalar_tensor_tensor(out=x3n[:, t, :], in0=y_of[:, 1, t, :], scalar=prob[1][:, t:t + 1],
                                               in1=x3n[:, t, :], op0=ALU.mult, op1=ALU.add).then_inc(out_ready, 1)

        @block.tensor
        def _(pe):
            def turn(dst, src):
                return nc.tensor.transpose(dst, src, ident[0:src.shape[0], 0:src.shape[0]])

            def turn_tiles(src, s, bank0=0):
                c, half = s // 2, s % 2
                for k in range(TPG):
                    last = turn(bank[(bank0 + s) % 8][:, k * P:(k + 1) * P], src[:, half * TPG + k, c * P:(c + 1) * P])
                return last

            pe.wait_ge(consts, N_CONST)
            pe.wait_ge(small_loaded, 16 * len(small))

            def turn_weight(nat, width, f0, s):
                w = nat.rearrange("p (c n) -> p c n", c=DC)
                for f in range(2):
                    for o in range(DC):
                        last = turn(bank[s % 8][:, (f * DC + o) * P:(f * DC + o + 1) * P], w[:, o, (f0 + f) * P:(f0 + f + 1) * P])
                return last

            for s, (nat, width, f0) in enumerate(((w1_nat, D, 0), (w2_nat, 2 * D, 0), (w2_nat, 2 * D, DC), (q_nat, D, 0),
                                                  (k_nat, D, 0), (v_nat, D, 0), (o_nat, D, 0))):
                turn_weight(nat, width, f0, s).then_inc(setup_done, 1)
            for s in range(4):
                if s < 2:
                    pe.wait_ge(xn_ready, TPG * (s + 1))
                if s > 0:
                    pe.wait_ge(setup_act, s)
                turn_tiles(xn, s, 7).then_inc(setup_done, 1)
            pe.wait_ge(setup_act, 11)
            for s in range(4):
                kc, half = s // 2, s % 2
                for c in range(DC):
                    last = nc.tensor.matmul(bank[(11 + s) % 8], w1T[:, c, kc * P:(kc + 1) * P], xnT[:, c, half * BANK:(half + 1) * BANK],
                                            start=c == 0, stop=c == DC - 1)
                last.then_inc(setup_done, 1)
            for s in range(4):
                for t in range(2):
                    for c in range(DC):
                        last = nc.tensor.matmul(bank[(15 + s) % 8][:, t * D:(t + 1) * D], xnT[:, c, (2 * s + t) * P:(2 * s + t + 1) * P],
                                                w2T[:, c, :], start=c == 0, stop=c == DC - 1)
                last.then_inc(setup_done, 1)
            pe.wait_ge(setup_act, 15)
            pe.wait_ge(setup_dve, 4)

            GR = TPB * CHUNKS
            WGR = EPB * NMAT * MATGROUPS
            with pe.Fori(0, BATCH // 2) as i:
                for n in range(2):
                    b = i * 2 + n

                    def turn_ctx(ch):
                        if ch % 2 == 0:
                            pe.wait_ge(ctx_loaded[n][ch // 2], i * 16 + 16)
                        for c in range(DC):
                            if ch == 0:
                                pe.wait_ge(probsT_ready, b * GR + FIRST)
                            else:
                                pe.wait_ge(ctxT_ready, b * (CHUNKS * DC) + (ch - 1) * DC + c + 1)
                            for k in range(TPG):
                                last = turn(bank[c][:, k * P:(k + 1) * P], ctx_sb[n][:, ch * TPG + k, c * P:(c + 1) * P])
                            last.then_inc(ctx_turned, 1)

                    def score(ch):
                        pe.wait_ge(ctxT_ready, b * (CHUNKS * DC) + (ch + 1) * DC)
                        for t in range(TPB):
                            pe.wait_ge(scores_out, b * GR + max(ch - 1, 0) * TPB + (t + 1 if ch else 0) + FIRST)
                            for c in range(DC):
                                last = nc.tensor.matmul(bank[2 + t], bf_st[n][:, c, t * P:(t + 1) * P], ctxT[:, ch % 2, c, :],
                                                        start=c == 0, stop=c == DC - 1)
                            last.then_inc(scores_done, 1)

                    def turn_expert(g):
                        k, gq = g // MATGROUPS, g % MATGROUPS
                        if gq == 0:
                            pe.wait_ge(w_loaded[k % 2], b * (16 * EPB * NMAT // 2) + 16 * (k // 2 + 1))
                        pe.wait_ge(w_out, b * WGR + max(g - 1, 0) + FIRST)
                        for q in range(TPG):
                            if k % NMAT < 2:
                                src = w_nat[k % 2].rearrange("p (c n) -> p c n", c=IC)[:, TPG * (gq % 2) + q, (gq // 2) * P:(gq // 2 + 1) * P]
                            else:
                                ic = 2 * gq + q // 2
                                src = w_nat[k % 2].rearrange("p (c n) -> p c n", c=DC)[:, q % 2, ic * P:(ic + 1) * P]
                            last = turn(bank[4 + g % 2][:, q * P:(q + 1) * P], src)
                        last.then_inc(w_turned, 1)

                    pe.wait_ge(bf_ready, b + 1)
                    turn_ctx(0)
                    for ch in range(CHUNKS):
                        if ch + 1 < CHUNKS:
                            turn_ctx(ch + 1)
                        score(ch)
                        for g in range(BESIDE * ch, BESIDE * (ch + 1)):
                            turn_expert(g)
                    for g in range(BESIDE * CHUNKS, BESIDE * CHUNKS + 2):
                        turn_expert(g)

                    def turn_probs(g):
                        t, k0 = g // CHUNKS, g % CHUNKS * TPG
                        if k0 % (KT // PIECES) == 0:
                            pe.wait_ge(exp_done, b * (TPB * PIECES) + t * PIECES + k0 // (KT // PIECES) + 1)
                        if g < 2:
                            pe.wait_ge(ctxT_ready, b * (CHUNKS * DC) + CHUNKS * DC)
                        else:
                            pe.wait_ge(probsT_ready, b * GR + g - 1 + FIRST)
                        for k in range(TPG):
                            last = turn(bank[g % 2][:, k * P:(k + 1) * P], scores[t][:, (k0 + k) * P:(k0 + k + 1) * P])
                        last.then_inc(probs_turned, 1)

                    def weigh(g):
                        t, k0 = g // CHUNKS, g % CHUNKS * TPG
                        pe.wait_ge(probsT_ready, b * GR + g + 1 + FIRST)
                        if g == 0:
                            pe.wait_ge(x1_ready, b + FIRST)
                        elif k0 == 0:
                            pe.wait_ge(o_ready, b * TPB + t + FIRST)
                        for k in range(TPG):
                            last = nc.tensor.matmul(bank[6][:, 0:D], pT[:, g % 4, k, :], ctx_sb[n][:, k0 + k, :],
                                                    start=k0 + k == 0, stop=k0 + k == KT - 1)
                        last.then_inc(pv_done, 1)

                    turn_probs(0)
                    for g in range(TPB * CHUNKS):
                        if g + 1 < TPB * CHUNKS:
                            turn_probs(g + 1)
                        weigh(g)
                    for t in range(TPB):
                        if t == 1:
                            for g in range(BESIDE * CHUNKS + 2, WGR - 3):
                                turn_expert(g)
                        pe.wait_ge(o_ready, b * TPB + t + 1 + FIRST)
                        pe.wait_ge(oT_ready, b * TPB + t + FIRST)
                        for c in range(DC):
                            last = turn(bank[7][:, t * D + c * P:t * D + (c + 1) * P], o_sb[:, t, c * P:(c + 1) * P])
                        last.then_inc(o_turned, 1)
                    for g in range(WGR - 3, WGR):
                        turn_expert(g)
                    for t in range(TPB):
                        pe.wait_ge(oT_ready, b * TPB + t + 1 + FIRST)
                        for c in range(DC):
                            last = nc.tensor.matmul(bank[6][:, t * D:(t + 1) * D], oT[:, t, c, :], w2T[:, DC + c, :],
                                                    start=c == 0, stop=c == DC - 1)
                    last.then_inc(fused_done, 1)

            pe.wait_ge(x1_ready, BATCH + FIRST)
            pe.wait_ge(w_out, BATCH * WGR + FIRST)
            for s in range(4):
                if s < 2:
                    pe.wait_ge(xn_ready, TILES + TPG * (s + 1))
                turn_tiles(x2n, s).then_inc(p2_done, 1)
            pe.wait_ge(p2_act, 4)
            for s in range(4, 4 + 4 * DC):
                w = (qwT, kwT)[(s - 4) // (2 * DC)]
                hc, half = (s - 4) // 2 % DC, s % 2
                if s >= 8:
                    pe.wait_ge(p2_act, s - 7)
                for c in range(DC):
                    last = nc.tensor.matmul(bank[s % 8], w[:, c, hc * P:(hc + 1) * P], x2nT[:, c, half * BANK:(half + 1) * BANK],
                                            start=c == 0, stop=c == DC - 1)
                last.then_inc(p2_done, 1)
            for s in range(4):
                at = 4 + 4 * DC + s
                pe.wait_ge(p2_act, at - 7)
                for t in range(2):
                    for c in range(DC):
                        last = nc.tensor.matmul(bank[at % 8][:, t * D:(t + 1) * D], x2nT[:, c, (2 * s + t) * P:(2 * s + t + 1) * P],
                                                vwT[:, c, :], start=c == 0, stop=c == DC - 1)
                last.then_inc(p2_done, 1)
            pe.wait_ge(p2_act, 4 + 4 * DC)
            pe.wait_ge(p2_dve, 4)
            pe.wait_ge(zeroed, 1 + DC)

            def local_score(b, u):
                t, hc = UNITS[u]
                pe.wait_ge(q_ready, b * len(UNITS) + u + 1)
                pe.wait_ge(row_max, b * len(UNITS) + u + FIRST)
                for h in range(HPC):
                    at = u * HPC * P + h * P if t == 0 else h * NTOK
                    last = nc.tensor.matmul(psum[:, at:at + SEEN[t]], q_own[u % 2][:, h, :],
                                            kT[:, hc, bass.ds(b * NTOK + KEY0[t], SEEN[t])], start=True, stop=True)
                last.then_inc(local_done, 1)

            def local_turn(b, u, g):
                tiles = UNITS[u][0] + 1
                at = GROUP0[u] + g
                pe.wait_ge(localT_ready, b * sum(GROUPS) + max(at - 1, 0) + FIRST)
                for k in range(TPG):
                    h, kt = (g * TPG + k) // tiles, k % tiles
                    last = turn(bank[4 + at % 2][:, k * P:(k + 1) * P], local[u][:, h, kt * P:(kt + 1) * P])
                last.then_inc(local_turned, 1)

            def local_weigh(b, u):
                t, hc = UNITS[u]
                tiles = t + 1
                if u == 0:
                    pe.wait_ge(v_ready, b + 1)
                pe.wait_ge(heads_ready, b * len(UNITS) + max(u - 1, 0) + FIRST)
                for g in range(GROUPS[u]):
                    pe.wait_ge(localT_ready, b * sum(GROUPS) + GROUP0[u] + g + 1 + FIRST)
                    for k in range(TPG):
                        h, kt = (g * TPG + k) // tiles, k % tiles
                        last = nc.tensor.matmul(bank[6 + u % 2][:, 0:P], v_own[:, kt, hc, h * P:(h + 1) * P], pT[:, (GROUP0[u] + g) % 4, k, :],
                                                start=g == 0 and k == 0, stop=g == GROUPS[u] - 1 and k == TPG - 1)
                    if g + 2 < GROUPS[u]:
                        local_turn(b, u, g + 2)
                last.then_inc(localpv_done, 1)

            def local_batch(b, more):
                for u in range(len(UNITS)):
                    pe.wait_ge(normed, b * len(UNITS) + u + 1)
                    local_turn(b, u, 0)
                    local_turn(b, u, 1)
                    if u < 2 or more:
                        local_score(b if u < 2 else b + 1, (u + 2) % 4)
                    local_weigh(b, u)

            local_score(0, 0)
            local_score(0, 1)
            with pe.Fori(0, BATCH - 1) as b:
                local_batch(b, True)
            local_batch(BATCH - 1, False)

            pe.wait_ge(heads_ready, BATCH * len(UNITS) + FIRST)
            for s in range(4):
                for t in range(2):
                    for c in range(DC):
                        last = nc.tensor.matmul(bank[s][:, t * D:(t + 1) * D], headsT[:, c, (2 * s + t) * P:(2 * s + t + 1) * P],
                                                owT[:, c, :], start=c == 0, stop=c == DC - 1)
                last.then_inc(p2c_done, 1)

            for s in range(4):
                if s < 2:
                    pe.wait_ge(xn_ready, 2 * TILES + TPG * (s + 1))
                turn_tiles(x3n, s).then_inc(p3_done, 1)
            pe.wait_ge(p3_act, 4)
            for t in range(TILES):
                for c in range(DC):
                    last = nc.tensor.matmul(bank[4][:, t * E:(t + 1) * E], x3nT[:, c, t * P:(t + 1) * P], gwT[:, c, :],
                                            start=c == 0, stop=c == DC - 1)
            last.then_inc(p3_done, 1)
            pe.wait_ge(chosen_ready, 1)
            rows = chosen.rearrange("p t e -> p (t e)")
            nc.tensor.matmul(bank[5][:, 0:TILES * E], earlier[:, :], rows, start=True, stop=True)
            nc.tensor.matmul(bank[5][:, TILES * E:2 * TILES * E], ones[:, :], rows, start=True, stop=True).then_inc(ranks_done, 1)

            pe.wait_ge(slots_ready, 1)

            def tile_turn(j, n, arrived):
                pe.wait_ge(xg_loaded[n], arrived)
                if j is not 0:
                    pe.wait_ge(xgT_ready, j)
                for c in range(DC):
                    last = turn(bank[7][:, c * P:(c + 1) * P], xg[n][:, c * P:(c + 1) * P])
                last.then_inc(xg_turned, 1)

            def tile_up(j, n, arrived):
                pe.wait_ge(up_loaded[n], arrived)
                pe.wait_ge(xgT_ready, j + 1)
                for m, done in enumerate((g_done, u_done)):
                    for half in range(2):
                        if j is not 0:
                            if m == 0:
                                pe.wait_ge(silu_ready, j * 2)
                            else:
                                pe.wait_ge(hid_ready, j)
                        for c in range(DC):
                            at = m * MAT + c * INNER + half * BANK
                            last = nc.tensor.matmul(bank[2 * m + half], xgT[n][:, c * P:(c + 1) * P], w_up[n][:, at:at + BANK],
                                                    start=c == 0, stop=c == DC - 1)
                        last.then_inc(done, 1)

            def tile_down(j, n, arrived):
                pe.wait_ge(down_loaded[n], arrived)
                pe.wait_ge(hid_ready, j + 1)
                if j is not 0:
                    pe.wait_ge(hidT_ready, j * 2)
                for half in range(2):
                    for k in range(TPG):
                        at = (half * TPG + k) * P
                        last = turn(bank[4 + half][:, k * P:(k + 1) * P], hid[n][:, at:at + P])
                    last.then_inc(hid_turned, 1)
                if j is not 0:
                    pe.wait_ge(y_ready, j)
                for ic in range(IC):
                    if ic % TPG == 0:
                        pe.wait_ge(hidT_ready, j * 2 + ic // TPG + 1)
                    at = ic * D
                    last = nc.tensor.matmul(bank[6][:, 0:D], hidT[n][:, ic * P:(ic + 1) * P], w_down[n][:, at:at + D],
                                            start=ic == 0, stop=ic == IC - 1)
                last.then_inc(y_done, 1)

            tile_turn(0, 0, 16)
            tile_up(0, 0, 16)
            tile_turn(1, 1, 16)

            def two_tiles(j2, more):
                tile_up(j2, 1, (j2 + 1) * 8)
                tile_turn(j2 + 1, 0, (j2 + 3) * 8)
                tile_down(j2 - 1, 0, (j2 + 1) * 8)
                tile_up(j2 + 1, 0, (j2 + 3) * 8)
                if more:
                    tile_turn(j2 + 2, 1, (j2 + 3) * 8)
                tile_down(j2, 1, (j2 + 1) * 8)

            with pe.Fori(1, SLOT_TILES - 2, 2) as j2:
                two_tiles(j2, True)
            two_tiles(SLOT_TILES - 2, False)
            tile_down(SLOT_TILES - 1, 0, (SLOT_TILES + 1) * 8)


_INS = ["x", "ctx_1024", "L0_xattn_w1_w", "L0_xattn_w1_b", "L0_xattn_w2_w", "L0_xattn_w2_b", "L0_attn_q_w", "L0_attn_q_b",
        "L0_attn_k_w", "L0_attn_k_b", "L0_attn_v_w", "L0_attn_v_b", "L0_attn_o_w", "L0_attn_o_b", "L0_ffn_gate_w",
        "L0_ffn_wg", "L0_ffn_wu", "L0_ffn_wd"]


def kernel(**inputs):
    import numpy as np
    import concourse.bacc as bacc
    from concourse.bass_utils import run_bass_kernel_spmd

    nc = bacc.Bacc("TRN2", target_bir_lowering=False, num_devices=1)
    arrays, args = {}, []
    for name in _INS:
        a = np.ascontiguousarray(inputs[name])
        arrays[name + "_dram"] = a
        args.append(nc.dram_tensor(name + "_dram", a.shape, mybir.dt.from_np(a.dtype), kind="ExternalInput").ap())
    out = nc.dram_tensor("out_dram", (BATCH, NTOK, D), F32, kind="ExternalOutput").ap()
    perceiver(nc, *args, out)
    r = run_bass_kernel_spmd(nc, [arrays], core_ids=[0])
    return r.results[0]["out_dram"]
```

```python
import concourse.bass as bass
from concourse import mybir
from contextlib import ExitStack

F32 = mybir.dt.float32
F32R = mybir.dt.float32r
I32 = mybir.dt.int32
ALU = mybir.AluOpType
ACT = mybir.ActivationFunctionType
X_AXIS = mybir.AxisListType.X

P = 128
BATCH, NTOK, D = 4, 256, 256
KEYS = 4096
TOK = BATCH * NTOK
TILES = TOK // P
TPB = NTOK // P
DUOS = TILES // 2
DC = D // P
KT = KEYS // P
BANK = 512
TPG = BANK // P
CHUNKS = KEYS // BANK
PIECES = KEYS // BANK
PAIR = 2
PAIRS = KT // PAIR
HEADS, DH, WIN = 16, 16, 64
HPC = P // DH
SEEN = [P, P + WIN]
KEY0 = [0, P - WIN]
UNITS = [(t, hc) for t in range(2) for hc in range(DC)]
GROUPS = [HPC * (t + 1) // 4 for t, _ in UNITS]
GROUP0 = [sum(GROUPS[:u]) for u in range(len(UNITS))]
E, INNER, TOPK = 8, 1024, 2
IC = INNER // P
MAT = D * INNER // P
NMAT = 3
MATGROUPS = MAT // BANK
SLOT_TILES = (TOK * TOPK + E * (P - 1)) // P
SLOTS = SLOT_TILES * P
ROW = D + 2
RESULTS = TOK * TOPK
WARM = 8
EPS = 1e-5
LOWEST = -3.0e38
MASKED = -1.0e30
FIRST = 1
EPB = E // BATCH
PPB = EPB * NMAT
GPB = PPB * MATGROUPS
BESIDE = 2
WAITING = BESIDE * CHUNKS // MATGROUPS
GPB_ACT = GPB - MATGROUPS


def perceiver(nc, x, ctx, w1_w, w1_b, w2_w, w2_b, q_w, q_b, k_w, k_b, v_w, v_b, o_w, o_b,
              gate_w, wg, wu, wd, out):
    stack = ExitStack()
    with stack:
        def sb(name, cols, dt=F32):
            return stack.enter_context(nc.sbuf_tensor(name, [P, cols], dt))

        def sem(name):
            return stack.enter_context(nc.semaphore(name))

        wt_dram = nc.dram_tensor("turned_weights", [E, P, NMAT * MAT], F32).ap()
        xg_dram = nc.dram_tensor("rows_by_expert", [SLOTS, ROW], F32).ap()
        y_dram = nc.dram_tensor("results_by_token", [RESULTS + P, D], F32).ap()

        region_a = sb("region_a", 2 * KT * D)
        region_s = sb("region_s", TPB * KEYS)
        region_w = sb("region_w", 4 * MAT)

        def cut(region, widths):
            at, parts = 0, []
            for w in widths:
                parts.append(region[:, at:at + w])
                at += w
            assert at <= region.shape[1], (at, region.shape)
            return parts

        ctx_sb = [region_a[:, n * KT * D:(n + 1) * KT * D].rearrange("p (t d) -> p t d", t=KT) for n in range(2)]
        scores = [region_s[:, n * KEYS:(n + 1) * KEYS] for n in range(TPB)]
        w_nat0, w_nat1, w_turn0, w_turn1 = cut(region_w, [MAT] * 4)
        w_nat, w_turn = [w_nat0, w_nat1], [w_turn0, w_turn1]
        xn_f, xnT_f, w1T_f, w1_nat, w2_nat, q_nat, k_nat, v_nat, o_nat = cut(
            region_s, [TILES * D, DC * TOK, DC * D, DC * D, DC * 2 * D, DC * D, DC * D, DC * D, DC * D])
        xn = xn_f.rearrange("p (t d) -> p t d", t=TILES)
        xnT = xnT_f.rearrange("p (c n) -> p c n", c=DC)
        w1T = w1T_f.rearrange("p (c n) -> p c n", c=DC)
        qT_f, kT_f, v_f, x2nT_f, sl0, sl1, sl2, sl3 = cut(region_a, [DC * TOK] * 4 + [HPC * P] * 2 + [HPC * NTOK] * 2)
        qT, kT, x2nT = [r.rearrange("p (c n) -> p c n", c=DC) for r in (qT_f, kT_f, x2nT_f)]
        v_tok = v_f.rearrange("p (t d) -> p t d", t=TILES)
        local = [s.rearrange("p (h k) -> p h k", h=HPC) for s in (sl0, sl1, sl2, sl3)]
        x2n_f, pT_f, _, headsT_f = cut(region_s, [TILES * D, 4 * BANK, DC * TOK, DC * TOK])
        pT = pT_f.rearrange("p (r k n) -> p r k n", r=4, k=TPG)
        x2n = x2n_f.rearrange("p (t d) -> p t d", t=TILES)
        q_own0, q_own1, v_own_f = cut(region_w, [HPC * P, HPC * P, TPB * DC * HPC * (P + DH)])
        headsT = headsT_f.rearrange("p (c n) -> p c n", c=DC)
        q_own = [s.rearrange("p (h n) -> p h n", h=HPC) for s in (q_own0, q_own1)]
        v_own = v_own_f.rearrange("p (t c n) -> p t c n", t=TPB, c=DC)
        w_up = [region_a[:, n * 2 * MAT:(n + 1) * 2 * MAT] for n in range(2)]
        w_down = [region_a[:, (4 + n) * MAT:(5 + n) * MAT] for n in range(2)]
        rows0, rows1, x3nT_f = cut(region_s, [TILES * ROW] * 2 + [DC * TOK])
        rows = [r.rearrange("p (t d) -> p t d", t=TILES) for r in (rows0, rows1)]
        x3n = rows[0][:, :, 0:D]
        x3nT = x3nT_f.rearrange("p (c n) -> p c n", c=DC)
        hid = [x3nT_f[:, n * INNER:(n + 1) * INNER] for n in range(2)]
        xg0, xg1, hidT0, hidT1, yt0, yt1, silu0, silu1 = cut(region_w, [ROW] * 2 + [INNER] * 2 + [D] * 2 + [INNER] * 2)
        xg, hidT, yt, silu = [xg0, xg1], [hidT0, hidT1], [yt0, yt1], [silu0, silu1]
        y_f = region_a[:, 0:2 * TILES * D]
        y_of = y_f.rearrange("p (t k d) -> p t k d", k=TOPK, t=TILES)

        xr_t = sb("residual", TILES * D)
        xr = xr_t[:, :].rearrange("p (t d) -> p t d", t=TILES)
        bfT_t = sb("bfT", DC * TOK)
        bfT = bfT_t[:, :].rearrange("p (c n) -> p c n", c=DC)
        def two_parts(name, cols):
            return [stack.enter_context(nc.sbuf_tensor(f"{name}_{part}", [P, cols], F32R)) for part in ("high", "low")]

        wide_parts = two_parts("wide", 3 * DC * BANK)
        turned_parts = two_parts("turned", 2 * BANK)
        ctxT_hi, ctxT_lo = [t[:, 0:2 * DC * BANK].rearrange("p (r c n) -> p r c n", r=2, c=DC) for t in wide_parts]
        val_hi, val_lo = [t[:, 0:2 * DC * BANK].rearrange("p (r k d) -> p r k d", r=4, k=PAIR) for t in wide_parts]
        bf_hi, bf_lo = [t[:, 2 * DC * BANK:].rearrange("p (n c k) -> p n c k", n=2, c=DC) for t in wide_parts]
        pT_hi, pT_lo = [t[:, :].rearrange("p (r k n) -> p r k n", r=2, k=PAIR) for t in turned_parts]
        w_hi, w_lo = [t[:, :].rearrange("p (r c n) -> p r c n", r=3, c=DC) for t in wide_parts]
        xgT_hi, xgT_lo = [t[:, 0:2 * DC * P].rearrange("p (n k) -> p n k", n=2) for t in turned_parts]
        w2T = sb("w2T", 2 * DC * D)[:, :].rearrange("p (c n) -> p c n", c=2 * DC)
        qwT = sb("qwT", DC * D)[:, :].rearrange("p (c n) -> p c n", c=DC)
        kwT = sb("kwT", DC * D)[:, :].rearrange("p (c n) -> p c n", c=DC)
        vwT = sb("vwT", DC * D)[:, :].rearrange("p (c n) -> p c n", c=DC)
        owT = sb("owT", DC * D)[:, :].rearrange("p (c n) -> p c n", c=DC)
        gwT = sb("gwT", DC * E)[:, :].rearrange("p (c e) -> p c e", c=DC)
        ident = sb("ident", P)
        no_row = sb("no_row", ROW)
        zeros = no_row[:, 0:D + 1]
        mask = [sb(f"mask{t}", SEEN[t]) for t in range(TPB)]
        head_rows = sb("head_rows", HPC)
        earlier = sb("earlier", P)
        ones = sb("ones", P)
        b1c = sb("b1_cols", DC)
        qbc = sb("qb_cols", DC)
        kbc = sb("kb_cols", DC)
        b2r = sb("b2_rows", D)
        vbr = sb("vb_rows", D)
        obr = sb("ob_rows", D)
        eps_c = sb("eps", 1)
        bn = sb("ln_stats", TILES * 6)[:, :].rearrange("p (t s) -> p t s", t=TILES)
        mv = sb("ln_mean_var", TILES * 2)[:, :].rearrange("p (t s) -> p t s", t=TILES)
        sd = sb("ln_sd", TILES)
        rstd = sb("ln_rstd", TILES)
        cmax = sb("chunk_max", TPB * CHUNKS)[:, :].rearrange("p (t c) -> p t c", t=TPB)
        nmax = sb("neg_max", TPB)
        lpart = sb("piece_sums", TPB * PIECES)[:, :].rearrange("p (t c) -> p t c", t=TPB)
        lsum = sb("sums", TPB)
        linv = sb("inv_sums", TPB)
        oT = sb("cross_outT", DC * NTOK)[:, :].rearrange("p (c n) -> p c n", c=DC)
        hmax, hbias, hsum, hinv = [sb(name, len(UNITS) * HPC)[:, :].rearrange("p (u h) -> p u h", u=len(UNITS))
                                   for name in ("head_max", "head_bias", "head_sum", "head_inv")]
        pause, act_pause, pool_pause = sb("pause", 1), sb("act_pause", 1), sb("pool_pause", PAIRS)
        lo = sb("logits", TILES * E)[:, :].rearrange("p (t e) -> p t e", t=TILES)
        above_f, ties_f, cmp23_f = cut(region_w[:, 4 * MAT - 2048:4 * MAT], [TILES * E * E] * 2 + [SLOT_TILES * (E - 1)])
        above = above_f.rearrange("p (t e f) -> p t e f", t=TILES, e=E)
        ties = ties_f.rearrange("p (t e f) -> p t e f", t=TILES, e=E)
        lower_i = sb("lower_i", E * E)[:, :].rearrange("p (e f) -> p e f", e=E)
        place = sb("place", TILES * E)[:, :].rearrange("p (t e) -> p t e", t=TILES)
        chosen = sb("chosen", TILES * E)[:, :].rearrange("p (t e) -> p t e", t=TILES)
        nth = [sb(f"choice{n}", TILES * E)[:, :].rearrange("p (t e) -> p t e", t=TILES) for n in range(TOPK)]
        lmax = sb("logit_max", TILES)
        ex = sb("gate_exp", TILES * E)[:, :].rearrange("p (t e) -> p t e", t=TILES)
        gsum = sb("gate_sum", TILES)
        ginv = sb("gate_inv", TILES)
        picked = [sb(f"picked{n}", TILES * E)[:, :].rearrange("p (t e) -> p t e", t=TILES) for n in range(TOPK)]
        psel = [sb(f"prob{n}", TILES) for n in range(TOPK)]
        way = [sb(f"way{n}", 2) for n in range(2)]
        weight = [sb(f"weight{n}", 1) for n in range(2)]
        target = [sb(f"target{n}", 1, I32) for n in range(2)]
        slotf = [sb(f"slotf{n}", TILES) for n in range(TOPK)]
        slot = [sb(f"slot{n}", TILES, I32) for n in range(TOPK)]
        before = sb("chosen_before", TILES * E)[:, :].rearrange("p (t e) -> p t e", t=TILES)
        pos = sb("positions", TILES * E)[:, :].rearrange("p (t e) -> p t e", t=TILES)
        csum = sb("chosen_sums", E)
        steps = sb("steps", E)
        need = sb("tiles_needed", E)
        first = sb("first_tile", E)
        tileno = sb("tile_numbers", SLOT_TILES)
        owner_f = sb("owner_f", SLOT_TILES)
        owner = sb("owner", SLOT_TILES, I32)
        cmp23 = cmp23_f.rearrange("p (j e) -> p j e", j=SLOT_TILES)

        psum = stack.enter_context(nc.psum_tensor("psum", [P, 8 * BANK], F32))
        bank = [psum[:, n * BANK:(n + 1) * BANK] for n in range(8)]

        consts = sem("consts")
        pool_step = sem("pool_step")
        x_loaded = [sem(f"x_loaded{s}") for s in range(DUOS)]
        b1_loaded, b2_loaded = sem("b1_loaded"), sem("b2_loaded")
        w1_loaded, w2_loaded, small_loaded, biases_loaded = sem("w1_loaded"), sem("w2_loaded"), sem("small_loaded"), sem("biases_loaded")
        zero_stored = sem("zero_stored")
        ctx_loaded = [[sem(f"ctx_loaded{n}_{q}") for q in range(4)] for n in range(2)]
        w_loaded = [sem(f"w_loaded{n}") for n in range(2)]
        w_stored = [sem(f"w_stored{n}") for n in range(2)]
        dve_step = sem("dve_step")
        var_ready, sd_ready, xn_ready = sem("var_ready"), sem("sd_ready"), sem("xn_ready")
        setup_done, setup_act, setup_dve = sem("setup_done"), sem("setup_act"), sem("setup_dve")
        b1_scaled = sem("b1_scaled")
        queries_high, queries_ready = sem("queries_high"), sem("queries_ready")
        ctx_turned, ctxT_high, ctxT_ready = sem("ctx_turned"), sem("ctxT_high"), sem("ctxT_ready")
        val_high, val_ready = [sem("values_high_even"), sem("values_high_odd")], sem("values_ready")
        scores_done, scores_out = sem("scores_done"), sem("scores_out")
        max_ready, exp_done = sem("max_ready"), sem("exp_done")
        probs_turned, probsT_high, probsT_ready = sem("probs_turned"), sem("probsT_high"), sem("probsT_ready")
        pv_done = sem("pv_done")
        w_turned, w_out, waiting_out = sem("w_turned"), sem("w_out"), sem("waiting_out")
        oT_ready = sem("oT_ready")
        fused_done, x1_ready = sem("fused_done"), sem("x1_ready")
        p2_done, proj_done, p2_act, p2_dve = sem("p2_done"), sem("proj_done"), sem("p2_act"), sem("p2_dve")
        zeroed = sem("zeroed")
        q_ready, v_ready = sem("q_ready"), sem("v_ready")
        local_done, row_max, bias_ready, local_exp = sem("local_done"), sem("row_max"), sem("bias_ready"), sem("local_exp")
        inv_ready, normed = sem("inv_ready"), sem("normed")
        local_turned, localT_ready, localpv_done = sem("local_turned"), sem("localT_ready"), sem("localpv_done")
        heads_ready = sem("heads_ready")
        p2c_done = sem("p2c_done")
        p3_done, p3_act = sem("p3_done"), sem("p3_act")
        lm_ready, gate_exp = sem("lm_ready"), sem("gate_exp_done")
        chosen_ready, counts_done, ranks_done = sem("chosen_ready"), sem("counts_done"), sem("ranks_done")
        sums_ready = sem("sums_ready")
        rows_ready, probs_written = sem("rows_ready"), sem("probs_written")
        slots_ready, owner_ready = sem("slots_ready"), sem("owner_ready")
        scattered = [sem(f"scattered{n}") for n in range(TOPK)]
        up_loaded = [sem(f"up_loaded{n}") for n in range(2)]
        down_loaded = [sem(f"down_loaded{n}") for n in range(2)]
        xg_loaded = [sem(f"xg_loaded{n}") for n in range(2)]
        xg_turned, xgT_high, xgT_ready = sem("xg_turned"), sem("xgT_high"), sem("xgT_ready")
        high_ready, low_ready = sem("high_ready"), sem("low_ready")
        g_done, u_done = sem("g_done"), sem("u_done")
        silu_ready, hid_ready = sem("silu_ready"), sem("hid_ready")
        hid_turned, hidT_ready = sem("hid_turned"), sem("hidT_ready")
        y_done, y_ready = sem("y_done"), sem("y_ready")
        y_stored = [sem(f"y_stored{n}") for n in range(2)]
        y_loaded = [sem(f"y_loaded{n}") for n in range(TILES)]
        paused = sem("paused")
        out_ready, out_stored = sem("out_ready"), sem("out_stored")

        rooms = [w_turned, pv_done, scores_done, local_done, localpv_done, probs_turned, *w_stored, local_turned,
                 probsT_ready, scores_out, w_out, x1_ready, row_max, localT_ready, heads_ready]

        small = [(w1_nat.rearrange("p (c n) -> p c n", c=DC), w1_w.rearrange("(c p) n -> p c n", p=P)),
                 (w2_nat.rearrange("p (c n) -> p c n", c=DC), w2_w.rearrange("(c p) n -> p c n", p=P)),
                 (q_nat.rearrange("p (c n) -> p c n", c=DC), q_w.rearrange("(c p) n -> p c n", p=P)),
                 (k_nat.rearrange("p (c n) -> p c n", c=DC), k_w.rearrange("(c p) n -> p c n", p=P)),
                 (v_nat.rearrange("p (c n) -> p c n", c=DC), v_w.rearrange("(c p) n -> p c n", p=P)),
                 (o_nat.rearrange("p (c n) -> p c n", c=DC), o_w.rearrange("(c p) n -> p c n", p=P))]
        biases = [(vbr[:, :], v_b.rearrange("(a n) -> a n", a=1).broadcast_to([P, D])),
                  (obr[:, :], o_b.rearrange("(a n) -> a n", a=1).broadcast_to([P, D]))]
        for c in range(DC):
            biases.append((gwT[:, c, :], gate_w[:, c * P:(c + 1) * P].rearrange("e p -> p e")))
        biases += [(cols[:, :], b.rearrange("(c p) -> p c", p=P)) for cols, b in ((qbc, q_b), (kbc, k_b))]
        N_CONST = 12

        block = stack.enter_context(nc.Block())

        @block.sync
        def _(sp):
            for s in range(DUOS):
                sp.dma_start(xr[:, 2 * s:2 * s + 2, :], x.rearrange("b (t p) d -> p (b t) d", p=P)[:, 2 * s:2 * s + 2, :]).then_inc(x_loaded[s], 16)
            small.insert(1, (b1c[:, :], w1_b.rearrange("(c p) -> p c", p=P)))
            small.insert(3, (b2r[:, :], w2_b.rearrange("(a n) -> a n", a=1).broadcast_to([P, D])))
            with nc.allow_non_contiguous_dma(reason="a small column, once"):
                for (dst, src), loaded in zip(small, [w1_loaded, b1_loaded, w2_loaded, b2_loaded] + [small_loaded] * (len(small) - 4)):
                    sp.dma_start(dst, src).then_inc(loaded, 16)

            def load_ctx(b, n, quarters):
                src = ctx[bass.ds(b, 1)].rearrange("a (p t) d -> p (a t) d", p=P)
                for q in quarters:
                    t = slice(q * KT // 4, (q + 1) * KT // 4)
                    sp.dma_start(ctx_sb[n][:, t, :], src[:, t, :]).then_inc(ctx_loaded[n][q], 16)

            def load_piece(b, k):
                e = b * EPB + k // NMAT
                m = k % NMAT
                if m < 2:
                    src = (wg, wu)[m][bass.ds(e, 1)].rearrange("a (c p) n -> p (a c) n", p=P)
                    dst = w_nat[k % 2].rearrange("p (c n) -> p c n", c=IC)
                else:
                    src = wd[bass.ds(e, 1)].rearrange("a (c p) n -> p (a c) n", p=P)
                    dst = w_nat[k % 2].rearrange("p (c n) -> p c n", c=DC)
                sp.dma_start(dst, src).then_inc(w_loaded[k % 2], 16)

            def store_piece(b, k):
                e = b * EPB + k // NMAT
                m = k % NMAT
                if k == WAITING:
                    sp.wait_ge(waiting_out, b * MATGROUPS + MATGROUPS)
                else:
                    sp.wait_ge(w_out, b * GPB_ACT + (k + 1 - (k > WAITING)) * MATGROUPS + FIRST)
                sp.dma_start(wt_dram[bass.ds(e, 1), :, m * MAT:(m + 1) * MAT].rearrange("a p n -> p (a n)"),
                             w_turn[k % 2]).then_inc(w_stored[k % 2], 16)

            load_ctx(0, 0, range(4))
            load_piece(0, 0)
            load_piece(0, 1)
            with nc.allow_non_contiguous_dma(reason="a few small columns, once"):
                for dst, src in biases:
                    sp.dma_start(dst, src).then_inc(biases_loaded, 16)

            def two_batches(i, more):
                for n in range(2):
                    b = i * 2 + n
                    for k in range(PPB):
                        store_piece(b, k)
                        if k + 2 < PPB:
                            load_piece(b, k + 2)
                        elif n == 0 or more:
                            load_piece(b + 1, k + 2 - PPB)
                        if k < 4 and (n == 0 or more):
                            if k == 0:
                                sp.wait_ge(pv_done, b * PAIRS + FIRST)
                            load_ctx(b + 1, 1 - n, [k])

            with sp.Fori(0, BATCH // 2 - 1) as i:
                two_batches(i, True)
            two_batches(BATCH // 2 - 1, False)

            sp.wait_ge(owner_ready, 1)
            for n in range(2):
                sp.wait_ge(w_stored[n], 16 * E * NMAT // 2 + FIRST)

            def expert_rows(j):
                e = sp.value_load(owner[0:1, bass.ds(j, 1)], min_val=0, max_val=E - 1)
                return wt_dram[bass.ds(e, 1), :, :].rearrange("a p n -> p (a n)")

            def load_rows(j, n, waits):
                if waits:
                    sp.wait_ge(xgT_ready, j - 1)
                sp.dma_start(xg[n], xg_dram[bass.ds(j * P, P), :]).then_inc(xg_loaded[n], 16)

            def load_up(j, n, waits):
                rows = expert_rows(j)
                if waits:
                    sp.wait_ge(low_ready, (j - 1) * 4)
                sp.dma_start(w_up[n], rows[:, 0:2 * MAT]).then_inc(up_loaded[n], 16)

            def load_down(j, n, waits):
                rows = expert_rows(j)
                if waits:
                    sp.wait_ge(y_done, j - 1)
                sp.dma_start(w_down[n], rows[:, 2 * MAT:3 * MAT]).then_inc(down_loaded[n], 16)

            load_up(0, 0, False)
            for n in range(TOPK):
                sp.wait_ge(scattered[n], 16 * TILES)
            for n in range(2):
                load_rows(n, n, False)
            load_up(1, 1, False)
            for n in range(2):
                load_down(n, n, False)
            load_rows(2, 0, True)
            load_up(2, 0, True)
            load_rows(3, 1, True)
            load_up(3, 1, True)
            load_down(2, 0, True)
            with sp.Fori(4, SLOT_TILES - 1, 2) as j2:
                load_rows(j2, 0, True)
                load_up(j2, 0, True)
                load_down(j2 - 1, 1, True)
                load_rows(j2 + 1, 1, True)
                load_up(j2 + 1, 1, True)
                load_down(j2, 0, True)
            load_rows(SLOT_TILES - 1, 0, True)
            load_up(SLOT_TILES - 1, 0, True)
            load_down(SLOT_TILES - 2, 1, True)
            load_down(SLOT_TILES - 1, 0, True)

            for n in range(2):
                sp.wait_ge(y_stored[n], 16 * ((SLOT_TILES + 1 - n) // 2))
            for t in range(TILES):
                sp.dma_start(y_of[:, t].rearrange("p k d -> p (k d)"),
                             y_dram[t * P * TOPK:(t + 1) * P * TOPK, :].rearrange("(p k) d -> p (k d)", k=TOPK)).then_inc(y_loaded[t], 16)
            for t in range(TILES):
                sp.wait_ge(out_ready, t + 1)
                sp.dma_start(out.rearrange("b (t p) d -> p (b t) d", p=P)[:, t, :], x3n[:, t, :]).then_inc(out_stored, 16)
            sp.wait_ge(out_stored, 16 * TILES)

        @block.gpsimd
        def _(pool):
            for room in rooms:
                pool.sem_inc(room, FIRST)
            nc.gpsimd.memset(zeros, 0.0).then_inc(consts, 1)
            nc.gpsimd.iota(no_row[:, D + 1:ROW], pattern=[[0, 1]], base=RESULTS, channel_multiplier=1,
                           allow_small_or_imprecise_dtypes=True).then_inc(consts, 1)
            nc.gpsimd.memset(eps_c[:, :], EPS).then_inc(consts, 1)
            nc.gpsimd.memset(ones[:, :], 1.0).then_inc(consts, 1)
            nc.gpsimd.memset(ident[:, :], 0.0).then_inc(pool_step, 1)
            nc.gpsimd.memset(mask[0][:, :], 0.0).then_inc(pool_step, 1)
            nc.gpsimd.memset(mask[1][:, :], 0.0).then_inc(pool_step, 1)
            nc.gpsimd.memset(head_rows[:, :], 1.0).then_inc(pool_step, 1)
            nc.gpsimd.memset(lower_i, 1.0).then_inc(pool_step, 1)
            pool.wait_ge(pool_step, 5)
            nc.gpsimd.affine_select(out=ident[:, :], in_=ident[:, :], compare_op=ALU.not_equal, fill=1.0, base=0,
                                    pattern=[[-1, P]], channel_multiplier=1).then_inc(consts, 1)
            nc.gpsimd.affine_select(out=earlier[:, :], in_=ones[:, :], compare_op=ALU.is_gt, fill=0.0, base=0,
                                    pattern=[[1, P]], channel_multiplier=-1).then_inc(consts, 1)
            nc.gpsimd.affine_select(out=lower_i, in_=lower_i, compare_op=ALU.is_gt, fill=0.0, base=0,
                                    pattern=[[1, E], [-1, E]], channel_multiplier=0).then_inc(consts, 1)
            nc.gpsimd.iota(steps[:, :], pattern=[[P, E]], base=0, channel_multiplier=0,
                           allow_small_or_imprecise_dtypes=True).then_inc(consts, 1)
            nc.gpsimd.iota(tileno[:, :], pattern=[[1, SLOT_TILES]], base=0, channel_multiplier=0,
                           allow_small_or_imprecise_dtypes=True).then_inc(consts, 1)
            for t in range(TPB):
                nc.gpsimd.affine_select(out=mask[t][:, :], in_=mask[t][:, :], compare_op=ALU.is_ge, fill=MASKED, base=t * P - KEY0[t],
                                        pattern=[[-1, SEEN[t]]], channel_multiplier=1).then_inc(pool_step, 1)
            nc.gpsimd.affine_select(out=head_rows[:, :], in_=head_rows[:, :], compare_op=ALU.is_ge, fill=0.0, base=0,
                                    pattern=[[-DH, HPC]], channel_multiplier=1).then_inc(pool_step, 1)
            pool.wait_ge(pool_step, 8)
            for t in range(TPB):
                nc.gpsimd.affine_select(out=mask[t][:, :], in_=mask[t][:, :], compare_op=ALU.is_ge, fill=MASKED, base=WIN - t * P + KEY0[t],
                                        pattern=[[1, SEEN[t]]], channel_multiplier=-1).then_inc(consts, 1)
            nc.gpsimd.affine_select(out=head_rows[:, :], in_=head_rows[:, :], compare_op=ALU.is_ge, fill=0.0, base=DH - 1,
                                    pattern=[[DH, HPC]], channel_multiplier=-1).then_inc(consts, 1)
            pool.wait_ge(consts, N_CONST)
            pool.wait_ge(setup_act, 11)
            with pool.Fori(0, BATCH // 2) as i:
                for n in range(2):
                    b = i * 2 + n
                    if n == 0:
                        pool.wait_ge(scores_done, i * (2 * TPB * CHUNKS) + FIRST)
                        for m in range(2):
                            nc.gpsimd.tensor_copy(bf_hi[:, m], bfT[:, :, bass.ds(i * (2 * NTOK) + m * NTOK, NTOK)]).then_inc(queries_high, 1)
                    for g in range(0, PAIRS, 2):
                        if g == 0:
                            pool.wait_ge(scores_done, b * (TPB * CHUNKS) + TPB * CHUNKS + FIRST)
                            for q in range(4):
                                pool.wait_ge(ctx_loaded[n][q], i * 16 + 16)
                        elif g >= 4:
                            pool.wait_ge(pv_done, b * PAIRS + g - 3 + FIRST)
                        if g == 0 or g >= 4:
                            nc.gpsimd.tensor_tensor(pool_pause[:, g:g + 1], zeros[:, 0:1], zeros[:, 0:1], ALU.add)
                        nc.gpsimd.tensor_copy(val_hi[:, g % 4], ctx_sb[n][:, g * PAIR:(g + 1) * PAIR, :]).then_inc(val_high[0], 1)

            pool.wait_ge(pv_done, BATCH * PAIRS + FIRST)
            pool.wait_ge(w_turned, BATCH * GPB + FIRST)
            for n in range(2):
                pool.wait_ge(w_stored[n], 16 * E * NMAT // 2 + FIRST)
            nc.gpsimd.memset(v_own_f, 0.0).then_inc(zeroed, 1)
            for hc in range(DC):
                nc.gpsimd.memset(local[DC + hc][:, :, 0:KEY0[1]], 0.0).then_inc(zeroed, 1)
            pool.dma_start(xg_dram.rearrange("(t p) d -> p t d", p=P),
                           no_row[:, :].rearrange("p (a d) -> p a d", a=1).broadcast_to([P, SLOT_TILES, ROW])).then_inc(zero_stored, 16)
            pool.wait_ge(p2_act, 4 + DC)

            def local_queries(b, u):
                t, hc = UNITS[u]
                src = qT[:, hc, bass.ds(b * NTOK + t * P, P)].rearrange("p (a n) -> p a n", a=1).broadcast_to([P, HPC, P])
                own = head_rows[:, :].rearrange("p (h a) -> p h a", a=1).broadcast_to([P, HPC, P])
                nc.gpsimd.tensor_tensor(q_own[u % 2], src, own, ALU.mult).then_inc(q_ready, 1)

            def local_norm(b, u):
                t = UNITS[u][0]
                pool.wait_ge(inv_ready, b * len(UNITS) + u + 1)
                part = local[u][:, :, KEY0[t]:KEY0[t] + SEEN[t]]
                nc.gpsimd.tensor_tensor(part, part, hinv[:, u, :].rearrange("p (h a) -> p h a", a=1).broadcast_to([P, HPC, SEEN[t]]),
                                        ALU.mult).then_inc(normed, 1)

            def local_batch(b, more):
                for u in range(len(UNITS)):
                    if u < 3 or more:
                        local_norm(b if u < 3 else b + 1, (u + 1) % 4)
                    if u < 1 or more:
                        pool.wait_ge(local_done, b * len(UNITS) + u + 2 + FIRST)
                        local_queries(b if u < 1 else b + 1, (u + 3) % 4)

            local_queries(0, 0)
            local_queries(0, 1)
            local_norm(0, 0)
            pool.wait_ge(local_done, 1 + FIRST)
            local_queries(0, 2)
            pool.wait_ge(p2_act, 4 + 3 * DC)
            with pool.Fori(0, BATCH - 1) as b:
                local_batch(b, True)
            local_batch(BATCH - 1, False)

            pool.wait_ge(localpv_done, BATCH * len(UNITS) + FIRST)
            for n in range(TOPK):
                nc.gpsimd.iota(rows[n][:, :, D + 1], pattern=[[P * TOPK, TILES]], base=n, channel_multiplier=TOPK,
                               allow_small_or_imprecise_dtypes=True).then_inc(rows_ready, 1)
            pool.wait_ge(rows_ready, TOPK + 2)
            pool.wait_ge(probs_written, TOPK)
            pool.wait_ge(zero_stored, 16)
            for n in range(TOPK):
                pool.wait_ge(slots_ready, n + 1)
                for t in range(TILES):
                    pool.indirect_dma_start(
                        out=xg_dram, out_offset=bass.IndirectOffsetOnAxis(ap=slot[n][:, t:t + 1], axis=0),
                        in_=rows[n][:, t, :], in_offset=None).then_inc(scattered[n], 16)

            def store_results(j, n, before):
                pool.wait_ge(y_ready, j + 1)
                if before is not None:
                    pool.wait_ge(y_stored[1 - n], before)
                if j is not 0:
                    pool.wait_ge(paused, j)
                nc.gpsimd.tensor_tensor(pool_pause[:, 0:1], zeros[:, 0:1], zeros[:, 0:1], ALU.add).then_inc(paused, 1)
                pool.indirect_dma_start(
                    out=y_dram, out_offset=bass.IndirectOffsetOnAxis(ap=target[n][:, :], axis=0),
                    in_=yt[n], in_offset=None).then_inc(y_stored[n], 16)

            store_results(0, 0, None)
            store_results(1, 1, 16)
            with pool.Fori(2, SLOT_TILES - 1, 2) as j2:
                for n in range(2):
                    store_results(j2 + n, n, j2 * 8 + n * 16)
            store_results(SLOT_TILES - 1, 0, SLOT_TILES // 2 * 16)

        @block.scalar
        def _(act):
            def deviation(k, s):
                two = slice(2 * s, 2 * s + 2)
                act.wait_ge(var_ready, k * DUOS + s + 1)
                nc.scalar.activation(sd[:, two], mv[:, two, 1], ACT.Sqrt, bias=eps_c[:, :]).then_inc(sd_ready, 1)

            def turned_norm(k, dst, banks, done, at, out):
                deviation(k, 0)
                for s in range(DUOS):
                    if s + 1 < DUOS:
                        deviation(k, s + 1)
                    act.wait_ge(done, at + s)
                    copy(dst[:, :, 2 * s * P:(2 * s + 2) * P], bank[banks[s]].rearrange("p (c n) -> p c n", c=DC)).then_inc(out, 1)

            def copy(dst, src):
                return nc.scalar.activation(dst, src, ACT.Copy)

            act.wait_ge(consts, N_CONST)
            nc.scalar.activation(act_pause[:, :], zeros[:, 0:1], ACT.Sqrt)
            turned_norm(0, xnT, range(3, 7), setup_done, 1, setup_act)
            for s, dst in enumerate((w1T, w2T[:, 0:DC, :], w2T[:, DC:2 * DC, :])):
                act.wait_ge(setup_done, DUOS + s + 1)
                copy(dst, bank[s].rearrange("p (c n) -> p c n", c=DC)).then_inc(setup_act, 1)
            act.wait_ge(b1_loaded, 16)
            nc.scalar.activation(b1c[:, :], b1c[:, :], ACT.Copy, scale=float(D) ** -0.5).then_inc(b1_scaled, 1)
            act.wait_ge(b1_scaled, 1)
            for s in range(4):
                act.wait_ge(setup_done, 8 + s)
                kc, half = s // 2, s % 2
                nc.scalar.activation(bfT[:, kc, half * BANK:(half + 1) * BANK], bank[(2, 7, 0, 1)[s]], ACT.Identity,
                                     bias=b1c[:, kc:kc + 1], scale=float(D) ** -0.5).then_inc(setup_act, 1)
            for s, dst in enumerate((qwT, kwT, vwT, owT)):
                act.wait_ge(setup_done, 16 + s)
                copy(dst, bank[(2, 7, 3, 4)[s]].rearrange("p (c n) -> p c n", c=DC)).then_inc(setup_act, 1)

            nc.scalar.activation(act_pause[:, :], zeros[:, 0:1], ACT.Exp)
            with act.Fori(0, BATCH // 2) as i:
                for n in range(2):
                    b = i * 2 + n

                    def expert_out(g):
                        k = g // MATGROUPS
                        if g % MATGROUPS == 0:
                            act.wait_ge(w_stored[k % 2], b * (16 * PPB // 2) + 16 * (k // 2) + FIRST)
                        act.wait_ge(w_turned, b * GPB + g + 1 + FIRST)
                        copy(w_turn[k % 2][:, (g % MATGROUPS) * BANK:(g % MATGROUPS + 1) * BANK], bank[4 + g % 2]).then_inc(w_out, 1)

                    def ctx_out(ch):
                        for c in range(DC):
                            act.wait_ge(ctx_turned, b * (CHUNKS * DC) + (ch * DC + c + 1))
                            if c == 0 and ch < 2:
                                act.wait_ge(pv_done, b * PAIRS + FIRST)
                            elif c == 0:
                                act.wait_ge(scores_done, b * (CHUNKS * TPB) + (ch - 1) * TPB + FIRST)
                            copy(ctxT_hi[:, ch % 2, c, :], bank[c]).then_inc(ctxT_high, 1)

                    def probs(k):
                        for t in range(TPB):
                            part = scores[t][:, k * (KEYS // PIECES):(k + 1) * (KEYS // PIECES)]
                            nc.scalar.activation(part, part, ACT.Exp, bias=nmax[:, t:t + 1],
                                                 accum_out=lpart[:, t, k:k + 1]).then_inc(exp_done, 1)

                    def values_high(g):
                        if g >= 4:
                            act.wait_ge(pv_done, b * PAIRS + g - 3 + FIRST)
                        copy(val_hi[:, g % 4], ctx_sb[n][:, g * PAIR:(g + 1) * PAIR, :]).then_inc(val_high[1], 1)

                    ctx_out(0)
                    for ch in range(CHUNKS):
                        for g in range(BESIDE * ch, BESIDE * (ch + 1)):
                            expert_out(g)
                        if ch + 1 < CHUNKS:
                            ctx_out(ch + 1)
                    act.wait_ge(max_ready, b * TPB + TPB)
                    act.wait_ge(x1_ready, b + FIRST)
                    probs(0)
                    values_high(1)
                    for g in range(PAIRS):
                        act.wait_ge(probs_turned, b * PAIRS + g + 1 + FIRST)
                        act.wait_ge(pv_done, b * PAIRS + max(g - 1, 0) + FIRST)
                        copy(pT_hi[:, g % 2], bank[g % 2].rearrange("p (k n) -> p k n", k=PAIR)).then_inc(probsT_high, 1)
                        if g % 2 == 0 and g // 2 + 1 < PIECES:
                            probs(g // 2 + 1)
                        elif g % 2 == 1 and g + 2 < PAIRS:
                            values_high(g + 2)
                    for g in range(BESIDE * CHUNKS + MATGROUPS, GPB):
                        expert_out(g)

            turned_norm(1, x2nT, range(DUOS), p2_done, 1, p2_act)
            act.wait_ge(biases_loaded, 16 * len(biases))
            for s in range(4 * DC):
                act.wait_ge(proj_done, s + 1)
                half, (dst, bias), c = s // (2 * DC), ((qT, qbc), (kT, kbc))[s // DC % 2], s % DC
                nc.scalar.activation(dst[:, c, half * BANK:(half + 1) * BANK], bank[(4 + s) % 8], ACT.Identity,
                                     bias=bias[:, c:c + 1]).then_inc(p2_act, 1)

            def local_softmax(b, u):
                t = UNITS[u][0]
                act.wait_ge(bias_ready, b * len(UNITS) + u + 1)
                for h in range(HPC):
                    part = local[u][:, h, KEY0[t]:KEY0[t] + SEEN[t]]
                    last = nc.scalar.activation(part, part, ACT.Exp, bias=hbias[:, u, h:h + 1], scale=float(DH) ** -0.5,
                                                accum_out=hsum[:, u, h:h + 1])
                last.then_inc(local_exp, 1)

            def local_batch(b, more):
                for u in range(len(UNITS)):
                    if u < 2 or more:
                        local_softmax(b if u < 2 else b + 1, (u + 2) % 4)

            local_softmax(0, 0)
            local_softmax(0, 1)
            with act.Fori(0, BATCH - 1) as b:
                local_batch(b, True)
            local_batch(BATCH - 1, False)

            turned_norm(2, x3nT, range(DUOS), p3_done, 1, p3_act)
            for half in range(2):
                t = slice(half * TPG, (half + 1) * TPG)
                copy(rows[1][:, t, 0:D], x3n[:, t, :]).then_inc(rows_ready, 1)
            act.wait_ge(lm_ready, 1)
            nc.scalar.activation(ex, ex, ACT.Exp).then_inc(gate_exp, 1)
            nc.scalar.activation(act_pause[:, :], zeros[:, 0:1], ACT.Silu)

            def group_of(n, g):
                return w_up[n].rearrange("p (m c n) -> p m c n", m=2, c=DC)[:, g // 2, :, g % 2 * BANK:(g % 2 + 1) * BANK]

            def high(n, g):
                copy(w_hi[:, g % 3], group_of(n, g)).then_inc(high_ready, 1)

            def tile_step(j, n, first=False, last=False):
                act.wait_ge(g_done, j * 2 + 1)
                high(n, 3)
                if not first:
                    act.wait_ge(hid_ready, j)
                nc.scalar.activation(silu[n][:, 0:BANK], bank[0], ACT.Silu).then_inc(silu_ready, 1)
                act.wait_ge(g_done, j * 2 + 2)
                nc.scalar.activation(silu[n][:, BANK:INNER], bank[1], ACT.Silu).then_inc(silu_ready, 1)
                if not first:
                    tile_hidT(j - 1, 1 - n)
                if not last:
                    act.wait_ge(up_loaded[1 - n], (j + 1 + n) * 8 + 8 if n else (j + 2) * 8)
                    act.wait_ge(u_done, j * 2 + 2)
                    for g in range(3):
                        high(1 - n, g)

            def tile_hidT(j, n):
                for half in range(2):
                    act.wait_ge(hid_turned, j * 2 + half + 1)
                    copy(hidT[n][:, half * BANK:(half + 1) * BANK], bank[4 + half]).then_inc(hidT_ready, 1)

            act.wait_ge(up_loaded[0], 16)
            for g in range(3):
                high(0, g)
            tile_step(0, 0, first=True)
            with act.Fori(1, SLOT_TILES - 2, 2) as j2:
                tile_step(j2, 1)
                tile_step(j2 + 1, 0)
            tile_step(SLOT_TILES - 2, 1)
            tile_step(SLOT_TILES - 1, 0, last=True)
            tile_hidT(SLOT_TILES - 1, 0)

        @block.vector
        def _(dve):
            step = [0]

            def then(ins):
                step[0] += 1
                ins.then_inc(dve_step, 1)
                dve.wait_ge(dve_step, step[0])

            def statistics(k, s):
                two = range(2 * s, 2 * s + 2)
                for t in two:
                    last = nc.vector.bn_stats(bn[:, t, :], xr[:, t, :])
                then(last)
                for t in two:
                    last = nc.vector.bn_aggr(mv[:, t, :], bn[:, t, :])
                last.then_inc(var_ready, 1)

            def normalise(k, s, dst):
                two = slice(2 * s, 2 * s + 2)
                dve.wait_ge(sd_ready, k * DUOS + s + 1)
                then(nc.vector.reciprocal(rstd[:, two], sd[:, two]))
                for t in range(2 * s, 2 * s + 2):
                    nc.vector.tensor_scalar(dst[:, t, :], xr[:, t, :], mv[:, t, 0:1], rstd[:, t:t + 1],
                                            ALU.subtract, ALU.mult).then_inc(xn_ready, 1)

            def layer_norm(k, dst, before):
                for s in range(DUOS):
                    before(s)
                    statistics(k, s)
                    if s > 0:
                        normalise(k, s - 1, dst)
                normalise(k, DUOS - 1, dst)

            layer_norm(0, xn, lambda s: dve.wait_ge(x_loaded[s], 16))
            for s in range(4):
                dve.wait_ge(setup_done, 12 + s)
                part = xr[:, 2 * s:2 * s + 2, :]
                then(nc.vector.tensor_tensor(part, part, bank[3 + s].rearrange("p (t d) -> p t d", t=2), ALU.add))
                if s == 0:
                    dve.wait_ge(b2_loaded, 16)
                nc.vector.tensor_tensor(part, part, b2r[:, :].rearrange("p (a d) -> p a d", a=1).broadcast_to([P, 2, D]),
                                        ALU.add).then_inc(setup_dve, 1)

            step_at = step[0]
            PER = 2
            with dve.Fori(0, BATCH // 2) as i:
                for n in range(2):
                    b = i * 2 + n

                    def then_b(ins, k):
                        ins.then_inc(dve_step, 1)
                        dve.wait_ge(dve_step, b * PER + (step_at + k))

                    def ctx_low(ch):
                        for c in range(DC):
                            dve.wait_ge(ctxT_high, b * (CHUNKS * DC) + (ch * DC + c + 1))
                            nc.vector.tensor_tensor(ctxT_lo[:, ch % 2, c, :], bank[c], ctxT_hi[:, ch % 2, c, :].bitcast(F32),
                                                    ALU.subtract).then_inc(ctxT_ready, 1)

                    dve.wait_ge(probs_turned, b * PAIRS + FIRST)
                    ctx_low(0)
                    if n == 0:
                        for m in range(2):
                            dve.wait_ge(queries_high, i * 2 + m + 1)
                            nc.vector.tensor_tensor(bf_lo[:, m], bfT[:, :, bass.ds(i * (2 * NTOK) + m * NTOK, NTOK)],
                                                    bf_hi[:, m].bitcast(F32), ALU.subtract).then_inc(queries_ready, 1)
                    for ch in range(CHUNKS):
                        if ch + 1 < CHUNKS:
                            ctx_low(ch + 1)
                        for t in range(TPB):
                            dve.wait_ge(scores_done, b * (CHUNKS * TPB) + (ch * TPB + t + 1) + FIRST)
                            nc.vector.tensor_scalar(scores[t][:, ch * BANK:(ch + 1) * BANK], bank[2 + t], 1.0, LOWEST, ALU.mult, ALU.max,
                                                    accum_out=cmax[:, t, ch:ch + 1]).then_inc(scores_out, 1)
                    dve.wait_ge(scores_out, b * (CHUNKS * TPB) + CHUNKS * TPB + FIRST)
                    for t in range(TPB):
                        nc.vector.tensor_reduce(nmax[:, t:t + 1], cmax[:, t, :], axis=X_AXIS, op=ALU.max, negate=True).then_inc(max_ready, 1)

                    def waiting_piece(g):
                        if g == 0:
                            dve.wait_ge(w_stored[WAITING % 2], b * (16 * PPB // 2) + 16 * (WAITING // 2) + FIRST)
                        at = WAITING * MATGROUPS + g
                        dve.wait_ge(w_turned, b * GPB + at + 1 + FIRST)
                        nc.vector.tensor_copy(w_turn[WAITING % 2][:, g * BANK:(g + 1) * BANK], bank[4 + at % 2]).then_inc(waiting_out, 1)

                    def values_low(g):
                        dve.wait_ge(val_high[g % 2], b * (PAIRS // 2) + g // 2 + 1)
                        nc.vector.tensor_tensor(val_lo[:, g % 4], ctx_sb[n][:, g * PAIR:(g + 1) * PAIR, :], val_hi[:, g % 4].bitcast(F32),
                                                ALU.subtract).then_inc(val_ready, 1)

                    def probs_low(g):
                        dve.wait_ge(probsT_high, b * PAIRS + g + 1)
                        nc.vector.tensor_tensor(pT_lo[:, g % 2], bank[g % 2].rearrange("p (k n) -> p k n", k=PAIR), pT_hi[:, g % 2].bitcast(F32),
                                                ALU.subtract).then_inc(probsT_ready, 1)

                    waiting_piece(0)
                    waiting_piece(1)
                    values_low(0)
                    waiting_piece(2)
                    waiting_piece(3)
                    for g in range(PAIRS):
                        probs_low(g)
                        if g == 0:
                            values_low(1)
                        if g + 2 < PAIRS:
                            values_low(g + 2)
                    dve.wait_ge(exp_done, b * (TPB * PIECES) + TPB * PIECES)
                    then_b(nc.vector.tensor_reduce(lsum[:, :], lpart, axis=X_AXIS, op=ALU.add), 1)
                    then_b(nc.vector.reciprocal(linv[:, :], lsum[:, :]), 2)
                    dve.wait_ge(pv_done, b * PAIRS + PAIRS + FIRST)
                    for c in range(DC):
                        last = nc.vector.tensor_copy(oT[:, c, :], bank[6 + c][:, 0:NTOK])
                    last.then_inc(oT_ready, 1)
                    dve.wait_ge(fused_done, b + 1)
                    for t in range(TPB):
                        part = xr[:, bass.ds(b * TPB + t, 1), :].rearrange("p a d -> p (a d)")
                        last = nc.vector.scalar_tensor_tensor(out=part, in0=bank[6][:, t * D:(t + 1) * D], scalar=linv[:, t:t + 1], in1=part,
                                                              op0=ALU.mult, op1=ALU.add)
                    last.then_inc(x1_ready, 1)
            step[0] += BATCH * PER

            dve.wait_ge(x1_ready, BATCH + FIRST)
            dve.wait_ge(probs_turned, BATCH * PAIRS + FIRST)
            layer_norm(1, x2n, lambda s: None)
            dve.wait_ge(xn_ready, 2 * TILES)
            dve.wait_ge(biases_loaded, 16 * len(biases))
            then(nc.vector.tensor_tensor(xr, xr, obr[:, :].rearrange("p (a d) -> p a d", a=1).broadcast_to([P, TILES, D]), ALU.add))
            def local_values(b):
                dve.wait_ge(localpv_done, b * len(UNITS) + FIRST)
                for t in range(TPB):
                    dst = v_own[:, t].rearrange("p c (h n) -> p (c h) n", h=HPC)[:, :, 0:DH]
                    last = nc.vector.tensor_copy(dst, v_tok[:, bass.ds(b * TPB + t, 1), :].rearrange("p a (h n) -> p (a h) n", n=DH))
                last.then_inc(v_ready, 1)

            def local_max(b, u):
                t = UNITS[u][0]
                dve.wait_ge(local_done, b * len(UNITS) + u + 1 + FIRST)
                wide = P if t == 0 else NTOK
                nc.vector.memset(pause[:, 0:1], 0.0)
                for h in range(HPC):
                    at = (u * HPC * P if t == 0 else 0) + h * wide
                    last = nc.vector.tensor_tensor_reduce(
                        out=local[u][:, h, KEY0[t]:KEY0[t] + SEEN[t]], in0=psum[:, at:at + SEEN[t]], in1=mask[t][:, :],
                        scale=1.0, scalar=LOWEST, op0=ALU.add, op1=ALU.max, accum_out=hmax[:, u, h:h + 1])
                last.then_inc(row_max, 1)
                dve.wait_ge(row_max, b * len(UNITS) + u + 1 + FIRST)
                nc.vector.tensor_scalar(hbias[:, u, :], hmax[:, u, :], -float(DH) ** -0.5, None, ALU.mult).then_inc(bias_ready, 1)

            def local_inv(b, u):
                dve.wait_ge(local_exp, b * len(UNITS) + u + 1)
                nc.vector.reciprocal(hinv[:, u, :], hsum[:, u, :]).then_inc(inv_ready, 1)

            def local_evict(b, u, groups):
                for g in groups:
                    at = GROUP0[u] + g
                    dve.wait_ge(local_turned, b * sum(GROUPS) + at + 1 + FIRST)
                    nc.vector.tensor_copy(pT[:, at % 4], bank[4 + at % 2].rearrange("p (k n) -> p k n", k=TPG)).then_inc(localT_ready, 1)

            def local_out(b, u):
                t, hc = UNITS[u]
                dve.wait_ge(localpv_done, b * len(UNITS) + u + 1 + FIRST)
                nc.vector.tensor_copy(headsT[:, hc, bass.ds(b * NTOK + t * P, P)], bank[6 + u % 2][:, 0:P]).then_inc(heads_ready, 1)

            def local_batch(b, more):
                for u in range(len(UNITS)):
                    local_evict(b, u, range(2))
                    if u < 3 or more:
                        local_inv(b if u < 3 else b + 1, (u + 1) % 4)
                    if u < 2 or more:
                        local_max(b if u < 2 else b + 1, (u + 2) % 4)
                    local_evict(b, u, range(2, GROUPS[u]))
                    local_out(b, u)
                if more:
                    local_values(b + 1)

            local_max(0, 0)
            local_max(0, 1)
            local_inv(0, 0)
            for s in range(4):
                dve.wait_ge(proj_done, 4 * DC + s + 1)
                nc.vector.tensor_tensor(v_tok[:, 2 * s:2 * s + 2, :], bank[(4 + 4 * DC + s) % 8].rearrange("p (t d) -> p t d", t=2),
                                        vbr[:, :].rearrange("p (a d) -> p a d", a=1).broadcast_to([P, 2, D]),
                                        ALU.add).then_inc(p2_dve, 1)
            dve.wait_ge(p2_dve, 4)
            dve.wait_ge(zeroed, 1 + DC)
            local_values(0)
            with dve.Fori(0, BATCH - 1) as b:
                local_batch(b, True)
            local_batch(BATCH - 1, False)
            def output(s):
                dve.wait_ge(p2c_done, s + 1)
                part = xr[:, 2 * s:2 * s + 2, :]
                then(nc.vector.tensor_tensor(part, part, bank[s].rearrange("p (t d) -> p t d", t=2), ALU.add))

            layer_norm(2, x3n, output)

            dve.wait_ge(p3_done, 5)
            then(nc.vector.tensor_copy(lo, bank[4][:, 0:TILES * E].rearrange("p (t e) -> p t e", t=TILES)))

            def over_e(col):
                return col.rearrange("p (t a) -> p t a", a=1).broadcast_to([P, TILES, E])

            then(nc.vector.tensor_reduce(lmax[:, :], lo, axis=X_AXIS, op=ALU.max))
            nc.vector.tensor_tensor(ex, lo, over_e(lmax[:, :]), ALU.subtract).then_inc(lm_ready, 1)
            other = lo.rearrange("p t (a f) -> p t a f", a=1).broadcast_to([P, TILES, E, E])
            own = lo.rearrange("p t (e a) -> p t e a", a=1).broadcast_to([P, TILES, E, E])
            nc.vector.tensor_tensor(above, other, own, ALU.is_gt)
            then(nc.vector.tensor_tensor(ties, other, own, ALU.is_equal))
            flat = "p t e f -> p t (e f)"
            low = lower_i.rearrange("p e f -> p (e f)").rearrange("p (a n) -> p a n", a=1).broadcast_to([P, TILES, E * E])
            then(nc.vector.tensor_tensor(ties.rearrange(flat), ties.rearrange(flat), low, ALU.mult))
            then(nc.vector.tensor_tensor(above.rearrange(flat), above.rearrange(flat), ties.rearrange(flat), ALU.add))
            then(nc.vector.tensor_reduce(place, above, axis=X_AXIS, op=ALU.add))
            nc.vector.tensor_scalar(chosen, place, float(TOPK) - 0.5, None, ALU.is_lt).then_inc(chosen_ready, 1)
            dve.wait_ge(chosen_ready, 1)
            by_tile = chosen.rearrange("p (a f) e -> p a e f", a=1).broadcast_to([P, TILES, E, TILES])
            tile_before = lower_i.rearrange("p t (a f) -> p t a f", a=1).broadcast_to([P, TILES, E, TILES])
            then(nc.vector.tensor_tensor(above, by_tile, tile_before, ALU.mult))
            nc.vector.tensor_reduce(before, above, axis=X_AXIS, op=ALU.add)
            nc.vector.tensor_reduce(csum[:, :], chosen.rearrange("p t e -> p e t"), axis=X_AXIS, op=ALU.add).then_inc(sums_ready, 1)
            for n in range(TOPK):
                nc.vector.tensor_scalar(nth[n], place, float(n), None, ALU.is_equal)
            dve.wait_ge(gate_exp, 1)
            then(nc.vector.tensor_tensor(ex, ex, chosen, ALU.mult))
            nc.vector.tensor_reduce(gsum[:, :], ex, axis=X_AXIS, op=ALU.add)
            nc.vector.tensor_tensor(picked[0], ex, nth[0], ALU.mult)
            then(nc.vector.tensor_tensor(picked[1], ex, nth[1], ALU.mult))
            nc.vector.reciprocal(ginv[:, :], gsum[:, :])
            nc.vector.tensor_reduce(psel[0][:, :], picked[0], axis=X_AXIS, op=ALU.add)
            then(nc.vector.tensor_reduce(psel[1][:, :], picked[1], axis=X_AXIS, op=ALU.add))
            for n in range(TOPK):
                nc.vector.tensor_tensor(rows[n][:, :, D], psel[n][:, :], ginv[:, :], ALU.mult).then_inc(probs_written, 1)
            dve.wait_ge(counts_done, 1)
            then(nc.vector.tensor_tensor(ties[:, 0], bank[6][:, 0:E].rearrange("p (e a) -> p e a", a=1).broadcast_to([P, E, E]),
                                         steps[:, :].rearrange("p (a k) -> p a k", a=1).broadcast_to([P, E, E]), ALU.is_gt))
            then(nc.vector.tensor_reduce(need[:, :], ties[:, 0], axis=X_AXIS, op=ALU.add))
            then(nc.vector.tensor_tensor(ties[:, 1], need[:, :].rearrange("p (a f) -> p a f", a=1).broadcast_to([P, E, E]), lower_i, ALU.mult))
            then(nc.vector.tensor_reduce(first[:, :], ties[:, 1], axis=X_AXIS, op=ALU.add))
            then(nc.vector.tensor_scalar(need[:, :], first[:, :], float(P), None, ALU.mult))
            dve.wait_ge(ranks_done, 1)
            then(nc.vector.tensor_tensor(pos, bank[5][:, 0:TILES * E].rearrange("p (t e) -> p t e", t=TILES),
                                         need[:, :].rearrange("p (a e) -> p a e", a=1).broadcast_to([P, TILES, E]), ALU.add))
            nc.vector.tensor_tensor(picked[0], pos, nth[0], ALU.mult)
            then(nc.vector.tensor_tensor(picked[1], pos, nth[1], ALU.mult))
            for n in range(TOPK):
                then(nc.vector.tensor_reduce(slotf[n][:, :], picked[n], axis=X_AXIS, op=ALU.add))
                nc.vector.tensor_copy(slot[n][:, :], slotf[n][:, :]).then_inc(slots_ready, 1)
            then(nc.vector.tensor_tensor(cmp23, tileno[:, :].rearrange("p (j a) -> p j a", a=1).broadcast_to([P, SLOT_TILES, E - 1]),
                                         first[:, 1:E].rearrange("p (a e) -> p a e", a=1).broadcast_to([P, SLOT_TILES, E - 1]), ALU.is_ge))
            then(nc.vector.tensor_reduce(owner_f[:, :], cmp23, axis=X_AXIS, op=ALU.add))
            nc.vector.tensor_copy(owner[:, :], owner_f[:, :]).then_inc(owner_ready, 1)

            def tile_xgT(j, n):
                dve.wait_ge(xg_turned, j + 1)
                nc.vector.tensor_copy(way[n][:, :], xg[n][:, D:ROW])
                nc.vector.tensor_copy(xgT_hi[:, n], bank[7][:, 0:DC * P]).then_inc(xgT_high, 1)
                dve.wait_ge(xgT_high, j + 1)
                nc.vector.tensor_tensor(xgT_lo[:, n], bank[7][:, 0:DC * P], xgT_hi[:, n].bitcast(F32), ALU.subtract).then_inc(xgT_ready, 1)

            def low(n, g, count):
                dve.wait_ge(high_ready, count)
                whole = w_up[n].rearrange("p (m c n) -> p m c n", m=2, c=DC)[:, g // 2, :, g % 2 * BANK:(g % 2 + 1) * BANK]
                nc.vector.tensor_tensor(w_lo[:, g % 3], whole, w_hi[:, g % 3].bitcast(F32), ALU.subtract).then_inc(low_ready, 1)

            def tile_hid(j, n):
                for half in range(2):
                    dve.wait_ge(silu_ready, j * 2 + half + 1)
                    dve.wait_ge(u_done, j * 2 + half + 1)
                    cols = slice(half * BANK, (half + 1) * BANK)
                    last = nc.vector.tensor_tensor(hid[n][:, cols], silu[n][:, cols], bank[2 + half], ALU.mult)
                last.then_inc(hid_ready, 1)

            def tile_way(j, n, again):
                if again is not None:
                    dve.wait_ge(y_stored[n], again)
                nc.vector.tensor_copy(weight[n][:, :], way[n][:, 0:1])
                return nc.vector.tensor_copy(target[n][:, :], way[n][:, 1:2])

            def tile_y(j, n):
                dve.wait_ge(y_done, j + 1)
                nc.vector.tensor_scalar(yt[n], bank[6][:, 0:D], weight[n][:, 0:1], None, ALU.mult).then_inc(y_ready, 1)

            def tile_step(j, n, fresh=False, last=False):
                if j is not 0:
                    tile_way(j - 1, 1 - n, None if fresh else (j - 2 + n) * 8)
                low(n, 3, j * 4 + 4)
                tile_hid(j, n)
                if not last:
                    tile_xgT(j + 1, 1 - n)
                    for g in range(3):
                        low(1 - n, g, (j + 1) * 4 + g + 1)
                if j is not 0:
                    tile_y(j - 1, 1 - n)

            for g in range(3):
                low(0, g, g + 1)
            tile_xgT(0, 0)
            for j in range(3):
                tile_step(j, j % 2, fresh=True)
            with dve.Fori(3, SLOT_TILES - 2, 2) as j2:
                tile_step(j2, 1)
                tile_step(j2 + 1, 0)
            tile_step(SLOT_TILES - 2, 1)
            tile_step(SLOT_TILES - 1, 0, last=True)
            then(tile_way(SLOT_TILES - 1, 0, 16 * (SLOT_TILES // 2)))
            tile_y(SLOT_TILES - 1, 0)

            for t in range(TILES):
                dve.wait_ge(y_loaded[t], 16)
                then(nc.vector.tensor_tensor(x3n[:, t, :], y_of[:, t, 0, :], y_of[:, t, 1, :], ALU.add))
                nc.vector.tensor_tensor(x3n[:, t, :], x3n[:, t, :], xr[:, t, :], ALU.add).then_inc(out_ready, 1)

        @block.tensor
        def _(pe):
            def turn(dst, src):
                return nc.tensor.transpose(dst, src, ident[0:src.shape[0], 0:src.shape[0]])

            def turn_two(k, s, src, dst):
                pe.wait_ge(xn_ready, k * TILES + 2 * s + 2)
                for c in range(DC):
                    for t in range(2):
                        last = turn(dst[:, (c * 2 + t) * P:(c * 2 + t + 1) * P], src[:, 2 * s + t, c * P:(c + 1) * P])
                return last

            pe.wait_ge(consts, 1)
            for _ in range(WARM):
                nc.tensor.matmul(bank[7][:, 0:D], zeros[:, 0:P], zeros[:, 0:D], start=True, stop=True)
            pe.wait_ge(consts, N_CONST)
            def turn_weight(nat, width, f0, s):
                w = nat.rearrange("p (c n) -> p c n", c=DC)
                for f in range(2):
                    for o in range(DC):
                        last = turn(bank[s][:, (f * DC + o) * P:(f * DC + o + 1) * P], w[:, o, (f0 + f) * P:(f0 + f + 1) * P])
                return last

            for s in range(DUOS):
                turn_two(0, s, xn, bank[3 + s]).then_inc(setup_done, 1)
            for s, (nat, width, f0, loaded) in enumerate(((w1_nat, D, 0, w1_loaded), (w2_nat, 2 * D, 0, w2_loaded), (w2_nat, 2 * D, DC, w2_loaded))):
                pe.wait_ge(loaded, 16)
                turn_weight(nat, width, f0, s).then_inc(setup_done, 1)
            pe.wait_ge(setup_act, 7)
            for s in range(4):
                kc, half = s // 2, s % 2
                for c in range(DC):
                    last = nc.tensor.matmul(bank[(2, 7, 0, 1)[s]], w1T[:, c, kc * P:(kc + 1) * P], xnT[:, c, half * BANK:(half + 1) * BANK],
                                            start=c == 0, stop=c == DC - 1)
                last.then_inc(setup_done, 1)
            for s in range(4):
                for t in range(2):
                    for c in range(DC):
                        last = nc.tensor.matmul(bank[3 + s][:, t * D:(t + 1) * D], xnT[:, c, (2 * s + t) * P:(2 * s + t + 1) * P],
                                                w2T[:, c, :], start=c == 0, stop=c == DC - 1)
                last.then_inc(setup_done, 1)
            pe.wait_ge(small_loaded, 16 * 4)
            pe.wait_ge(setup_act, 9)
            for s, nat in enumerate((q_nat, k_nat, v_nat, o_nat)):
                if s >= 2:
                    pe.wait_ge(setup_dve, s - 1)
                turn_weight(nat, D, 0, (2, 7, 3, 4)[s]).then_inc(setup_done, 1)
            pe.wait_ge(setup_act, 15)
            pe.wait_ge(setup_dve, 4)

            with pe.Fori(0, BATCH // 2) as i:
                for n in range(2):
                    b = i * 2 + n

                    def turn_ctx(ch):
                        if ch % 2 == 0:
                            pe.wait_ge(ctx_loaded[n][ch // 2], i * 16 + 16)
                        for c in range(DC):
                            if ch == 0:
                                pe.wait_ge(probsT_ready, b * PAIRS + FIRST)
                            else:
                                pe.wait_ge(ctxT_ready, b * (CHUNKS * DC) + (ch - 1) * DC + c + 1)
                            for k in range(TPG):
                                last = turn(bank[c][:, k * P:(k + 1) * P], ctx_sb[n][:, ch * TPG + k, c * P:(c + 1) * P])
                            last.then_inc(ctx_turned, 1)

                    def score(ch):
                        if ch == 0:
                            pe.wait_ge(queries_ready, b + 1)
                        pe.wait_ge(ctxT_ready, b * (CHUNKS * DC) + (ch + 1) * DC)
                        for t in range(TPB):
                            pe.wait_ge(scores_out, b * (TPB * CHUNKS) + max(ch - 1, 0) * TPB + (t + 1 if ch else 0) + FIRST)
                            for c in range(DC):
                                for m, (q, k) in enumerate(((bf_lo, ctxT_hi), (bf_hi, ctxT_lo), (bf_hi, ctxT_hi))):
                                    last = nc.tensor.matmul(bank[2 + t], q[:, n, c, t * P:(t + 1) * P], k[:, ch % 2, c, :],
                                                            start=c == 0 and m == 0, stop=c == DC - 1 and m == 2)
                            last.then_inc(scores_done, 1)

                    def turn_expert(g):
                        k, gq = g // MATGROUPS, g % MATGROUPS
                        if gq == 0:
                            pe.wait_ge(w_loaded[k % 2], b * (16 * PPB // 2) + 16 * (k // 2 + 1))
                        if 0 <= g - 2 - WAITING * MATGROUPS < MATGROUPS:
                            pe.wait_ge(waiting_out, b * MATGROUPS + g - 1 - WAITING * MATGROUPS)
                        else:
                            pe.wait_ge(w_out, b * GPB_ACT + max(g - 1 - (MATGROUPS if g > WAITING * MATGROUPS + 2 else 0), 0) + FIRST)
                        for q in range(TPG):
                            if k % NMAT < 2:
                                src = w_nat[k % 2].rearrange("p (c n) -> p c n", c=IC)[:, TPG * (gq % 2) + q, (gq // 2) * P:(gq // 2 + 1) * P]
                            else:
                                ic = 2 * gq + q // 2
                                src = w_nat[k % 2].rearrange("p (c n) -> p c n", c=DC)[:, q % 2, ic * P:(ic + 1) * P]
                            last = turn(bank[4 + g % 2][:, q * P:(q + 1) * P], src)
                        last.then_inc(w_turned, 1)

                    turn_ctx(0)
                    for ch in range(CHUNKS):
                        for g in range(BESIDE * ch, BESIDE * (ch + 1)):
                            turn_expert(g)
                        if ch + 1 < CHUNKS:
                            turn_ctx(ch + 1)
                        score(ch)
                    for g in range(WAITING * MATGROUPS, (WAITING + 1) * MATGROUPS):
                        turn_expert(g)

                    def turn_probs(g):
                        if g % 2 == 0:
                            pe.wait_ge(exp_done, b * (TPB * PIECES) + (g // 2 + 1) * TPB)
                        if g < 2:
                            pe.wait_ge(ctxT_ready, b * (CHUNKS * DC) + CHUNKS * DC)
                        else:
                            pe.wait_ge(probsT_ready, b * PAIRS + g - 1 + FIRST)
                        for k in range(PAIR):
                            for t in range(TPB):
                                at = k * NTOK + t * P
                                last = turn(bank[g % 2][:, at:at + P], scores[t][:, (g * PAIR + k) * P:(g * PAIR + k + 1) * P])
                        last.then_inc(probs_turned, 1)

                    def weigh(g):
                        pe.wait_ge(val_ready, b * PAIRS + g + 1)
                        pe.wait_ge(probsT_ready, b * PAIRS + g + 1 + FIRST)
                        if g == 0:
                            pe.wait_ge(x1_ready, b + FIRST)
                        for k in range(PAIR):
                            for c in range(DC):
                                for m, (v, p) in enumerate(((val_lo, pT_hi), (val_hi, pT_lo), (val_hi, pT_hi))):
                                    last = nc.tensor.matmul(bank[6 + c][:, 0:NTOK], v[:, g % 4, k, c * P:(c + 1) * P], p[:, g % 2, k, :],
                                                            start=g == 0 and k == 0 and m == 0,
                                                            stop=g == PAIRS - 1 and k == PAIR - 1 and m == 2)
                        last.then_inc(pv_done, 1)

                    turn_probs(0)
                    for g in range(PAIRS):
                        if g + 1 < PAIRS:
                            turn_probs(g + 1)
                        weigh(g)
                    for g in range((WAITING + 1) * MATGROUPS, GPB):
                        turn_expert(g)
                    pe.wait_ge(oT_ready, b + 1)
                    for t in range(TPB):
                        for c in range(DC):
                            last = nc.tensor.matmul(bank[6][:, t * D:(t + 1) * D], oT[:, c, t * P:(t + 1) * P], w2T[:, DC + c, :],
                                                    start=c == 0, stop=c == DC - 1)
                    last.then_inc(fused_done, 1)

            pe.wait_ge(x1_ready, BATCH + FIRST)
            pe.wait_ge(w_out, BATCH * GPB_ACT + FIRST)
            def project(s):
                half, w, hc = s // (2 * DC), (qwT, kwT)[s // DC % 2], s % DC
                if s >= 4:
                    pe.wait_ge(p2_act, s - 3)
                for c in range(DC):
                    last = nc.tensor.matmul(bank[(4 + s) % 8], w[:, c, hc * P:(hc + 1) * P], x2nT[:, c, half * BANK:(half + 1) * BANK],
                                            start=c == 0, stop=c == DC - 1)
                last.then_inc(proj_done, 1)

            for s in range(DUOS):
                turn_two(1, s, x2n, bank[s]).then_inc(p2_done, 1)
                if s >= 1:
                    pe.wait_ge(p2_act, 2)
                    project(s - 1)
            pe.wait_ge(p2_act, 4)
            for s in range(DUOS - 1, 4 * DC):
                project(s)
            pe.wait_ge(p2_act, 4 + 4 * DC)

            def local_score(b, u):
                t, hc = UNITS[u]
                pe.wait_ge(q_ready, b * len(UNITS) + u + 1)
                pe.wait_ge(row_max, b * len(UNITS) + (0 if u == 1 else u) + FIRST)
                for h in range(HPC):
                    at = u * HPC * P + h * P if t == 0 else h * NTOK
                    last = nc.tensor.matmul(psum[:, at:at + SEEN[t]], q_own[u % 2][:, h, :],
                                            kT[:, hc, bass.ds(b * NTOK + KEY0[t], SEEN[t])], start=True, stop=True)
                last.then_inc(local_done, 1)

            def local_turn(b, u, g):
                tiles = UNITS[u][0] + 1
                at = GROUP0[u] + g
                pe.wait_ge(localT_ready, b * sum(GROUPS) + max(at - 1, 0) + FIRST)
                for k in range(TPG):
                    h, kt = (g * TPG + k) // tiles, k % tiles
                    last = turn(bank[4 + at % 2][:, k * P:(k + 1) * P], local[u][:, h, kt * P:(kt + 1) * P])
                last.then_inc(local_turned, 1)

            def local_weigh(b, u):
                t, hc = UNITS[u]
                tiles = t + 1
                if u == 0:
                    pe.wait_ge(v_ready, b + 1)
                pe.wait_ge(heads_ready, b * len(UNITS) + max(u - 1, 0) + FIRST)
                for g in range(GROUPS[u]):
                    pe.wait_ge(localT_ready, b * sum(GROUPS) + GROUP0[u] + g + 1 + FIRST)
                    for k in range(TPG):
                        h, kt = (g * TPG + k) // tiles, k % tiles
                        last = nc.tensor.matmul(bank[6 + u % 2][:, 0:P], v_own[:, kt, hc, h * P:(h + 1) * P], pT[:, (GROUP0[u] + g) % 4, k, :],
                                                start=g == 0 and k == 0, stop=g == GROUPS[u] - 1 and k == TPG - 1)
                    if g + 2 < GROUPS[u]:
                        local_turn(b, u, g + 2)
                last.then_inc(localpv_done, 1)

            def local_batch(b, more):
                for u in range(len(UNITS)):
                    pe.wait_ge(normed, b * len(UNITS) + u + 1)
                    local_turn(b, u, 0)
                    local_turn(b, u, 1)
                    if u < 2 or more:
                        local_score(b if u < 2 else b + 1, (u + 2) % 4)
                    local_weigh(b, u)

            local_score(0, 0)
            local_score(0, 1)
            for s in range(4):
                at = 4 + 4 * DC + s
                pe.wait_ge(p2_act, at - 7)
                for t in range(2):
                    for c in range(DC):
                        last = nc.tensor.matmul(bank[at % 8][:, t * D:(t + 1) * D], x2nT[:, c, (2 * s + t) * P:(2 * s + t + 1) * P],
                                                vwT[:, c, :], start=c == 0, stop=c == DC - 1)
                last.then_inc(proj_done, 1)
            pe.wait_ge(p2_dve, 4)
            pe.wait_ge(zeroed, 1 + DC)
            with pe.Fori(0, BATCH - 1) as b:
                local_batch(b, True)
            local_batch(BATCH - 1, False)

            pe.wait_ge(heads_ready, BATCH * len(UNITS) + FIRST)
            for s in range(4):
                for t in range(2):
                    for c in range(DC):
                        last = nc.tensor.matmul(bank[s][:, t * D:(t + 1) * D], headsT[:, c, (2 * s + t) * P:(2 * s + t + 1) * P],
                                                owT[:, c, :], start=c == 0, stop=c == DC - 1)
                last.then_inc(p2c_done, 1)

            def logits(s):
                pe.wait_ge(p3_act, s + 1)
                for t in range(2 * s, 2 * s + 2):
                    for c in range(DC):
                        last = nc.tensor.matmul(bank[4][:, t * E:(t + 1) * E], x3nT[:, c, t * P:(t + 1) * P], gwT[:, c, :],
                                                start=c == 0, stop=c == DC - 1)
                return last

            for s in range(DUOS):
                turn_two(2, s, x3n, bank[s]).then_inc(p3_done, 1)
                if s > 0:
                    logits(s - 1)
            last = logits(DUOS - 1)
            last.then_inc(p3_done, 1)
            pe.wait_ge(chosen_ready, 1)
            nc.tensor.matmul(bank[5][:, 0:TILES * E], earlier[:, :], chosen.rearrange("p t e -> p (t e)"), start=True, stop=False)
            pe.wait_ge(sums_ready, 1)
            nc.tensor.matmul(bank[6][:, 0:E], ones[:, :], csum[:, :], start=True, stop=True).then_inc(counts_done, 1)
            nc.tensor.matmul(bank[5][:, 0:TILES * E], ones[:, :], before.rearrange("p t e -> p (t e)"), start=False, stop=True).then_inc(ranks_done, 1)

            pe.wait_ge(slots_ready, 1)

            def tile_turn(j, n, arrived):
                pe.wait_ge(xg_loaded[n], arrived)
                if j is not 0:
                    pe.wait_ge(xgT_ready, j)
                for c in range(DC):
                    last = turn(bank[7][:, c * P:(c + 1) * P], xg[n][:, c * P:(c + 1) * P])
                last.then_inc(xg_turned, 1)

            def turn_hid(j, n):
                pe.wait_ge(hid_ready, j + 1)
                if j is not 0:
                    pe.wait_ge(hidT_ready, j * 2)
                for half in range(2):
                    for k in range(TPG):
                        at = (half * TPG + k) * P
                        last = turn(bank[4 + half][:, k * P:(k + 1) * P], hid[n][:, at:at + P])
                    last.then_inc(hid_turned, 1)

            def tile_up(j, n):
                for g in range(2 * DC):
                    pe.wait_ge(low_ready, j * 4 + g + 1)
                    if g == 0:
                        pe.wait_ge(xgT_ready, j + 1)
                        if j is not 0:
                            pe.wait_ge(silu_ready, j * 2)
                    elif g == 2 and j is not 0:
                        pe.wait_ge(hid_ready, j)
                    for c in range(DC):
                        cols = slice(c * P, (c + 1) * P)
                        parts = ((xgT_lo, w_hi), (xgT_hi, w_lo), (xgT_hi, w_hi))
                        for m, (rows, w) in enumerate(parts):
                            last = nc.tensor.matmul(bank[g], rows[:, n, cols], w[:, g % 3, c, :],
                                                    start=c == 0 and m == 0, stop=c == DC - 1 and m == len(parts) - 1)
                    last.then_inc((g_done, u_done)[g // 2], 1)
                    if g == 1 and j is not 0:
                        turn_hid(j - 1, 1 - n)

            def tile_down(j, n, arrived):
                pe.wait_ge(down_loaded[n], arrived)
                if j is not 0:
                    pe.wait_ge(y_ready, j)
                for ic in range(IC):
                    if ic % TPG == 0:
                        pe.wait_ge(hidT_ready, j * 2 + ic // TPG + 1)
                    at = ic * D
                    last = nc.tensor.matmul(bank[6][:, 0:D], hidT[n][:, ic * P:(ic + 1) * P], w_down[n][:, at:at + D],
                                            start=ic == 0, stop=ic == IC - 1)
                last.then_inc(y_done, 1)

            pe.wait_ge(low_ready, 3)
            for _ in range(WARM):
                nc.tensor.matmul(bank[7][:, 0:D], zeros[:, 0:P], zeros[:, 0:D], start=True, stop=True)
            tile_turn(0, 0, 16)
            tile_up(0, 0)
            tile_turn(1, 1, 16)

            def two_tiles(j2, more):
                tile_up(j2, 1)
                tile_turn(j2 + 1, 0, (j2 + 3) * 8)
                tile_down(j2 - 1, 0, (j2 + 1) * 8)
                tile_up(j2 + 1, 0)
                if more:
                    tile_turn(j2 + 2, 1, (j2 + 3) * 8)
                tile_down(j2, 1, (j2 + 1) * 8)

            with pe.Fori(1, SLOT_TILES - 2, 2) as j2:
                two_tiles(j2, True)
            two_tiles(SLOT_TILES - 2, False)
            turn_hid(SLOT_TILES - 1, 0)
            tile_down(SLOT_TILES - 1, 0, (SLOT_TILES + 1) * 8)


_INS = ["x", "ctx_1024", "L0_xattn_w1_w", "L0_xattn_w1_b", "L0_xattn_w2_w", "L0_xattn_w2_b", "L0_attn_q_w", "L0_attn_q_b",
        "L0_attn_k_w", "L0_attn_k_b", "L0_attn_v_w", "L0_attn_v_b", "L0_attn_o_w", "L0_attn_o_b", "L0_ffn_gate_w",
        "L0_ffn_wg", "L0_ffn_wu", "L0_ffn_wd"]


def kernel(**inputs):
    import numpy as np
    import concourse.bacc as bacc
    from concourse.bass_utils import run_bass_kernel_spmd

    nc = bacc.Bacc("TRN2", target_bir_lowering=False, num_devices=1)
    arrays, args = {}, []
    for name in _INS:
        a = np.ascontiguousarray(inputs[name])
        arrays[name + "_dram"] = a
        args.append(nc.dram_tensor(name + "_dram", a.shape, mybir.dt.from_np(a.dtype), kind="ExternalInput").ap())
    out = nc.dram_tensor("out_dram", (BATCH, NTOK, D), F32, kind="ExternalOutput").ap()
    perceiver(nc, *args, out)
    r = run_bass_kernel_spmd(nc, [arrays], core_ids=[0])
    return r.results[0]["out_dram"]
```
